# Optimizing a Trainium2 kernel written in Bass

```python
import numpy as np
import jax
import jax.numpy as jnp

def _softmax(x, axis=-1):
    return jax.nn.softmax(x, axis=axis)

def _gelu(x):
    return jax.nn.gelu(x, approximate=True)

def _silu(x):
    return jax.nn.silu(x)

def _sigmoid(x):
    return jax.nn.sigmoid(x)

def _layernorm(x, axis=-1, eps=1e-05):
    m = jnp.mean(x, axis=axis, keepdims=True)
    v = jnp.var(x, axis=axis, keepdims=True)
    return (x - m) / jnp.sqrt(v + eps)

def _scatter_add(tgt, idx, src, axis=0):
    return tgt.at[idx].add(src)

def _segment_sum(src, seg, n):
    return jax.ops.segment_sum(src, seg, n)
kernel_name = 'mk_early_fusion_d2_tok_img768_r4_163ef3'

def setup_inputs(seed: int=0):
    np.random.seed(seed)
    _w = jnp.asarray

    def _rec_inputs():
        import jax
        import jax.numpy as jnp
        _rk = jax.random.key(seed)
        x = -7.10856e-05 + 0.999911 * jax.random.normal(jax.random.fold_in(_rk, 1), (2, 32, 128, 128), jnp.float32)
        txt = -0.00271877 + 0.451779 * jax.random.normal(jax.random.fold_in(_rk, 2), (2, 77, 192), jnp.float32)
        return (x, txt)
    x, txt = _rec_inputs()

    def _L0_tok_setup():
        import jax, jax.numpy as jnp
        import numpy as np
        B, C, H, W = (8, 32, 128, 128)
        P = 8
        D = 128
        NH, DH = (8, 64)
        M = 512
        L = 2
        DOUT = 192
        INNER = NH * DH

        def _ln(x, g, b, eps=1e-05):
            mu = x.mean(-1, keepdims=True)
            xc = x - mu
            var = (xc * xc).mean(-1, keepdims=True)
            return xc * jax.lax.rsqrt(var + eps) * g + b

        def _forward(im, conv_w, conv_b, ln1_g, ln1_b, qkv_w, out_w, out_b, ln2_g, ln2_b, ff1_w, ff1_b, ff2_w, ff2_b, lnf_g, lnf_b, head_w, head_b):
            b, c, h, w = im.shape
            hp, wp = (h // P, w // P)
            patches = im.reshape(b, c, hp, P, wp, P)
            x = jnp.einsum('bchpwq,dcpq->bhwd', patches, conv_w)
            x = x.reshape(b, hp * wp, -1) + conv_b
            n = hp * wp
            scale = DH ** (-0.5)
            for i in range(ln1_g.shape[0]):
                y = _ln(x, ln1_g[i], ln1_b[i])
                qkv = y @ qkv_w[i]
                q, k, v = jnp.split(qkv, 3, axis=-1)
                to_heads = lambda t: t.reshape(b, n, NH, DH).transpose(0, 2, 1, 3)
                q, k, v = (to_heads(q), to_heads(k), to_heads(v))
                q = jax.nn.softmax(q, axis=-1) * scale
                k = jax.nn.softmax(k, axis=-2)
                ctx = jnp.einsum('bhnd,bhne->bhde', k, v)
                att = jnp.einsum('bhnd,bhde->bhne', q, ctx)
                att = att.transpose(0, 2, 1, 3).reshape(b, n, INNER)
                x = x + att @ out_w[i] + out_b[i]
                y = _ln(x, ln2_g[i], ln2_b[i])
                hdn = jax.nn.gelu(y @ ff1_w[i] + ff1_b[i], approximate=False)
                x = x + hdn @ ff2_w[i] + ff2_b[i]
            return _ln(x, lnf_g, lnf_b) @ head_w + head_b
        key = jax.random.key(seed)
        ks = iter(jax.random.split(key, 32))
        g = lambda shape, s=0.02: (jax.random.normal(next(ks), shape) * s).astype(jnp.float32)
        inp = {'im': jax.random.normal(next(ks), (B, C, H, W), dtype=jnp.float32), 'conv_w': g((D, C, P, P)), 'conv_b': jnp.zeros((D,), jnp.float32), 'ln1_g': jnp.ones((L, D), jnp.float32), 'ln1_b': jnp.zeros((L, D), jnp.float32), 'qkv_w': g((L, D, 3 * INNER)), 'out_w': g((L, INNER, D)), 'out_b': jnp.zeros((L, D), jnp.float32), 'ln2_g': jnp.ones((L, D), jnp.float32), 'ln2_b': jnp.zeros((L, D), jnp.float32), 'ff1_w': g((L, D, M)), 'ff1_b': jnp.zeros((L, M), jnp.float32), 'ff2_w': g((L, M, D)), 'ff2_b': jnp.zeros((L, D), jnp.float32), 'lnf_g': jnp.ones((D,), jnp.float32), 'lnf_b': jnp.zeros((D,), jnp.float32), 'head_w': g((D, DOUT)), 'head_b': jnp.zeros((DOUT,), jnp.float32)}
        return inp
    _L0_tok_all = _L0_tok_setup()
    _L0_tok_in = {k: v for k, v in _L0_tok_all.items() if k in ('conv_w', 'conv_b', 'ln1_g', 'ln1_b', 'qkv_w', 'out_w', 'out_b', 'ln2_g', 'ln2_b', 'ff1_w', 'ff1_b', 'ff2_w', 'ff2_b', 'lnf_g', 'lnf_b', 'head_w', 'head_b')}
    del _L0_tok_all

    def _L0_attn_setup():
        import jax, jax.numpy as jnp
        import numpy as np
        EMBED_DIM = 192
        SEQ_LEN = 256
        BATCH = 16
        ALPHA = 0.99
        key = jax.random.key(seed)
        k_x, k_w, k_b = jax.random.split(key, 3)
        d = EMBED_DIM
        x = jax.random.normal(k_x, (BATCH, SEQ_LEN, d), dtype=jnp.float32)
        lim = 1.0 / np.sqrt(d)
        W_qkv = jax.random.uniform(k_w, (3 * d, d), dtype=jnp.float32, minval=-lim, maxval=lim)
        b_qkv = jax.random.uniform(k_b, (3 * d,), dtype=jnp.float32, minval=-lim, maxval=lim)
        return {'x': x, 'W_qkv': W_qkv, 'b_qkv': b_qkv}
    _L0_attn_all = _L0_attn_setup()
    _L0_attn_in = {k: v for k, v in _L0_attn_all.items() if k in ('W_qkv', 'b_qkv')}
    del _L0_attn_all

    def _L0_ffn_setup():
        import jax, jax.numpy as jnp
        import numpy as np
        B, N, DIM, HEADS = (4, 256, 192, 12)
        HIDDEN, E, TOPK = (768, 8, 2)
        EPS = 1e-05

        def _layernorm(x, g, b):
            mu = jnp.mean(x, axis=-1, keepdims=True)
            var = jnp.var(x, axis=-1, keepdims=True)
            return (x - mu) * jax.lax.rsqrt(var + EPS) * g + b
        key = jax.random.key(seed)
        ks = jax.random.split(key, 10)
        s = 0.02
        return {'x': jax.random.normal(ks[0], (B, N, DIM), dtype=jnp.float32), 'ln1_g': jnp.ones((DIM,), jnp.float32), 'ln1_b': jnp.zeros((DIM,), jnp.float32), 'qkv_w': jax.random.normal(ks[1], (3 * DIM, DIM), jnp.float32) * s, 'proj_w': jax.random.normal(ks[2], (DIM, DIM), jnp.float32) * s, 'proj_b': jnp.zeros((DIM,), jnp.float32), 'ln2_g': jnp.ones((DIM,), jnp.float32), 'ln2_b': jnp.zeros((DIM,), jnp.float32), 'gate_w': jax.random.normal(ks[3], (E, DIM), jnp.float32) * s, 'gate_b': jnp.zeros((E,), jnp.float32), 'w1': jax.random.normal(ks[4], (E, HIDDEN, DIM), jnp.float32) * s, 'b1': jnp.zeros((E, HIDDEN), jnp.float32), 'w2': jax.random.normal(ks[5], (E, DIM, HIDDEN), jnp.float32) * s, 'b2': jnp.zeros((E, DIM), jnp.float32)}
    _L0_ffn_all = _L0_ffn_setup()
    _L0_ffn_in = {k: v for k, v in _L0_ffn_all.items() if k in ('ln1_g', 'ln1_b', 'qkv_w', 'proj_w', 'proj_b', 'ln2_g', 'ln2_b', 'gate_w', 'gate_b', 'w1', 'b1', 'w2', 'b2')}
    del _L0_ffn_all

    def _L1_attn_setup():
        import jax, jax.numpy as jnp
        import numpy as np
        B, N, C = (8, 1024, 192)
        H = 8
        G = 2
        HD = C // H
        HG = H // G
        SCALE = HD ** (-0.5)
        key = jax.random.key(seed)
        k0, k1, k2, k3 = jax.random.split(key, 4)
        std = 0.02
        return {'x': jax.random.normal(k0, (B, N, C), dtype=jnp.float32), 'Wq': jax.random.normal(k1, (C, HD * G), dtype=jnp.float32) * std, 'Wkv': jax.random.normal(k2, (C, 2 * C), dtype=jnp.float32) * std, 'Wproj': jax.random.normal(k3, (C, C), dtype=jnp.float32) * std, 'bproj': jnp.zeros((C,), dtype=jnp.float32)}
    _L1_attn_all = _L1_attn_setup()
    _L1_attn_in = {k: v for k, v in _L1_attn_all.items() if k in ('Wq', 'Wkv', 'Wproj', 'bproj')}
    del _L1_attn_all

    def _L1_ffn_setup():
        import jax, jax.numpy as jnp
        import numpy as np
        B, N, D, E, F, K = (2, 512, 192, 8, 768, 2)
        V_MAX = 3.0
        FEAT_CLAMP = 10.0

        def bk_green_diag(a):
            aT = jnp.swapaxes(a, 0, 1)

            def step(c, ai):
                d = ai - 1.0 / c
                return (d, d)
            d0 = aT[0]
            _, d_rest = jax.lax.scan(step, d0, aT[1:])
            d = jnp.concatenate([d0[None], d_rest], axis=0)
            eN = aT[-1]
            _, e_rest = jax.lax.scan(step, eN, aT[:-1], reverse=True)
            e = jnp.concatenate([e_rest, eN[None]], axis=0)
            G = 1.0 / (d + e - aT)
            return jnp.swapaxes(G, 0, 1)
        key = jax.random.key(seed)
        ks = jax.random.split(key, 8)
        s = lambda k, shape, sc: jax.random.normal(k, shape, jnp.float32) * sc
        return {'x': s(ks[0], (B, N, D), 1.0), 'v_w': s(ks[1], (D,), 0.02), 'v_b': jnp.zeros((), jnp.float32), 'gate_w': s(ks[2], (D, E), 0.02), 'gate_b': jnp.zeros((E,), jnp.float32), 'w1': s(ks[3], (E, D, F), 0.02), 'b1': jnp.zeros((E, F), jnp.float32), 'w2': s(ks[4], (E, F, D), 0.02), 'b2': jnp.zeros((E, D), jnp.float32), 'out_w': s(ks[5], (2, D), 0.02), 'out_b': jnp.zeros((D,), jnp.float32), 'bk_scale': jnp.ones((D,), jnp.float32)}
    _L1_ffn_all = _L1_ffn_setup()
    _L1_ffn_in = {k: v for k, v in _L1_ffn_all.items() if k in ('v_w', 'v_b', 'gate_w', 'gate_b', 'w1', 'b1', 'w2', 'b2', 'out_w', 'out_b', 'bk_scale')}
    del _L1_ffn_all
    return {'x': x, 'txt': txt, 'L0_tok_conv_w': _L0_tok_in['conv_w'], 'L0_tok_conv_b': _L0_tok_in['conv_b'], 'L0_tok_ln1_g': _L0_tok_in['ln1_g'], 'L0_tok_ln1_b': _L0_tok_in['ln1_b'], 'L0_tok_qkv_w': _L0_tok_in['qkv_w'], 'L0_tok_out_w': _L0_tok_in['out_w'], 'L0_tok_out_b': _L0_tok_in['out_b'], 'L0_tok_ln2_g': _L0_tok_in['ln2_g'], 'L0_tok_ln2_b': _L0_tok_in['ln2_b'], 'L0_tok_ff1_w': _L0_tok_in['ff1_w'], 'L0_tok_ff1_b': _L0_tok_in['ff1_b'], 'L0_tok_ff2_w': _L0_tok_in['ff2_w'], 'L0_tok_ff2_b': _L0_tok_in['ff2_b'], 'L0_tok_lnf_g': _L0_tok_in['lnf_g'], 'L0_tok_lnf_b': _L0_tok_in['lnf_b'], 'L0_tok_head_w': _L0_tok_in['head_w'], 'L0_tok_head_b': _L0_tok_in['head_b'], 'L0_attn_W_qkv': _L0_attn_in['W_qkv'], 'L0_attn_b_qkv': _L0_attn_in['b_qkv'], 'L0_ffn_ln1_g': _L0_ffn_in['ln1_g'], 'L0_ffn_ln1_b': _L0_ffn_in['ln1_b'], 'L0_ffn_qkv_w': _L0_ffn_in['qkv_w'], 'L0_ffn_proj_w': _L0_ffn_in['proj_w'], 'L0_ffn_proj_b': _L0_ffn_in['proj_b'], 'L0_ffn_ln2_g': _L0_ffn_in['ln2_g'], 'L0_ffn_ln2_b': _L0_ffn_in['ln2_b'], 'L0_ffn_gate_w': _L0_ffn_in['gate_w'], 'L0_ffn_gate_b': _L0_ffn_in['gate_b'], 'L0_ffn_w1': _L0_ffn_in['w1'], 'L0_ffn_b1': _L0_ffn_in['b1'], 'L0_ffn_w2': _L0_ffn_in['w2'], 'L0_ffn_b2': _L0_ffn_in['b2'], 'L1_attn_Wq': _L1_attn_in['Wq'], 'L1_attn_Wkv': _L1_attn_in['Wkv'], 'L1_attn_Wproj': _L1_attn_in['Wproj'], 'L1_attn_bproj': _L1_attn_in['bproj'], 'L1_ffn_v_w': _L1_ffn_in['v_w'], 'L1_ffn_v_b': _L1_ffn_in['v_b'], 'L1_ffn_gate_w': _L1_ffn_in['gate_w'], 'L1_ffn_gate_b': _L1_ffn_in['gate_b'], 'L1_ffn_w1': _L1_ffn_in['w1'], 'L1_ffn_b1': _L1_ffn_in['b1'], 'L1_ffn_w2': _L1_ffn_in['w2'], 'L1_ffn_b2': _L1_ffn_in['b2'], 'L1_ffn_out_w': _L1_ffn_in['out_w'], 'L1_ffn_out_b': _L1_ffn_in['out_b'], 'L1_ffn_bk_scale': _L1_ffn_in['bk_scale']}

def reference(x, txt, L0_tok_conv_w, L0_tok_conv_b, L0_tok_ln1_g, L0_tok_ln1_b, L0_tok_qkv_w, L0_tok_out_w, L0_tok_out_b, L0_tok_ln2_g, L0_tok_ln2_b, L0_tok_ff1_w, L0_tok_ff1_b, L0_tok_ff2_w, L0_tok_ff2_b, L0_tok_lnf_g, L0_tok_lnf_b, L0_tok_head_w, L0_tok_head_b, L0_attn_W_qkv, L0_attn_b_qkv, L0_ffn_ln1_g, L0_ffn_ln1_b, L0_ffn_qkv_w, L0_ffn_proj_w, L0_ffn_proj_b, L0_ffn_ln2_g, L0_ffn_ln2_b, L0_ffn_gate_w, L0_ffn_gate_b, L0_ffn_w1, L0_ffn_b1, L0_ffn_w2, L0_ffn_b2, L1_attn_Wq, L1_attn_Wkv, L1_attn_Wproj, L1_attn_bproj, L1_ffn_v_w, L1_ffn_v_b, L1_ffn_gate_w, L1_ffn_gate_b, L1_ffn_w1, L1_ffn_b1, L1_ffn_w2, L1_ffn_b2, L1_ffn_out_w, L1_ffn_out_b, L1_ffn_bk_scale):
    import jax
    import jax.numpy as jnp

    def _L0_tok_ref(im, conv_w, conv_b, ln1_g, ln1_b, qkv_w, out_w, out_b, ln2_g, ln2_b, ff1_w, ff1_b, ff2_w, ff2_b, lnf_g, lnf_b, head_w, head_b):
        import jax, jax.numpy as jnp
        import numpy as np
        B, C, H, W = (8, 32, 128, 128)
        P = 8
        D = 128
        NH, DH = (8, 64)
        M = 512
        L = 2
        DOUT = 192
        INNER = NH * DH

        def _ln(x, g, b, eps=1e-05):
            mu = x.mean(-1, keepdims=True)
            xc = x - mu
            var = (xc * xc).mean(-1, keepdims=True)
            return xc * jax.lax.rsqrt(var + eps) * g + b

        def _forward(im, conv_w, conv_b, ln1_g, ln1_b, qkv_w, out_w, out_b, ln2_g, ln2_b, ff1_w, ff1_b, ff2_w, ff2_b, lnf_g, lnf_b, head_w, head_b):
            b, c, h, w = im.shape
            hp, wp = (h // P, w // P)
            patches = im.reshape(b, c, hp, P, wp, P)
            x = jnp.einsum('bchpwq,dcpq->bhwd', patches, conv_w)
            x = x.reshape(b, hp * wp, -1) + conv_b
            n = hp * wp
            scale = DH ** (-0.5)
            for i in range(ln1_g.shape[0]):
                y = _ln(x, ln1_g[i], ln1_b[i])
                qkv = y @ qkv_w[i]
                q, k, v = jnp.split(qkv, 3, axis=-1)
                to_heads = lambda t: t.reshape(b, n, NH, DH).transpose(0, 2, 1, 3)
                q, k, v = (to_heads(q), to_heads(k), to_heads(v))
                q = jax.nn.softmax(q, axis=-1) * scale
                k = jax.nn.softmax(k, axis=-2)
                ctx = jnp.einsum('bhnd,bhne->bhde', k, v)
                att = jnp.einsum('bhnd,bhde->bhne', q, ctx)
                att = att.transpose(0, 2, 1, 3).reshape(b, n, INNER)
                x = x + att @ out_w[i] + out_b[i]
                y = _ln(x, ln2_g[i], ln2_b[i])
                hdn = jax.nn.gelu(y @ ff1_w[i] + ff1_b[i], approximate=False)
                x = x + hdn @ ff2_w[i] + ff2_b[i]
            return _ln(x, lnf_g, lnf_b) @ head_w + head_b
        return _forward(im, conv_w, conv_b, ln1_g, ln1_b, qkv_w, out_w, out_b, ln2_g, ln2_b, ff1_w, ff1_b, ff2_w, ff2_b, lnf_g, lnf_b, head_w, head_b)

    def _L0_attn_ref(x, W_qkv, b_qkv):
        import jax, jax.numpy as jnp
        import numpy as np
        EMBED_DIM = 192
        SEQ_LEN = 256
        BATCH = 16
        ALPHA = 0.99
        bs, sl, d = x.shape
        qkv = x @ W_qkv.T + b_qkv
        q, k, v = jnp.split(qkv, 3, axis=-1)
        idx = jnp.arange(sl)
        diff = idx[:, None] - idx[None, :]
        M = jnp.where(diff >= 0, jnp.float32(ALPHA) ** diff.astype(jnp.float32), 0.0)
        dim_sqrt = jnp.asarray(d, jnp.float32) ** 0.5
        scores = jnp.einsum('bsd,btd->bst', q, k) / dim_sqrt * M
        out = jnp.einsum('bst,btd->bsd', scores, v)
        return out

    def _L0_ffn_ref(x, ln1_g, ln1_b, qkv_w, proj_w, proj_b, ln2_g, ln2_b, gate_w, gate_b, w1, b1, w2, b2):
        import jax, jax.numpy as jnp
        import numpy as np
        B, N, DIM, HEADS = (4, 256, 192, 12)
        HIDDEN, E, TOPK = (768, 8, 2)
        EPS = 1e-05

        def _layernorm(x, g, b):
            mu = jnp.mean(x, axis=-1, keepdims=True)
            var = jnp.var(x, axis=-1, keepdims=True)
            return (x - mu) * jax.lax.rsqrt(var + EPS) * g + b
        b, n, d = x.shape
        hd = d // HEADS
        scale = hd ** (-0.5)
        h = _layernorm(x, ln1_g, ln1_b)
        qkv = h @ qkv_w.T
        qkv = qkv.reshape(b, n, 3, HEADS, hd).transpose(2, 0, 3, 1, 4)
        q, k, v = (qkv[0], qkv[1], qkv[2])
        attn = jax.nn.softmax(jnp.einsum('bhnd,bhmd->bhnm', q, k) * scale, axis=-1)
        a = jnp.einsum('bhnm,bhmd->bhnd', attn, v)
        a = a.transpose(0, 2, 1, 3).reshape(b, n, d)
        a = a @ proj_w.T + proj_b
        x = x + a
        h2 = _layernorm(x, ln2_g, ln2_b)
        t = h2.reshape(-1, d)
        T = t.shape[0]
        logits = t @ gate_w.T + gate_b
        top_val, top_idx = jax.lax.top_k(logits, TOPK)
        score = jax.nn.softmax(top_val, axis=-1)
        cw = jnp.zeros((T, E), t.dtype).at[jnp.arange(T)[:, None], top_idx].add(score)
        out = jnp.zeros_like(t)
        for e in range(E):
            he = jax.nn.gelu(t @ w1[e].T + b1[e], approximate=False)
            ye = he @ w2[e].T + b2[e]
            out = out + cw[:, e:e + 1] * ye
        return x + out.reshape(b, n, d)

    def _L1_attn_ref(x, Wq, Wkv, Wproj, bproj):
        import jax, jax.numpy as jnp
        import numpy as np
        B, N, C = (8, 1024, 192)
        H = 8
        G = 2
        HD = C // H
        HG = H // G
        SCALE = HD ** (-0.5)
        b, n, c = x.shape
        q = (x @ Wq).reshape(b, 1, n, G, HD).transpose(0, 3, 1, 2, 4)
        kv = (x @ Wkv).reshape(b, n, 2, G, HG, HD).transpose(2, 0, 3, 4, 1, 5)
        k = kv[0] * SCALE
        v = kv[1]
        attn = jnp.einsum('bghnd,bghne->bghde', k.astype(jnp.float32), v.astype(jnp.float32))
        attn = jax.nn.softmax(attn, axis=-1).astype(x.dtype)
        qs = q[:, :, 0]
        out = jnp.einsum('bghde,bgne->bghnd', attn, qs)
        out = out.transpose(0, 2, 1, 3, 4).reshape(b, n, c)
        return out @ Wproj + bproj

    def _L1_ffn_ref(x, v_w, v_b, gate_w, gate_b, w1, b1, w2, b2, out_w, out_b, bk_scale):
        import jax, jax.numpy as jnp
        import numpy as np
        B, N, D, E, F, K = (2, 512, 192, 8, 768, 2)
        V_MAX = 3.0
        FEAT_CLAMP = 10.0

        def bk_green_diag(a):
            aT = jnp.swapaxes(a, 0, 1)

            def step(c, ai):
                d = ai - 1.0 / c
                return (d, d)
            d0 = aT[0]
            _, d_rest = jax.lax.scan(step, d0, aT[1:])
            d = jnp.concatenate([d0[None], d_rest], axis=0)
            eN = aT[-1]
            _, e_rest = jax.lax.scan(step, eN, aT[:-1], reverse=True)
            e = jnp.concatenate([e_rest, eN[None]], axis=0)
            G = 1.0 / (d + e - aT)
            return jnp.swapaxes(G, 0, 1)
        v = jnp.clip(x @ v_w + v_b, -V_MAX, V_MAX)
        a = (-2.0 + v).astype(jnp.complex64) - 1j
        G = bk_green_diag(a)
        feats = jnp.stack([G.real, G.imag], axis=-1)
        logits = x @ gate_w + gate_b
        probs = jax.nn.softmax(logits, axis=-1)
        topv, topi = jax.lax.top_k(probs, K)
        topv = topv / jnp.sum(topv, axis=-1, keepdims=True)
        comb = jnp.sum(topv[..., None] * jax.nn.one_hot(topi, E, dtype=x.dtype), axis=2)
        h = jax.nn.gelu(jnp.einsum('bnd,edf->bnef', x, w1) + b1)
        y = jnp.einsum('bnef,efd->bned', h, w2) + b2
        ffn_out = jnp.einsum('bne,bned->bnd', comb, y)
        feats_c = jnp.clip(feats, -FEAT_CLAMP, FEAT_CLAMP)
        spec_out = feats_c @ out_w + out_b
        return ffn_out + bk_scale * spec_out
    h = _L0_tok_ref(x, L0_tok_conv_w, L0_tok_conv_b, L0_tok_ln1_g, L0_tok_ln1_b, L0_tok_qkv_w, L0_tok_out_w, L0_tok_out_b, L0_tok_ln2_g, L0_tok_ln2_b, L0_tok_ff1_w, L0_tok_ff1_b, L0_tok_ff2_w, L0_tok_ff2_b, L0_tok_lnf_g, L0_tok_lnf_b, L0_tok_head_w, L0_tok_head_b)
    h = jnp.concatenate([h, txt], axis=1)
    h = h + _L0_attn_ref(_layernorm(h, axis=-1), L0_attn_W_qkv, L0_attn_b_qkv)
    h = h + _L0_ffn_ref(_layernorm(h, axis=-1), L0_ffn_ln1_g, L0_ffn_ln1_b, L0_ffn_qkv_w, L0_ffn_proj_w, L0_ffn_proj_b, L0_ffn_ln2_g, L0_ffn_ln2_b, L0_ffn_gate_w, L0_ffn_gate_b, L0_ffn_w1, L0_ffn_b1, L0_ffn_w2, L0_ffn_b2)
    h = h + _L1_attn_ref(_layernorm(h, axis=-1), L1_attn_Wq, L1_attn_Wkv, L1_attn_Wproj, L1_attn_bproj)
    h = h + _L1_ffn_ref(_layernorm(h, axis=-1), L1_ffn_v_w, L1_ffn_v_b, L1_ffn_gate_w, L1_ffn_gate_b, L1_ffn_w1, L1_ffn_b1, L1_ffn_w2, L1_ffn_b2, L1_ffn_out_w, L1_ffn_out_b, L1_ffn_bk_scale)
    return h

_drawn_inputs = setup_inputs


def setup_inputs(seed=0):
    import zlib

    import numpy as np

    out = dict(_drawn_inputs(seed))
    spreads = {'L0_tok_conv_b': (0.0, 0.1),
     'L0_tok_ln1_g': (1.0, 0.6),
     'L0_tok_ln1_b': (0.0, 0.8),
     'L0_tok_out_b': (0.0, 0.1),
     'L0_tok_ln2_g': (1.0, 0.6),
     'L0_tok_ln2_b': (0.0, 0.462),
     'L0_tok_ff1_b': (0.0, 0.1),
     'L0_tok_ff2_b': (0.0, 0.1),
     'L0_tok_lnf_g': (1.0, 0.2),
     'L0_tok_lnf_b': (0.0, 0.1),
     'L0_tok_head_b': (0.0, 0.1),
     'L0_ffn_ln1_g': (1.0, 0.6),
     'L0_ffn_ln1_b': (0.0, 0.8),
     'L0_ffn_proj_b': (0.0, 0.327),
     'L0_ffn_ln2_g': (1.0, 0.6),
     'L0_ffn_ln2_b': (0.0, 0.8),
     'L0_ffn_gate_b': (0.0, 0.558),
     'L0_ffn_b1': (0.0, 0.8),
     'L0_ffn_b2': (0.0, 0.469),
     'L1_attn_bproj': (0.0, 0.331),
     'L1_ffn_gate_b': (0.0, 0.714),
     'L1_ffn_b1': (0.0, 0.8),
     'L1_ffn_b2': (0.0, 0.478),
     'L1_ffn_out_b': (0.0, 0.315),
     'L1_ffn_bk_scale': (1.0, 0.6)}
    factors = {'L0_tok_qkv_w': 5.644,
     'L0_tok_out_w': 6.334,
     'L0_ffn_qkv_w': 8.0,
     'L0_ffn_proj_w': 8.0,
     'L0_ffn_gate_w': 3.302,
     'L0_ffn_w1': 4.13,
     'L0_ffn_w2': 3.829,
     'L1_attn_Wq': 6.181,
     'L1_attn_Wkv': 6.393,
     'L1_attn_Wproj': 6.507,
     'L1_ffn_v_w': 64.0,
     'L1_ffn_gate_w': 2.777,
     'L1_ffn_w1': 4.177,
     'L1_ffn_w2': 3.903,
     'L1_ffn_out_w': 64.0}
    for name, (base, spread) in spreads.items():
        noise = np.random.default_rng([zlib.crc32(name.encode()), seed]).standard_normal(out[name].shape)
        drawn = base * np.exp(spread * noise) if base else spread * noise
        out[name] = jnp.asarray(drawn.astype(out[name].dtype))
    for name, factor in factors.items():
        out[name] = (out[name] * factor).astype(out[name].dtype)
    return out
```

```python
import concourse.bass as bass
from concourse import mybir
from contextlib import ExitStack

F32 = mybir.dt.float32
F32R = mybir.dt.float32r
U32 = mybir.dt.uint32
ALU = mybir.AluOpType
ACT = mybir.ActivationFunctionType
AX = mybir.AxisListType

B = 2
TOK = 256
TXT = 77
N = TOK + TXT
NP = N + 1
COLS = B * NP
KP = 2048 // 128
D = 128
INNER = 512
DH = 64
LAYERS = 2
C = 192
CH = 96
ROWS = (128, 128, TXT)
NT = 3 * B
HEADS = 12
HD = 16
PAIRS = HEADS // 2
EXPERTS = 8
HID = 768
HC = HID // 128
EPS = 1e-5
G1 = 2
HG = 4
HD1 = C // (G1 * HG)
CL = 19
CN = 18
SL = CL * CN
CHAINS = 2 * B

LN_TAGS = [("t0ln1", 4), ("t0ln2", 4), ("t1ln1", 4), ("t1ln2", 4), ("tlnf", 4), ("ret", NT), ("ffn0", NT), ("ln1", NT),
           ("ln2", NT), ("att1", NT), ("ffn1", NT)]
LN_ORDER = {tag: n for n, (tag, _) in enumerate(LN_TAGS)}
LN_BASE = {tag: sum(nt for _, nt in LN_TAGS[:n]) for n, (tag, _) in enumerate(LN_TAGS)}
TURN = {tag: n for n, tag in enumerate(("ret", "ln1", "proj", "ln2", "att1", "ffn1"))}


def fusion_kernel(nc, a, out):
    ctx = ExitStack()
    with ctx:
        def sb(name, shape, dt=F32):
            return ctx.enter_context(nc.sbuf_tensor(name, shape, dt))

        def sem(name):
            return ctx.enter_context(nc.semaphore(name))

        P = ctx.enter_context(nc.psum_tensor("P", [128, 8, 512], F32))

        ident = sb("ident", [128, 128])
        neghalf = sb("neghalf", [128, 8])
        stats = sb("stats", [128, NT, 6])
        mv = sb("mv", [128, NT, 2])
        varr = sb("varr", [128, NT])
        rstd = sb("rstd", [128, NT])
        decay = sb("decay", [128, 3, N])
        rows = sb("rows", [128, 7, C])
        tokrows = sb("tokrows", [128, 5, D])
        gate_rows = sb("gate_rows", [128, 3, EXPERTS])
        tokcols = sb("tokcols", [128, 2 * (2 * LAYERS + 1)])
        ff1b = sb("ff1b", [128, LAYERS * 4])
        chcols = sb("chcols", [CH, 4 + 4 + 4])
        signs = sb("signs", [128, 2])
        b1s = sb("b1s", [128, 2, EXPERTS, HC])
        b1now = [sb(f"b1now{i}", [128, HC]) for i in range(2)]
        b2s = sb("b2s", [EXPERTS, 2, C])
        gmask = sb("gmask", [CH, HG, HD1])
        outw_rows = sb("outw_rows", [1, 2, C])

        region = {"B": sb("regB", [128, 9216]), "C": sb("regC", [128, 10432])}
        used = {"B": 0, "C": 0}
        regB = region["B"]

        def carve(where, parts, *shape):
            size = 1
            for n in shape:
                size *= n
            flat = region[where][0:parts, used[where]:used[where] + size]
            used[where] += size
            names = "abcdef"[:len(shape)]
            return flat.rearrange(f"p ({' '.join(names)}) -> p {' '.join(names)}", **dict(zip(names[1:], shape[1:]))) \
                if len(shape) > 1 else flat

        regA = sb("regA", [128, 2 * HC * COLS + 2 * 2 * PAIRS * 128])
        patches = regA[:, 0:KP * 512].rearrange("p (c n) -> p c n", c=KP)
        convw = regA[:, KP * 512:KP * 512 + KP * D].rearrange("p (c n) -> p c n", c=KP)
        hidT = [regA[:, i * HC * COLS:(i + 1) * HC * COLS].rearrange("p (c n) -> p c n", c=HC) for i in range(2)]
        wqkv = carve("C", 128, LAYERS, 3 * INNER)
        wout = carve("C", 128, LAYERS, 4, D)
        wff1 = carve("C", 128, LAYERS, 512)
        wff2 = carve("C", 128, LAYERS, 4, D)
        whead = carve("C", 128, C)
        xt = carve("C", 128, 4, D)
        yn = sb("yn", [128, NT, C])
        ynt = yn[:, 0:4, 0:D]
        yT = carve("C", 128, 512)
        qs = regB[:, 0:2048].rearrange("p (t c) -> p t c", t=4)
        vt = regB[:, 2048:4096].rearrange("p (t c) -> p t c", t=4)
        kt = regB[:, 4096:6144].rearrange("p (t c) -> p t c", t=4)
        ke = regB[:, 6144:8192].rearrange("p (c n) -> p c n", c=4)
        qT = carve("C", 128, 4, 512)
        hT = qs
        bd = carve("C", 128, B, 4, 128)
        w2 = regB[:, 8192:9216].rearrange("p (b q d) -> p b q d", b=B, q=4)
        segmax = sb("segmax", [128, 4, 8])
        segsum = sb("segsum", [128, 4, 8])
        kmax = sb("kmax", [128, 4, B])
        ksum = sb("ksum", [128, 4, B])

        x2 = region["C"][:, 10432 - NT * C:].rearrange("p (t c) -> p t c", t=NT)
        used["C"] = 0
        wva = carve("C", CH, 2, C)
        wpa = carve("C", CH, 2, C)
        w1q = carve("C", CH, 2, 64)
        w1kv = carve("C", CH, 2, 2 * C)
        w1p = carve("C", 128, 2, C)
        mixed = regB[:, NT * 2 * C + COLS:NT * 2 * C + COLS + B * 2 * N].rearrange("p (b m) -> p b m", b=B)
        cm = carve("C", CH, 4, HG, HD1)
        cc = carve("C", CH, 4, HD1)
        at = carve("C", CH, 4, 32)
        atT = carve("C", 64, B, HG, 4, 32)
        h = sb("h", [128, NT, C])
        tT = sb("tT", [CH, 2, COLS])
        lg = sb("lg", [128, NT, EXPERTS])
        m8 = sb("m8", [128, NT, 8])
        i8 = sb("i8", [128, NT, 8], U32)
        idf = sb("idf", [128, NT, 2])
        s01 = sb("s01", [128, NT, 2])
        gtmp = sb("gtmp", [128, NT])
        cwA = sb("cwA", [128, NT, EXPERTS])
        cw = sb("cw", [128, NT, EXPERTS])
        cwT = sb("cwT", [EXPERTS, COLS])
        w1s = [sb(f"w1s{i}", [CH, 2, HID]) for i in range(2)]
        w2s = [sb(f"w2s{i}", [128, HC, C]) for i in range(2)]
        qkT = regB[0:CH, 0:4 * COLS].rearrange("p (m n) -> p m n", m=4)
        sT = regB[:, 4 * COLS:4 * COLS + B * 3 * N].rearrange("p (t n) -> p t n", t=B * 3)
        vtok = regB[:, 4670:4670 + NT * C].rearrange("p (t c) -> p t c", t=NT)
        qst = sb("qst", [128, PAIRS, NP], F32R)
        khi = sb("khi", [128, 2, NP], F32R)
        kst = sb("kst", [128, PAIRS, NP], F32R)
        mx = sb("mx", [128, 3, HEADS])
        mxT = sb("mxT", [HEADS, NP], F32R)
        selw = regB[0:HEADS, 0:HEADS * 128].rearrange("p (h n) -> p h n", h=HEADS)
        selr = sb("selr", [HEADS, HEADS, 128], F32R)
        vaug = regB[:, 0:NT * HEADS * 32].rearrange("p (t h e) -> p t h e", t=NT, h=HEADS)
        pt = regB[:, 2304:2304 + 2 * 3 * N].rearrange("p (u n) -> p u n", u=6)
        ao = regB[:, 4310:4310 + 3 * N].rearrange("p (g n) -> p g n", g=3)
        rden = sb("rden", [128, 4])
        wqa = regA[0:CH, 2 * HC * COLS:].rearrange("p (k m n) -> p k m n", k=2, m=2)
        wret = sb("wret", [CH, 2, 3 * C])
        wgate = sb("wgate", [CH, 2, 2 * EXPERTS + 2])
        q1T = regB[0:64, NT * 2 * C:NT * 2 * C + COLS]
        kv = regB[:, 0:NT * 2 * C].rearrange("p (t c) -> p t c", t=NT)
        c1 = sb("c1", [CH, 4])
        used["B"] = used["C"] = 0
        sE = carve("B", 1, 2 + CL, 2, 2, CHAINS, CN)
        sc = carve("B", 1, 6, 2, CHAINS, CN)
        st = carve("B", 1, 8, 2, CHAINS, CN)
        sa = carve("C", 1, CHAINS, SL)
        sG = carve("C", 1, CL, 2, CHAINS, CN)
        start_ = carve("C", 1, 2, CHAINS, CN)
        gf = carve("C", 1, B, 2, SL)
        negone = carve("C", 1, B * SL)
        ftmp = carve("C", 1, 4, N)

        S = {}

        def s(name):
            if name not in S:
                S[name] = sem(name)
            return S[name]

        block = ctx.enter_context(nc.Block())

        def col(i):
            return (i // 3) * NP + (i % 3) * 128

        def vlayernorm_stats(dve, tag, src, nt):
            for t in range(nt):
                nc.vector.bn_stats(stats[:, t, :], src[:, t, :]).then_inc(s("ln_stats"), 1)
            dve.wait_ge(s("ln_stats"), LN_BASE[tag] + nt)
            for t in range(nt):
                nc.vector.bn_aggr(mv[:, t, :], stats[:, t, :]).then_inc(s("ln_mean"), 1)

        def vlayernorm_apply(dve, tag, dst, src, nt):
            dve.wait_ge(s("ln_mean"), LN_BASE[tag] + nt)
            dve.wait_ge(s("ln_rstd"), LN_ORDER[tag] + 1)
            for t in range(nt):
                nc.vector.tensor_scalar(dst[:, t, :], src[:, t, :], mv[:, t, 0:1], rstd[:, t:t + 1],
                                        ALU.subtract, ALU.mult).then_inc(s("ln_norm"), 1)

        def vlayernorm(dve, tag, dst, src, nt):
            vlayernorm_stats(dve, tag, src, nt)
            vlayernorm_apply(dve, tag, dst, src, nt)

        def prstd(pool, tag, nt):
            pool.wait_ge(s("ln_mean"), LN_BASE[tag] + nt)
            nc.gpsimd.tensor_scalar(varr[:, 0:nt], mv[:, 0:nt, 1], EPS, 0.0, ALU.add, ALU.add)\
                .then_inc(s("ln_var"), 1)
            pool.wait_ge(s("ln_var"), LN_ORDER[tag] + 1)
            nc.gpsimd.tensor_tensor(rstd[:, 0:nt], varr[:, 0:nt], neghalf[:, 0:nt], ALU.pow)\
                .then_inc(s("ln_rstd"), 1)

        def reshuffled(u, quarter):
            b, first = u // 8, (u % 8) * N
            skip = (quarter - first) % 4
            n = (N - skip + 3) // 4
            m = (first + skip - quarter) // 4
            part = slice(32 * quarter, 32 * quarter + 32)
            return mixed[part, b, m:m + n], P[part, 4 + u % 4, skip:skip + 4 * (n - 1) + 1:4]

        def ttranspose(pe, tag, src):
            for i in range(NT):
                if tag != "proj":
                    pe.wait_ge(s("ln_norm"), LN_BASE[tag] + i + 1)
                r = ROWS[i % 3]
                for k in range(2):
                    last = nc.tensor.transpose(P[0:CH, (i // 3) * 2 + k, (i % 3) * 128:(i % 3) * 128 + r],
                                               src[0:r, i, k * CH:(k + 1) * CH], ident[0:r, 0:r])
                if i % 3 == 2:
                    last.then_inc(s("turned"), 1)

        def aevacuate(act, tag, cols):
            for b in range(B):
                act.wait_ge(s("turned"), B * TURN[tag] + b + 1)
                for k in range(2):
                    dst, src = tT[:, k, b * NP:b * NP + N], P[0:CH, b * 2 + k, 0:N]
                    if cols is None:
                        last = nc.scalar.activation(dst, src, ACT.Copy)
                    else:
                        last = nc.scalar.activation(dst, src, ACT.Identity, bias=chcols[:, cols + 2 + k:cols + 3 + k],
                                                    scale=chcols[:, cols + k:cols + k + 1])
                    last.then_inc(s("turned_out"), 1)

        def spectral(pool):
            count = [0]
            g = nc.gpsimd

            def link(ins):
                count[0] += 1
                ins.then_inc(s("spec_step"), 1)
                pool.wait_ge(s("spec_step"), count[0])

            av = sa[:, :, :].rearrange("o x (n l) -> o x n l", l=CL)

            def recip(re_o, im_o, re, im, sl):
                link(g.tensor_tensor(st[:, 0, 0][sl], re, re, ALU.mult))
                link(g.tensor_tensor(st[:, 0, 1][sl], im, im, ALU.mult))
                link(g.tensor_tensor(st[:, 1, 0][sl], st[:, 0, 0][sl], st[:, 0, 1][sl], ALU.add))
                link(g.tensor_tensor(st[:, 1, 1][sl], st[:, 1, 0][sl], neg[sl], ALU.pow))
                link(g.tensor_tensor(re_o, re, st[:, 1, 1][sl], ALU.mult))
                link(g.tensor_tensor(st[:, 2, 0][sl], im, st[:, 1, 1][sl], ALU.mult))
                link(g.tensor_scalar(im_o, st[:, 2, 0][sl], -1.0, 0.0, ALU.mult, ALU.add))

            neg = negone[:, 0:CHAINS * CN].rearrange("o (x n) -> o x n", x=CHAINS)
            full = (slice(None), slice(None), slice(None))
            one = (slice(None), slice(None), slice(0, 1))
            pool.wait_ge(s("sa_ready"), 2 * B)
            link(g.memset(negone[:, :], -1.0))
            link(g.memset(start_[:, :, :, :], 0.0))
            link(g.memset(sE[:, 0:2, :, :, :, :], 0.0))
            link(g.memset(sE[:, 0, 1, 0, :, :], 1.0))
            link(g.memset(sE[:, 1, 0, 0, :, :], 1.0))
            link(g.tensor_scalar(sa[:, :, 0:N], sa[:, :, 0:N], 3.0, -3.0, ALU.min, ALU.max))
            link(g.tensor_scalar(sa[:, :, 0:N], sa[:, :, 0:N], -2.0, 0.0, ALU.add, ALU.add))
            for i in range(CL):
                for w in range(2):
                    new, p1, p2 = sE[:, i + 2, w], sE[:, i + 1, w], sE[:, i, w]
                    arw = av[:, :, :, i]
                    for z in range(2):
                        link(g.tensor_tensor(st[:, 3 + z, 0], p1[:, z], arw, ALU.mult))
                        link(g.tensor_tensor(st[:, 5 + z, 0], st[:, 3 + z, 0], p2[:, z], ALU.subtract))
                    link(g.tensor_tensor(new[:, 0], st[:, 5, 0], p1[:, 1], ALU.add))
                    link(g.tensor_tensor(new[:, 1], st[:, 6, 0], p1[:, 0], ALU.subtract))
            for n in range(CN - 1):
                ur, ui = start_[:, 0, :, n:n + 1], start_[:, 1, :, n:n + 1]

                def mobius(dst, row):
                    ar, ai = sE[:, row, 0, 0, :, n:n + 1], sE[:, row, 0, 1, :, n:n + 1]
                    br, bi = sE[:, row, 1, 0, :, n:n + 1], sE[:, row, 1, 1, :, n:n + 1]
                    t = lambda q: st[:, q, 0, :, 0:1]
                    link(g.tensor_tensor(t(3), br, ur, ALU.mult))
                    link(g.tensor_tensor(t(4), bi, ui, ALU.mult))
                    link(g.tensor_tensor(t(5), br, ui, ALU.mult))
                    link(g.tensor_tensor(t(6), bi, ur, ALU.mult))
                    link(g.tensor_tensor(t(3), t(3), t(4), ALU.subtract))
                    link(g.tensor_tensor(t(5), t(5), t(6), ALU.add))
                    link(g.tensor_tensor(dst[:, 0, :, 0:1], ar, t(3), ALU.add))
                    link(g.tensor_tensor(dst[:, 1, :, 0:1], ai, t(5), ALU.add))

                mobius(sc[:, 0], CL + 1)
                mobius(sc[:, 1], CL)
                recip(sc[:, 2, 0, :, 0:1], sc[:, 2, 1, :, 0:1], sc[:, 0, 0, :, 0:1], sc[:, 0, 1, :, 0:1], one)
                wr, wi = sc[:, 2, 0, :, 0:1], sc[:, 2, 1, :, 0:1]
                dr, di = sc[:, 1, 0, :, 0:1], sc[:, 1, 1, :, 0:1]
                t = lambda q: st[:, q, 0, :, 0:1]
                link(g.tensor_tensor(t(3), dr, wr, ALU.mult))
                link(g.tensor_tensor(t(4), di, wi, ALU.mult))
                link(g.tensor_tensor(t(5), dr, wi, ALU.mult))
                link(g.tensor_tensor(t(6), di, wr, ALU.mult))
                link(g.tensor_tensor(start_[:, 0, :, n + 1:n + 2], t(3), t(4), ALU.subtract))
                link(g.tensor_tensor(start_[:, 1, :, n + 1:n + 2], t(5), t(6), ALU.add))
            for i in range(CL):
                if i == 0:
                    ur, ui = start_[:, 0], start_[:, 1]
                else:
                    recip(sc[:, 3, 0], sc[:, 3, 1], sG[:, i - 1, 0], sG[:, i - 1, 1], full)
                    ur, ui = sc[:, 3, 0], sc[:, 3, 1]
                link(g.tensor_tensor(sG[:, i, 0], av[:, :, :, i], ur, ALU.subtract))
                link(g.tensor_scalar(sG[:, i, 1], ui, -1.0, -1.0, ALU.mult, ALU.add))
            for b in range(B):
                for z in range(2):
                    fw = sG[:, :, z, b, :].rearrange("o l n -> o n l")
                    link(g.tensor_copy(gf[:, b, z, :].rearrange("o (n l) -> o n l", l=CL), fw))
                    bw = sG[:, :, z, B + b, :].rearrange("o l n -> o n l")
                    link(g.tensor_copy(sa[:, B + b, :].rearrange("o (n l) -> o n l", l=CL), bw))
                    link(g.tensor_tensor(gf[:, b, z, 0:N], gf[:, b, z, 0:N], sa[:, B + b, 0:N][:, ::-1], ALU.add))
                link(g.tensor_tensor(gf[:, b, 0, 0:N], gf[:, b, 0, 0:N], sa[:, b, 0:N], ALU.subtract))
                link(g.tensor_scalar(gf[:, b, 1, 0:N], gf[:, b, 1, 0:N], 1.0, 0.0, ALU.add, ALU.add))
                r2, i2, m2, rc = (ftmp[:, k, :] for k in range(4))
                gr, gi = gf[:, b, 0, 0:N], gf[:, b, 1, 0:N]
                link(g.tensor_tensor(r2, gr, gr, ALU.mult))
                link(g.tensor_tensor(i2, gi, gi, ALU.mult))
                link(g.tensor_tensor(m2, r2, i2, ALU.add))
                link(g.tensor_tensor(rc, m2, negone[:, 0:N], ALU.pow))
                link(g.tensor_tensor(gr, gr, rc, ALU.mult))
                link(g.tensor_tensor(gi, gi, rc, ALU.mult))
                link(g.tensor_scalar(gr, gr, 10.0, -10.0, ALU.min, ALU.max))
                g.tensor_scalar(gi, gi, -1.0, 0.0, ALU.mult, ALU.add).then_inc(s("spec_step"), 1)
                count[0] += 1
                pool.wait_ge(s("spec_step"), count[0])
                g.tensor_scalar(gi, gi, 10.0, -10.0, ALU.min, ALU.max).then_inc(s("feats_ready"), 1)

        def moe_act(act, moe):
            m = f"m{moe}"
            aevacuate(act, "ln2" if moe == 0 else "ffn1", 8 if moe == 0 else None)
            act.wait_ge(s(m + "_gate_in"), 1)
            if moe == 0:
                nc.scalar.activation(gtmp[:, :], gtmp[:, :], ACT.Exp).then_inc(s(m + "_gate_exp"), 1)
            else:
                nc.scalar.activation(lg[:, :, :], lg[:, :, :], ACT.Exp).then_inc(s(m + "_gate_exp"), 1)
            act.wait_ge(s(m + "_cwT"), 1)
            nc.scalar.activation(cwT[:, :].rearrange("e (b n) -> e b n", b=B)[:, :, 0:N], P[0:EXPERTS, 0:2, 0:N],
                                 ACT.Copy).then_inc(s(m + "_cwT_out"), 1)
            with act.Fori(0, EXPERTS // 2) as i:
                for par in range(2):
                    nc.scalar.activation(b1now[par][:, :], b1s[:, moe, bass.ds(i * 2 + par, 1), :], ACT.Copy)\
                        .then_inc(s(m + "_b1"), 1)
                    act.wait_ge(s(m + "_b1"), i * 2 + par + 1)
                    for c in range(HC):
                        for b in range(B):
                            u = c * B + b
                            act.wait_ge(s(m + "_h1"), (i * 2 + par) * (HC * B) + u + 1)
                            nc.scalar.activation(hidT[par][:, c, b * NP:b * NP + N], P[:, u % 4, 0:N],
                                                 ACT.Gelu if moe == 0 else ACT.Gelu_apprx_tanh,
                                                 bias=b1now[par][:, c:c + 1]).then_inc(s(m + "_hid"), 1)

        def moe_vector(dve, moe, acc, link):
            v = nc.vector
            m = f"m{moe}"
            dve.wait_ge(s(m + "_logits"), 1)
            dve.wait_ge(s("pads_zeroed"), 3)
            for i in range(NT):
                r = ROWS[i % 3]
                link(v.tensor_tensor(lg[0:r, i, :], P[0:r, 4, i * 8:i * 8 + 8], gate_rows[0:r, moe, :], ALU.add))
            if moe == 1:
                link(v.tensor_reduce(gtmp[:, :], lg[:, :, :], AX.X, ALU.max))
                v.tensor_tensor(lg[:, :, :], lg[:, :, :], gtmp[:, :].unsqueeze(2).broadcast_to([128, NT, 8]), ALU.subtract)\
                    .then_inc(s(m + "_gate_in"), 1)
                dve.wait_ge(s(m + "_gate_exp"), 1)
                link(v.tensor_reduce(gtmp[:, :], lg[:, :, :], AX.X, ALU.add))
                link(v.reciprocal(gtmp[:, :], gtmp[:, :]))
                link(v.tensor_tensor(lg[:, :, :], lg[:, :, :], gtmp[:, :].unsqueeze(2).broadcast_to([128, NT, 8]), ALU.mult))
            for i in range(NT):
                link(v.max(m8[:, i, :], lg[:, i, :]))
                link(v.max_index(i8[:, i, :], m8[:, i, :], lg[:, i, :]))
            link(v.tensor_copy(idf[:, :, :], i8[:, :, 0:2]))
            if moe == 0:
                v.tensor_tensor(gtmp[:, :], m8[:, :, 1], m8[:, :, 0], ALU.subtract).then_inc(s(m + "_gate_in"), 1)
                dve.wait_ge(s(m + "_gate_exp"), 1)
                link(v.tensor_scalar(s01[:, :, 0], gtmp[:, :], 1.0, None, ALU.add))
                link(v.reciprocal(s01[:, :, 0], s01[:, :, 0]))
                link(v.tensor_tensor(s01[:, :, 1], s01[:, :, 0], gtmp[:, :], ALU.mult))
            else:
                link(v.tensor_tensor(gtmp[:, :], m8[:, :, 0], m8[:, :, 1], ALU.add))
                link(v.reciprocal(gtmp[:, :], gtmp[:, :]))
                link(v.tensor_tensor(s01[:, :, :], m8[:, :, 0:2], gtmp[:, :].unsqueeze(2).broadcast_to([128, NT, 2]), ALU.mult))
            for i in range(NT):
                link(v.tensor_scalar(cwA[:, i, :], gate_rows[:, 2, :], idf[:, i, 0:1], s01[:, i, 0:1], ALU.is_equal, ALU.mult))
                link(v.tensor_scalar(cw[:, i, :], gate_rows[:, 2, :], idf[:, i, 1:2], s01[:, i, 1:2], ALU.is_equal, ALU.mult))
                v.tensor_tensor(cw[:, i, :], cw[:, i, :], cwA[:, i, :], ALU.add).then_inc(s(m + "_cw"), 1)
            for i in range(NT):
                r = ROWS[i % 3]
                dve.wait_ge(s(m + "_b2"), i + 1)
                v.tensor_tensor(acc[0:r, i, :], acc[0:r, i, :], P[0:r, 4 + i % 4, 0:C], ALU.add).then_inc(s(m + "_acc"), 1)
            with dve.Fori(0, EXPERTS) as e:
                for i in range(NT):
                    r = ROWS[i % 3]
                    dve.wait_ge(s(m + "_y"), e * NT + i + 1)
                    dve.wait_ge(s(m + "_acc"), e * NT + i + 1)
                    v.scalar_tensor_tensor(acc[0:r, i, :], P[0:r, 4 + i % 4, 0:C], cw[0:r, i, bass.ds(e, 1)], acc[0:r, i, :],
                                           ALU.mult, ALU.add).then_inc(s(m + "_acc"), 1)
            dve.wait_ge(s(m + "_acc"), NT * (EXPERTS + 1))

        def moe_tensor(pe, moe):
            mm = nc.tensor.matmul
            m = f"m{moe}"
            tag = "ln2" if moe == 0 else "ffn1"
            ttranspose(pe, tag, yn)
            pe.wait_ge(s("turned_out"), 2 * B * TURN[tag] + 2 * B)
            for i in range(NT):
                r = ROWS[i % 3]
                for k in range(2):
                    last = mm(P[0:r, 4, i * 8:i * 8 + 8], tT[:, k, col(i):col(i) + r], wgate[:, k, 8 * moe:8 * moe + 8],
                              start=(k == 0), stop=(k == 1))
            last.then_inc(s(m + "_logits"), 1)
            if moe == 1:
                for b in range(B):
                    for k in range(2):
                        last = mm(P[0:1, 6 + b, 0:N], wgate[:, k, 16:17], tT[:, k, b * NP:b * NP + N], start=(k == 0), stop=(k == 1))
                    last.then_inc(s("spec_v"), 1)
            for i in range(NT):
                r = ROWS[i % 3]
                pe.wait_ge(s(m + "_cw"), i + 1)
                last = nc.tensor.transpose(P[0:EXPERTS, i // 3, (i % 3) * 128:(i % 3) * 128 + r], cw[0:r, i, :], ident[0:r, 0:r])
            last.then_inc(s(m + "_cwT"), 1)
            pe.wait_ge(s(m + "_cwT_out"), 1)
            if moe == 1:
                pe.wait_ge(s("sa_ready"), 2 * B)
            for i in range(NT):
                r = ROWS[i % 3]
                if i >= 4:
                    pe.wait_ge(s(m + "_acc"), i - 3)
                mm(P[0:r, 4 + i % 4, 0:C], cwT[:, col(i):col(i) + r], b2s[:, moe, :], start=True, stop=True)\
                    .then_inc(s(m + "_b2"), 1)
            with pe.Fori(0, EXPERTS // 2) as e2:
                for par in range(2):
                    e = e2 * 2 + par
                    pe.wait_ge(s(f"w1_in{par}"), (e2 + 1 + moe * (EXPERTS // 2)) * 16)
                    pe.wait_ge(s(f"w2_in{par}"), (e2 + 1 + moe * (EXPERTS // 2)) * 16)
                    for c in range(HC):
                        for b in range(B):
                            u = c * B + b
                            if u >= 4:
                                pe.wait_ge(s(m + "_hid"), e * (HC * B) + u - 3)
                            for k in range(2):
                                last = mm(P[:, u % 4, 0:N], w1s[par][:, k, c * 128:(c + 1) * 128],
                                          tT[:, k, b * NP:b * NP + N], start=(k == 0), stop=(k == 1))
                            last.then_inc(s(m + "_h1"), 1)
                    pe.wait_ge(s(m + "_hid"), (e + 1) * (HC * B))
                    for i in range(NT):
                        r = ROWS[i % 3]
                        pe.wait_ge(s(m + "_acc"), e * NT + i + (5 if i < 2 else 1 if i < 4 else 3))
                        for c in range(HC):
                            last = mm(P[0:r, 4 + i % 4, 0:C], hidT[par][:, c, col(i):col(i) + r], w2s[par][:, c, :],
                                      start=(c == 0), stop=(c == HC - 1))
                        last.then_inc(s(m + "_y"), 1)

        @block.sync
        def _(sp):
            pat = a["patches"].rearrange("(c p) n -> p c n", p=128)
            cwv = a["conv_w"].rearrange("(c p) n -> p c n", p=128)
            for g in range(4):
                sp.dma_start(convw[:, 4 * g:4 * g + 4, :], cwv[:, 4 * g:4 * g + 4, :]).then_inc(s(f"patches_in{g}"), 16)
                sp.dma_start(patches[:, 4 * g:4 * g + 4, :], pat[:, 4 * g:4 * g + 4, :]).then_inc(s(f"patches_in{g}"), 16)
            for n, (dst, name, pat_) in enumerate([
                    (wqkv[:, :, :], "qkv_w", "l p n -> p l n"), (wout[:, :, :, :], "out_w", "l (q p) n -> p l q n"),
                    (wff1[:, :, :], "ff1_w", "l p n -> p l n"), (wff2[:, :, :, :], "ff2_w", "l (q p) n -> p l q n")]):
                kw = {"p": 128} if "q" in pat_ else {}
                src = a[name].rearrange(pat_, **kw)
                if n in (1, 3):
                    for l in range(LAYERS):
                        sp.dma_start(dst[:, l, :, :], src[:, l, :, :]).then_inc(s("tok_weights_in"), 16)
                else:
                    sp.dma_start(dst, src).then_inc(s("tok_weights_in"), 16)
            sp.dma_start(whead[:, :], a["head_w"]).then_inc(s("tok_weights_in"), 16)
            for dst, name in ((wret, "ret_w"), (wgate, "gate_w")):
                sp.dma_start(dst[:, :, :], a[name].rearrange("(k p) n -> p k n", p=CH)).then_inc(s("weights_in"), 16)
            sp.wait_ge(s("conv"), 4)
            for m in range(2):
                sp.dma_start(wqa[:, :, m, :], a["qk_w"][m].rearrange("(k p) n -> p k n", p=CH)).then_inc(s("weights_in"), 16)
            sp.wait_ge(s("head"), 4)
            for dst, name in ((wva, "v_w"), (wpa, "proj_w"), (w1q, "q1_w"), (w1kv, "kv1_w")):
                sp.dma_start(dst[:, :, :], a[name].rearrange("(k p) n -> p k n", p=CH)).then_inc(s("attention_weights_in"), 16)
            sp.dma_start(w1p[:, :, :], a["proj1_w"]).then_inc(s("attention_weights_in"), 16)
            for moe in range(2):
                for e in range(EXPERTS):
                    par, turn = e % 2, moe * EXPERTS + e
                    if turn >= 2:
                        sp.wait_ge(s(f"m{(turn - 2) // EXPERTS}_y"), ((turn - 2) % EXPERTS + 1) * NT)
                    sp.dma_start(w1s[par][:, :, :], a["w1"][moe, e].rearrange("(k p) n -> p k n", p=CH))\
                        .then_inc(s(f"w1_in{par}"), 16)
                    sp.dma_start(w2s[par][:, :, :], a["w2"][moe, e].rearrange("(k p) n -> p k n", p=128))\
                        .then_inc(s(f"w2_in{par}"), 16)
            ov = out
            for b in range(B):
                for j in range(3):
                    sp.wait_ge(s("out_ready"), b * 3 + j + 1)
                    sp.dma_start(ov[b, j * 128:j * 128 + ROWS[j], :], h[0:ROWS[j], b * 3 + j, :]).then_inc(s("out_stored"), 16)
            sp.wait_ge(s("out_stored"), 16 * NT)

        @block.gpsimd
        def _(pool):
            nc.gpsimd.memset(neghalf[:, :], -0.5).then_inc(s("neghalf_set"), 1)
            nc.gpsimd.memset(h[:, :, :], 0.0).then_inc(s("h_zeroed"), 1)
            nc.gpsimd.memset(bd[:, :, :, :], 0.0).then_inc(s("bd_zeroed"), 1)
            nc.gpsimd.memset(tT[:, :, :], 0.0).then_inc(s("pads_zeroed"), 1)
            nc.gpsimd.memset(mx[:, :, :], 0.0).then_inc(s("pads_zeroed"), 1)
            nc.gpsimd.memset(yn[:, :, :], 0.0).then_inc(s("yn_zeroed"), 1)
            nc.gpsimd.memset(lg[:, :, :], 0.0).then_inc(s("pads_zeroed"), 1)
            pool.wait_ge(s("neghalf_set"), 1)
            pool.wait_ge(s("consts_in"), 16 * 12)
            nc.gpsimd.tensor_copy(selr[:, :, :], selw[:, :, :]).then_inc(s("selr_set"), 1)
            for l in range(LAYERS):
                prstd(pool, f"t{l}ln1", 4)
                prstd(pool, f"t{l}ln2", 4)
            prstd(pool, "tlnf", 4)
            for tag in ("ret", "ffn0", "ln1", "ln2", "att1", "ffn1"):
                prstd(pool, tag, NT)
            nc.gpsimd.memset(sa[:, :, N:SL], 0.0).then_inc(s("sa_zeroed"), 1)
            spectral(pool)

        @block.scalar
        def _(act):
            one = lambda x: x.rearrange("(o n) -> o n", o=1)
            for dst, src in ((ident[:, :], a["ident"]), (tokrows[:, :, :], a["tok_rows"].partition_broadcast(128)),
                             (tokcols[:, :], a["tok_cols"]), (ff1b[:, :], a["ff1_b"]), (chcols[:, :], a["ch_cols"]),
                             (signs[:, :], a["signs"]), (selw[:, :, :], a["sel"]), (rows[:, :, :], a["rows"].partition_broadcast(128)),
                             (gate_rows[:, :, :], a["gate_rows"].partition_broadcast(128)), (decay[:, :, :], a["decay"]),
                             (b1s[:, :, :, :], a["b1"]), (b2s[:, :, :], a["b2"].rearrange("m e c -> e m c"))):
                act.dma_start(dst, src).then_inc(s("consts_in"), 16)
            act.dma_start(gmask[:, :, :], a["gmask"]).then_inc(s("late_in"), 16)
            act.dma_start(outw_rows[:, :, :], a["outw_rows"]).then_inc(s("late_in"), 16)
            act.wait_ge(s("h_zeroed"), 1)
            for b in range(B):
                act.dma_start(h[0:TXT, b * 3 + 2, :], a["txt"][b]).then_inc(s("txt_in"), 16)
            act.wait_ge(s("consts_in"), 16 * 12)
            for l in range(LAYERS):
                t = f"t{l}"
                act.wait_ge(s("tok_turned"), 2 * l + 1)
                nc.scalar.activation(yT[:, :], P[:, 0, :], ACT.Identity, bias=tokcols[:, 4 * l + 1:4 * l + 2],
                                     scale=tokcols[:, 4 * l:4 * l + 1]).then_inc(s("tok_y"), 1)
                for q in range(4):
                    act.wait_ge(s("tok_kmax"), 4 * l + q + 1)
                    for b in range(B):
                        nc.scalar.activation(ke[:, q, b * TOK:(b + 1) * TOK], P[:, 4 + q, b * TOK:(b + 1) * TOK], ACT.Exp,
                                             bias=kmax[:, q, b:b + 1], accum_out=ksum[:, q, b:b + 1]).then_inc(s("tok_kexp"), 1)
                for q in range(4):
                    act.wait_ge(s("tok_qsub"), 4 * l + q + 1)
                    nc.scalar.activation(qs[:, q, :], qs[:, q, :], ACT.Exp).then_inc(s("tok_qexp"), 1)
                for q in range(4):
                    act.wait_ge(s("tok_v"), 4 * l + q + 1)
                    nc.scalar.activation(vt[:, q, :], P[:, q, :], ACT.Copy).then_inc(s("tok_vout"), 1)
                for q in range(4):
                    act.wait_ge(s("tok_kturned"), 4 * l + q + 1)
                    nc.scalar.activation(kt[:, :, q * 128:(q + 1) * 128], P[:, 4 + q, :].rearrange("p (t c) -> p t c", t=4),
                                         ACT.Copy).then_inc(s("tok_kt"), 1)
                for q in range(4):
                    act.wait_ge(s("tok_qturned"), 4 * l + q + 1)
                    nc.scalar.activation(qT[:, :, q * 128:(q + 1) * 128], P[:, q, :].rearrange("p (c n) -> p c n", c=4),
                                         ACT.Copy).then_inc(s("tok_qT"), 1)
                act.wait_ge(s("tok_turned"), 2 * l + 2)
                nc.scalar.activation(yT[:, :], P[:, 0, :], ACT.Identity, bias=tokcols[:, 4 * l + 3:4 * l + 4],
                                     scale=tokcols[:, 4 * l + 2:4 * l + 3]).then_inc(s("tok_y"), 1)
                for q in range(4):
                    act.wait_ge(s("tok_ff1"), 4 * l + q + 1)
                    nc.scalar.activation(hT[:, q, :], P[:, 4 + q, :], ACT.Gelu, bias=ff1b[:, 4 * l + q:4 * l + q + 1])\
                        .then_inc(s("tok_gelu"), 1)
            act.wait_ge(s("tok_turned"), 2 * LAYERS + 1)
            nc.scalar.activation(yT[:, :], P[:, 0, :], ACT.Identity, bias=tokcols[:, 9:10],
                                 scale=tokcols[:, 8:9]).then_inc(s("tok_y"), 1)
            act.wait_ge(s("pads_zeroed"), 3)
            aevacuate(act, "ret", None)
            for m in range(4):
                for b in range(B):
                    u = m * B + b
                    act.wait_ge(s("ret_qk"), u + 1)
                    nc.scalar.activation(qkT[:, m, b * NP:b * NP + N], P[0:CH, 4 + u % 4, 0:N], ACT.Identity,
                                         bias=chcols[:, m:m + 1]).then_inc(s("ret_qk_out"), 1)
            aevacuate(act, "ln1", 4)
            for b in range(B):
                for p in range(PAIRS):
                    u = b * PAIRS + p
                    act.wait_ge(s("qk_stack"), u + 1)
                    if u >= 2:
                        act.wait_ge(s("k_lo"), u - 1)
                    if b == 1 and p == 0:
                        act.wait_ge(s("att_scoresT"), 3 * HEADS)
                    nc.scalar.activation(qst[:, p, :], P[:, 2 * (u % 2), 0:NP], ACT.Identity,
                                         scale=signs[:, 0:1]).then_inc(s("q_hi"), 1)
                    nc.scalar.activation(khi[:, u % 2, :], P[:, 2 * (u % 2) + 1, 0:NP], ACT.Copy).then_inc(s("k_hi"), 1)
                act.wait_ge(s("att_maxT"), b + 1)
                nc.scalar.activation(mxT[:, 0:N], P[0:HEADS, 0, 0:N], ACT.Copy).then_inc(s("att_max_out"), 1)
                if b == 0:
                    nc.scalar.activation(mxT[:, N:NP], ident[0:HEADS, 127:128], ACT.Copy).then_inc(s("att_max_pad"), 1)
                for hh in range(HEADS):
                    for j in range(3):
                        u = (b * HEADS + hh) * 3 + j
                        r = ROWS[j]
                        act.wait_ge(s("att_scoresT"), u + 1)
                        if u >= 6:
                            act.wait_ge(s("att_pv"), u - 5)
                        nc.scalar.activation(pt[0:r, u % 6, :], P[0:r, 4 + u % 2, 0:N], ACT.Exp).then_inc(s("att_exp"), 1)
                    if hh % 4 == 3:
                        grp = b * 3 + hh // 4
                        act.wait_ge(s("att_pv"), (b * HEADS + hh + 1) * 3)
                        if grp >= 3:
                            act.wait_ge(s("att_o_turned"), 3 * (grp - 2))
                        nc.scalar.activation(ao[:, grp % 3, :], P[:, 6, 0:N], ACT.Copy).then_inc(s("att_ao"), 1)
            aevacuate(act, "proj", None)
            moe_act(act, 0)
            aevacuate(act, "att1", None)
            for b in range(B):
                act.wait_ge(s("q1"), b + 1)
                nc.scalar.activation(q1T[:, b * NP:b * NP + N], P[0:64, 4 + b, 0:N], ACT.Copy).then_inc(s("q1_out"), 1)
            for i in range(NT):
                act.wait_ge(s("kv1"), i + 1)
                r = ROWS[i % 3]
                nc.scalar.activation(kv[0:r, i, :], P[0:r, i % 4, 0:2 * C], ACT.Copy).then_inc(s("kv1_out"), 1)
            act.wait_ge(s("ctx_sub"), 1)
            nc.scalar.activation(cc[:, :, :], cc[:, :, :], ACT.Exp, scale=float(HD1) ** -0.5).then_inc(s("ctx_exp"), 1)
            for u in range(0, 2 * HG * G1, 2):
                act.wait_ge(s("heads1"), u + 1)
                for quarter in range(4):
                    dst, src = reshuffled(u, quarter)
                    last = nc.scalar.activation(dst, src, ACT.Copy)
                last.then_inc(s("heads1_even"), 1)
            moe_act(act, 1)

        @block.vector
        def _(dve):
            count = [0]

            def link(ins):
                count[0] += 1
                ins.then_inc(s("dve_step"), 1)
                dve.wait_ge(s("dve_step"), count[0])

            v = nc.vector
            dve.wait_ge(s("consts_in"), 16 * 12)
            dve.wait_ge(s("yn_zeroed"), 1)
            for t in range(4):
                dve.wait_ge(s("conv"), t + 1)
                link(v.tensor_tensor(xt[:, t, :], P[:, t, 0:D], tokrows[:, 0, :], ALU.add))

            for l in range(LAYERS):
                t = f"t{l}"
                vlayernorm(dve, t + "ln1", ynt, xt, 4)
                for q in range(4):
                    dve.wait_ge(s("tok_k"), 4 * l + q + 1)
                    link(v.tensor_reduce(kmax[:, q, :], P[:, 4 + q, :].rearrange("p (b n) -> p b n", b=B), AX.X, ALU.max))
                    v.tensor_scalar(kmax[:, q, :], kmax[:, q, :], -1.0, None, ALU.mult).then_inc(s("tok_kmax"), 1)
                for q in range(4):
                    dve.wait_ge(s("tok_q"), 4 * l + q + 1)
                    dve.wait_ge(s("selr_set"), 1)
                    seg = P[:, q, :].rearrange("p (h d) -> p h d", d=DH)
                    link(v.tensor_reduce(segmax[:, q, :], seg, AX.X, ALU.max))
                    v.tensor_tensor(qs[:, q, :].rearrange("p (h d) -> p h d", d=DH), seg,
                                    segmax[:, q, :].unsqueeze(2).broadcast_to([128, 8, DH]), ALU.subtract)\
                        .then_inc(s("tok_qsub"), 1)
                for q in range(4):
                    dve.wait_ge(s("tok_qexp"), 4 * l + q + 1)
                    seg = qs[:, q, :].rearrange("p (h d) -> p h d", d=DH)
                    link(v.tensor_reduce(segsum[:, q, :], seg, AX.X, ALU.add))
                    link(v.reciprocal(segsum[:, q, :], segsum[:, q, :]))
                    link(v.tensor_scalar(segsum[:, q, :], segsum[:, q, :], DH ** -0.5, None, ALU.mult))
                    v.tensor_tensor(seg, seg, segsum[:, q, :].unsqueeze(2).broadcast_to([128, 8, DH]), ALU.mult)\
                        .then_inc(s("tok_qsoft"), 1)
                dve.wait_ge(s("tok_kexp"), 8 * l + 8)
                v.reciprocal(ksum[:, :, :], ksum[:, :, :]).then_inc(s("tok_kinv"), 1)
                for b in range(B):
                    dve.wait_ge(s("tok_ctx"), 2 * l + b + 1)
                    if l == 0 and b == 0:
                        dve.wait_ge(s("bd_zeroed"), 1)
                    for z in range(2):
                        r = slice(64 * z, 64 * z + 64)
                        v.tensor_copy(bd[r, b, :, 64 * z:64 * z + 64],
                                      P[r, 4 + b, :].rearrange("p (q d) -> p q d", q=4)[:, :, 64 * z:64 * z + 64])\
                            .then_inc(s("tok_bd"), 1)
                dve.wait_ge(s("tok_kinv"), 1 * l + 1)
                for b in range(B):
                    dve.wait_ge(s("tok_w2"), 2 * l + b + 1)
                    v.tensor_tensor(w2[:, b, :, :], P[:, 6 + b, :].rearrange("p (q d) -> p q d", q=4),
                                    ksum[:, :, b].unsqueeze(2).broadcast_to([128, 4, D]), ALU.mult).then_inc(s("tok_w2_out"), 1)
                for i in range(4):
                    dve.wait_ge(s("tok_att"), 4 * l + i + 1)
                    link(v.tensor_tensor(xt[:, i, :], xt[:, i, :], P[:, 4 + i, 0:D], ALU.add))
                    link(v.tensor_tensor(xt[:, i, :], xt[:, i, :], tokrows[:, 1 + l, :], ALU.add))
                vlayernorm(dve, t + "ln2", ynt, xt, 4)
                for i in range(4):
                    dve.wait_ge(s("tok_ff2"), 4 * l + i + 1)
                    link(v.tensor_tensor(xt[:, i, :], xt[:, i, :], P[:, i, 0:D], ALU.add))
                    link(v.tensor_tensor(xt[:, i, :], xt[:, i, :], tokrows[:, 3 + l, :], ALU.add))
            vlayernorm(dve, "tlnf", ynt, xt, 4)
            dve.wait_ge(s("h_zeroed"), 1)
            for i in range(4):
                dve.wait_ge(s("head"), i + 1)
                link(v.tensor_tensor(h[:, (i // 2) * 3 + i % 2, :], P[:, 4 + i, 0:C], rows[:, 0, :], ALU.add))
            dve.wait_ge(s("txt_in"), 32)

            vlayernorm(dve, "ret", yn, h, NT)
            for i in range(NT):
                dve.wait_ge(s("ret_v"), i + 1)
                r = ROWS[i % 3]
                v.tensor_tensor(vtok[0:r, i, :], P[0:r, i % 4, 0:C], rows[0:r, 1, :], ALU.add).then_inc(s("ret_v_out"), 1)
            for b in range(B):
                for j in range(3):
                    u = b * 3 + j
                    r = ROWS[j]
                    dve.wait_ge(s("ret_scores"), u + 1)
                    v.tensor_tensor(sT[0:r, u, j * 128:N], P[0:r, 4 + u % 4, j * 128:N], decay[0:r, j, j * 128:N], ALU.mult)\
                        .then_inc(s("ret_scores_out"), 1)
            for i in range(NT):
                dve.wait_ge(s("ret_o"), i + 1)
                r = ROWS[i % 3]
                v.tensor_tensor(h[0:r, i, :], h[0:r, i, :], P[0:r, i % 4, 0:C], ALU.add).then_inc(s("ret_o_out"), 1)
            dve.wait_ge(s("ret_o_out"), NT)

            vlayernorm(dve, "ffn0", x2, h, NT)
            dve.wait_ge(s("ln_norm"), LN_BASE["ffn0"] + NT)
            dve.wait_ge(s("turned"), B * TURN["ret"] + B)
            vlayernorm(dve, "ln1", yn, x2, NT)
            v.memset(vaug, 0.0).then_inc(s("vaug_zeroed"), 1)
            dve.wait_ge(s("vaug_zeroed"), 1)
            v.memset(vaug[:, :, :, HD:HD + 1], 1.0).then_inc(s("vaug_ones"), 1)
            for i in range(NT):
                dve.wait_ge(s("att_v"), i + 1)
                r = ROWS[i % 3]
                v.tensor_copy(vaug[0:r, i, :, 0:HD], P[0:r, 4 + i % 4, 0:C].rearrange("p (h d) -> p h d", d=HD))\
                    .then_inc(s("att_v_out"), 1)
            for b in range(B):
                for p in range(PAIRS):
                    u = b * PAIRS + p
                    dve.wait_ge(s("q_hi"), u + 1)
                    for z in range(2):
                        r = slice(32 + 64 * z, 64 + 64 * z)
                        v.scalar_tensor_tensor(qst[r, p, :], P[r, 2 * (u % 2), 0:NP], signs[r, 0:1], qst[r, p, :].bitcast(F32),
                                               ALU.mult, ALU.subtract).then_inc(s("q_lo"), 1)
                    dve.wait_ge(s("k_hi"), u + 1)
                    v.scalar_tensor_tensor(kst[:, p, :], P[:, 2 * (u % 2) + 1, 0:NP], signs[:, 1:2], khi[:, u % 2, :].bitcast(F32),
                                           ALU.mult, ALU.subtract).then_inc(s("k_lo"), 1)
                    for z in range(2):
                        w = (u * 2 + z)
                        dve.wait_ge(s("att_scores"), 3 * (w + 1))
                        for i in range(3):
                            r = ROWS[i]
                            v.tensor_reduce(mx[0:r, i, 2 * p + z:2 * p + z + 1], P[0:r, 4 + (w * 3 + i) % 4, 0:N], AX.X, ALU.max)\
                                .then_inc(s("att_max"), 1)
                for g in range(3):
                    grp = b * 3 + g
                    for i in range(3):
                        r = ROWS[i]
                        dve.wait_ge(s("att_o_turned"), grp * 3 + 3)
                        o = P[0:r, 7, i * 128:(i + 1) * 128].rearrange("p (h e) -> p h e", e=32)
                        link(v.reciprocal(rden[0:r, :], o[:, :, HD]))
                        v.tensor_tensor(yn[0:r, b * 3 + i, g * 64:(g + 1) * 64].rearrange("p (h e) -> p h e", e=HD), o[:, :, 0:HD],
                                        rden[0:r, :].unsqueeze(2).broadcast_to([r, 4, HD]), ALU.mult).then_inc(s("att_o"), 1)
                        dve.wait_ge(s("att_o"), grp * 3 + i + 1)
            for i in range(NT):
                dve.wait_ge(s("att_proj"), i + 1)
                r = ROWS[i % 3]
                v.tensor_tensor(x2[0:r, i, :], x2[0:r, i, :], P[0:r, i % 4, 0:C], ALU.add).then_inc(s("att_proj_out"), 1)
                dve.wait_ge(s("att_proj_out"), i + 1)
                link(v.tensor_tensor(x2[0:r, i, :], x2[0:r, i, :], rows[0:r, 2, :], ALU.add))
            vlayernorm(dve, "ln2", yn, x2, NT)
            moe_vector(dve, 0, x2, link)
            for i in range(NT):
                r = ROWS[i % 3]
                link(v.tensor_tensor(h[0:r, i, :], h[0:r, i, :], x2[0:r, i, :], ALU.add))

            dve.wait_ge(s("turned"), B * TURN["ln2"] + B)
            vlayernorm(dve, "att1", yn, h, NT)
            dve.wait_ge(s("late_in"), 32)
            dve.wait_ge(s("ctx1"), 4)
            link(v.memset(at[:, :, :], 0.0))
            for g in range(4):
                link(v.tensor_tensor(cm[:, g, :, :], P[0:CH, 4 + g, 0:CH].rearrange("p (h e) -> p h e", e=HD1), gmask[:, :, :], ALU.mult))
            link(v.tensor_reduce(cc[:, :, :], cm[:, :, :, :].rearrange("p g h e -> p g e h"), AX.X, ALU.add))
            link(v.tensor_reduce(c1[:, :], cc[:, :, :], AX.X, ALU.max))
            v.tensor_tensor(cc[:, :, :], cc[:, :, :], c1[:, :].unsqueeze(2).broadcast_to([CH, 4, HD1]), ALU.subtract)\
                .then_inc(s("ctx_sub"), 1)
            dve.wait_ge(s("ctx_exp"), 1)
            link(v.tensor_reduce(c1[:, :], cc[:, :, :], AX.X, ALU.add))
            link(v.reciprocal(c1[:, :], c1[:, :]))
            v.tensor_tensor(at[:, :, 0:HD1], cc[:, :, :], c1[:, :].unsqueeze(2).broadcast_to([CH, 4, HD1]), ALU.mult)\
                .then_inc(s("ctx_soft"), 1)
            link(v.memset(atT[:, :, :, :, :], 0.0))
            dve.wait_ge(s("at_turned"), 1)
            for b in range(B):
                v.tensor_copy(atT[:, b, :, :, 0:HD1], P[0:64, b, 0:CH].rearrange("p (h o d) -> p h o d", h=HG, o=1)
                              .broadcast_to([64, HG, 4, HD1])).then_inc(s("at_spread"), 1)
            for u in range(1, 2 * HG * G1, 2):
                dve.wait_ge(s("heads1"), u + 1)
                for quarter in range(4):
                    dst, src = reshuffled(u, quarter)
                    last = v.tensor_copy(dst, src)
                last.then_inc(s("heads1_odd"), 1)
            for i in range(NT):
                dve.wait_ge(s("att1_o"), i + 1)
                r = ROWS[i % 3]
                v.tensor_tensor(h[0:r, i, :], h[0:r, i, :], P[0:r, i % 4, 0:C], ALU.add).then_inc(s("att1_o_out"), 1)
                dve.wait_ge(s("att1_o_out"), i + 1)
                link(v.tensor_tensor(h[0:r, i, :], h[0:r, i, :], rows[0:r, 3, :], ALU.add))

            dve.wait_ge(s("turned"), B * TURN["att1"] + B)
            vlayernorm(dve, "ffn1", yn, h, NT)
            dve.wait_ge(s("sa_zeroed"), 1)
            for b in range(B):
                dve.wait_ge(s("spec_v"), b + 1)
                for back in range(2):
                    src = P[0:1, 6 + b, 0:N]
                    v.tensor_scalar(sa[:, back * B + b, 0:N], src[:, ::-1] if back else src, rows[0:1, 6, 0:1], None, ALU.add)\
                        .then_inc(s("sa_ready"), 1)
            moe_vector(dve, 1, h, link)
            for i in range(NT):
                r = ROWS[i % 3]
                dve.wait_ge(s("spec_o"), i + 1)
                link(v.tensor_tensor(x2[0:r, i, :], P[0:r, i % 4, 0:C], rows[0:r, 4, :], ALU.add))
                link(v.tensor_tensor(x2[0:r, i, :], x2[0:r, i, :], rows[0:r, 5, :], ALU.mult))
                v.tensor_tensor(h[0:r, i, :], h[0:r, i, :], x2[0:r, i, :], ALU.add).then_inc(s("out_ready"), 1)

        @block.tensor
        def _(pe):
            mm = nc.tensor.matmul
            for g in range(4):
                pe.wait_ge(s(f"patches_in{g}"), 32)
                for t in range(4):
                    for c in range(4 * g, 4 * g + 4):
                        last = mm(P[:, t, 0:D], patches[:, c, t * 128:(t + 1) * 128], convw[:, c, :],
                                  start=(c == 0), stop=(c == KP - 1))
                    if g == 3:
                        last.then_inc(s("conv"), 1)
            pe.wait_ge(s("consts_in"), 16 * 12)
            pe.wait_ge(s("tok_weights_in"), 16 * 7)

            def turn4(tag):
                for t in range(4):
                    pe.wait_ge(s("ln_norm"), LN_BASE[tag] + t + 1)
                    last = nc.tensor.transpose(P[:, 0, t * 128:(t + 1) * 128], ynt[:, t, :], ident[:, :])
                last.then_inc(s("tok_turned"), 1)

            for l in range(LAYERS):
                t = f"t{l}"
                turn4(t + "ln1")
                pe.wait_ge(s("tok_y"), 2 * l + 1)
                for q in range(4):
                    mm(P[:, 4 + q, :], wqkv[:, l, INNER + q * 128:INNER + (q + 1) * 128], yT[:, :], start=True, stop=True)\
                        .then_inc(s("tok_k"), 1)
                for q in range(4):
                    mm(P[:, q, :], yT[:, q * 128:(q + 1) * 128], wqkv[:, l, 0:INNER], start=True, stop=True)\
                        .then_inc(s("tok_q"), 1)
                for q in range(4):
                    pe.wait_ge(s("tok_qsub"), 4 * l + q + 1)
                    mm(P[:, q, :], yT[:, q * 128:(q + 1) * 128], wqkv[:, l, 2 * INNER:3 * INNER], start=True, stop=True)\
                        .then_inc(s("tok_v"), 1)
                for q in range(4):
                    pe.wait_ge(s("tok_kexp"), 8 * l + 2 * (q + 1))
                    for i in range(4):
                        last = nc.tensor.transpose(P[:, 4 + q, i * 128:(i + 1) * 128], ke[:, q, i * 128:(i + 1) * 128], ident[:, :])
                    last.then_inc(s("tok_kturned"), 1)
                for q in range(4):
                    pe.wait_ge(s("tok_qsoft"), 4 * l + q + 1)
                    pe.wait_ge(s("tok_vout"), 4 * l + q + 1)
                    for c in range(4):
                        last = nc.tensor.transpose(P[:, q, c * 128:(c + 1) * 128], qs[:, q, c * 128:(c + 1) * 128], ident[:, :])
                    last.then_inc(s("tok_qturned"), 1)
                pe.wait_ge(s("tok_kt"), 4 * l + 4)
                for b in range(B):
                    for q in range(4):
                        for z in range(2):
                            last = mm(P[:, 4 + b, q * 128:(q + 1) * 128], vt[:, 2 * b + z, q * 128:(q + 1) * 128],
                                      kt[:, 2 * b + z, q * 128:(q + 1) * 128], start=(z == 0), stop=(z == 1))
                    last.then_inc(s("tok_ctx"), 1)
                for b in range(B):
                    pe.wait_ge(s("tok_bd"), 4 * l + 2 * (b + 1))
                    for q in range(4):
                        last = mm(P[:, 6 + b, q * 128:(q + 1) * 128], bd[:, b, q, :], wout[:, l, q, :], start=True, stop=True)
                    last.then_inc(s("tok_w2"), 1)
                pe.wait_ge(s("tok_qT"), 4 * l + 4)
                pe.wait_ge(s("tok_w2_out"), 2 * l + 2)
                for i in range(4):
                    for q in range(4):
                        last = mm(P[:, 4 + i, 0:D], qT[:, q, i * 128:(i + 1) * 128], w2[:, i // 2, q, :],
                                  start=(q == 0), stop=(q == 3))
                    last.then_inc(s("tok_att"), 1)
                turn4(t + "ln2")
                pe.wait_ge(s("tok_y"), 2 * l + 2)
                for q in range(4):
                    mm(P[:, 4 + q, :], wff1[:, l, q * 128:(q + 1) * 128], yT[:, :], start=True, stop=True)\
                        .then_inc(s("tok_ff1"), 1)
                pe.wait_ge(s("tok_gelu"), 4 * l + 4)
                for i in range(4):
                    for q in range(4):
                        last = mm(P[:, i, 0:D], hT[:, q, i * 128:(i + 1) * 128], wff2[:, l, q, :], start=(q == 0), stop=(q == 3))
                    last.then_inc(s("tok_ff2"), 1)
            turn4("tlnf")
            pe.wait_ge(s("tok_y"), 2 * LAYERS + 1)
            for i in range(4):
                mm(P[:, 4 + i, 0:C], yT[:, i * 128:(i + 1) * 128], whead[:, :], start=True, stop=True).then_inc(s("head"), 1)

            pe.wait_ge(s("weights_in"), 16 * 4)
            ttranspose(pe, "ret", yn)
            pe.wait_ge(s("turned_out"), 2 * B * TURN["ret"] + 2 * B)
            for i in range(NT):
                r = ROWS[i % 3]
                if i >= 4:
                    pe.wait_ge(s("ret_v_out"), i - 3)
                for k in range(2):
                    last = mm(P[0:r, i % 4, 0:C], tT[:, k, col(i):col(i) + r], wret[:, k, 2 * C:3 * C], start=(k == 0), stop=(k == 1))
                last.then_inc(s("ret_v"), 1)
            for m in range(4):
                for b in range(B):
                    u = m * B + b
                    if u >= 4:
                        pe.wait_ge(s("ret_qk_out"), u - 3)
                    for k in range(2):
                        last = mm(P[0:CH, 4 + u % 4, 0:N], wret[:, k, m * CH:(m + 1) * CH], tT[:, k, b * NP:b * NP + N],
                                  start=(k == 0), stop=(k == 1))
                    last.then_inc(s("ret_qk"), 1)
            pe.wait_ge(s("ret_qk_out"), 8)
            for b in range(B):
                for j in range(3):
                    u = b * 3 + j
                    r = ROWS[j]
                    if u >= 4:
                        pe.wait_ge(s("ret_scores_out"), u - 3)
                    for k in range(2):
                        last = mm(P[0:r, 4 + u % 4, j * 128:N], qkT[:, 2 + k, b * NP + j * 128:b * NP + j * 128 + r],
                                  qkT[:, k, b * NP + j * 128:b * NP + N], start=(k == 0), stop=(k == 1))
                    last.then_inc(s("ret_scores"), 1)
            pe.wait_ge(s("ret_scores_out"), NT)
            pe.wait_ge(s("ret_v_out"), NT)
            for b in range(B):
                for i in range(3):
                    if b * 3 + i >= 4:
                        pe.wait_ge(s("ret_o_out"), b * 3 + i - 3)
                    r = ROWS[i]
                    for j in range(i + 1):
                        last = mm(P[0:r, (b * 3 + i) % 4, 0:C], sT[0:ROWS[j], b * 3 + j, i * 128:i * 128 + r],
                                  vtok[0:ROWS[j], b * 3 + j, :], start=(j == 0), stop=(j == i))
                    last.then_inc(s("ret_o"), 1)

            pe.wait_ge(s("attention_weights_in"), 16 * 5)
            ttranspose(pe, "ln1", yn)
            pe.wait_ge(s("turned_out"), 2 * B * TURN["ln1"] + 2 * B)
            for i in range(NT):
                r = ROWS[i % 3]
                if i >= 4:
                    pe.wait_ge(s("att_v_out"), i - 3)
                for k in range(2):
                    last = mm(P[0:r, 4 + i % 4, 0:C], tT[:, k, col(i):col(i) + r], wva[:, k, :], start=(k == 0), stop=(k == 1))
                last.then_inc(s("att_v"), 1)
            pe.wait_ge(s("att_v_out"), NT)
            pe.wait_ge(s("vaug_ones"), 1)
            pe.wait_ge(s("selr_set"), 1)
            for b in range(B):
                if b == 1:
                    pe.wait_ge(s("att_exp"), 3 * HEADS)
                    pe.wait_ge(s("att_o"), 9)
                for p in range(PAIRS):
                    u = b * PAIRS + p
                    if u >= 2:
                        pe.wait_ge(s("k_lo"), u - 1)
                    for m in range(2):
                        for k in range(2):
                            last = mm(P[:, 2 * (u % 2) + m, 0:NP], wqa[:, k, m, p * 128:(p + 1) * 128], tT[:, k, b * NP:(b + 1) * NP],
                                      start=(k == 0), stop=(k == 1))
                    last.then_inc(s("qk_stack"), 1)
                    pe.wait_ge(s("q_lo"), 2 * (u + 1))
                    pe.wait_ge(s("k_lo"), u + 1)
                    for z in range(2):
                        for i in range(3):
                            w = (u * 2 + z) * 3 + i
                            if w >= 4:
                                pe.wait_ge(s("att_max"), w - 3)
                            rows_ = slice(64 * z, 64 * z + 64)
                            mm(P[0:ROWS[i], 4 + w % 4, 0:NP], qst[rows_, p, i * 128:i * 128 + ROWS[i]], kst[rows_, p, :],
                               start=True, stop=True).then_inc(s("att_scores"), 1)
                pe.wait_ge(s("att_max"), (b + 1) * HEADS * 3)
                for i in range(3):
                    r = ROWS[i]
                    last = nc.tensor.transpose(P[0:HEADS, 0, i * 128:i * 128 + r], mx[0:r, i, :], ident[0:r, 0:r])
                last.then_inc(s("att_maxT"), 1)
                pe.wait_ge(s("att_max_out"), b + 1)
                pe.wait_ge(s("att_max_pad"), 1)

                def pv(u):
                    hh, j = (u // 3) % HEADS, u % 3
                    r = ROWS[j]
                    if hh % 4 == 0 and j == 0 and u >= 12:
                        pe.wait_ge(s("att_ao"), u // 12)
                    pe.wait_ge(s("att_exp"), u + 1)
                    mm(P[32 * (hh % 4):32 * (hh % 4) + 32, 6, 0:N], vaug[0:r, (u // (3 * HEADS)) * 3 + j, hh, :], pt[0:r, u % 6, :],
                       start=(j == 0), stop=(j == 2), tile_position=None).then_inc(s("att_pv"), 1)
                    if hh % 4 == 3 and j == 2:
                        grp = u // 12
                        pe.wait_ge(s("att_ao"), grp + 1)
                        if grp >= 1:
                            pe.wait_ge(s("att_o"), 3 * grp)
                        for i in range(3):
                            nc.tensor.transpose(P[0:ROWS[i], 7, i * 128:(i + 1) * 128], ao[:, grp % 3, i * 128:i * 128 + ROWS[i]],
                                                ident[:, :]).then_inc(s("att_o_turned"), 1)

                base = b * HEADS * 3
                for hh in range(HEADS):
                    for j in range(3):
                        u = base + hh * 3 + j
                        r = ROWS[j]
                        if u >= 2:
                            pe.wait_ge(s("att_exp"), u - 1)
                        rows_ = slice(64 * (hh % 2), 64 * (hh % 2) + 64)
                        mm(P[0:r, 4 + u % 2, 0:NP], kst[rows_, hh // 2, j * 128:j * 128 + r], qst[rows_, hh // 2, :],
                           start=True, stop=False)
                        mm(P[0:r, 4 + u % 2, 0:NP], selr[:, hh, 0:r], mxT[:, :], start=False, stop=True).then_inc(s("att_scoresT"), 1)
                        if u > base:
                            pv(u - 1)
                pv(base + HEADS * 3 - 1)
            pe.wait_ge(s("att_o"), 3 * B * 3)
            ttranspose(pe, "proj", yn)
            pe.wait_ge(s("turned_out"), 2 * B * TURN["proj"] + 2 * B)
            for i in range(NT):
                r = ROWS[i % 3]
                if i >= 4:
                    pe.wait_ge(s("att_proj_out"), i - 3)
                for k in range(2):
                    last = mm(P[0:r, i % 4, 0:C], tT[:, k, col(i):col(i) + r], wpa[:, k, :], start=(k == 0), stop=(k == 1))
                last.then_inc(s("att_proj"), 1)
            moe_tensor(pe, 0)

            ttranspose(pe, "att1", yn)
            pe.wait_ge(s("turned_out"), 2 * B * TURN["att1"] + 2 * B)
            for b in range(B):
                for k in range(2):
                    last = mm(P[0:64, 4 + b, 0:N], w1q[:, k, :], tT[:, k, b * NP:b * NP + N], start=(k == 0), stop=(k == 1))
                last.then_inc(s("q1"), 1)
            for i in range(NT):
                r = ROWS[i % 3]
                if i >= 4:
                    pe.wait_ge(s("kv1_out"), i - 3)
                for k in range(2):
                    last = mm(P[0:r, i % 4, 0:2 * C], tT[:, k, col(i):col(i) + r], w1kv[:, k, :], start=(k == 0), stop=(k == 1))
                last.then_inc(s("kv1"), 1)
            pe.wait_ge(s("kv1_out"), NT)
            for b in range(B):
                for g in range(G1):
                    for j in range(3):
                        r = ROWS[j]
                        last = mm(P[0:CH, 4 + b * 2 + g, 0:CH], kv[0:r, b * 3 + j, g * CH:(g + 1) * CH],
                                  kv[0:r, b * 3 + j, C + g * CH:C + (g + 1) * CH], start=(j == 0), stop=(j == 2))
                    last.then_inc(s("ctx1"), 1)
            pe.wait_ge(s("ctx_soft"), 1)
            for b in range(B):
                last = nc.tensor.transpose(P[0:64, b, 0:CH], at[:, 2 * b:2 * b + 2, :].rearrange("p g e -> p (g e)"), ident[0:CH, 0:CH])
            last.then_inc(s("at_turned"), 1)
            pe.wait_ge(s("at_spread"), B)
            for u in range(2 * HG * G1):
                if u >= 4:
                    pe.wait_ge(s("heads1_odd" if u % 2 else "heads1_even"), (u - 4) // 2 + 1)
                b, hh, g = u // 8, u % 8 // G1, u % G1
                mm(P[:, 4 + u % 4, 0:N], atT[32 * g:32 * g + 32, b, hh, :, :].rearrange("p q d -> p (q d)"),
                   q1T[32 * g:32 * g + 32, b * NP:b * NP + N], start=True, stop=True).then_inc(s("heads1"), 1)
            pe.wait_ge(s("heads1_even"), 8)
            pe.wait_ge(s("heads1_odd"), 8)
            for i in range(NT):
                r = ROWS[i % 3]
                if i >= 4:
                    pe.wait_ge(s("att1_o_out"), i - 3)
                first = (i % 3) * 256
                for half in range(2):
                    last = mm(P[0:r, i % 4, 0:C], mixed[:, i // 3, first + half:first + half + 2 * r - 1:2], w1p[:, half, :],
                              start=(half == 0), stop=(half == 1))
                last.then_inc(s("att1_o"), 1)
            moe_tensor(pe, 1)
            for i in range(NT):
                r = ROWS[i % 3]
                pe.wait_ge(s("feats_ready"), i // 3 + 1)
                if i >= 4:
                    pe.wait_ge(s("out_ready"), i - 3)
                for z in range(2):
                    last = mm(P[0:r, i % 4, 0:C], gf[:, i // 3, z, (i % 3) * 128:(i % 3) * 128 + r], outw_rows[:, z, :],
                              start=(z == 0), stop=(z == 1))
                last.then_inc(s("spec_o"), 1)


def kernel(**inputs):
    import numpy as np
    import concourse.bacc as bacc
    from concourse.bass_utils import run_bass_kernel_spmd as run

    x = {k: np.asarray(v) for k, v in inputs.items()}
    f = np.float32
    T = np.transpose
    pad = lambda w, n: np.concatenate([w, np.zeros((w.shape[0], n - w.shape[1]), w.dtype)], axis=1)
    halves = lambda v_: v_.reshape(2, CH).T
    bc = lambda v_: np.broadcast_to(v_, (C,))
    heads = x["L0_ffn_qkv_w"][:2 * C].reshape(2, HEADS, 1, HD, C)
    qk = np.broadcast_to(heads, (2, HEADS, 4, HD, C)).reshape(2, HEADS * 4 * HD, C)
    wq1 = x["L1_attn_Wq"]
    wp1 = x["L1_attn_Wproj"].reshape(2, 4, HD1, C)
    spread = T(np.concatenate([wp1, np.zeros((2, 4, 32 - HD1, C), f)], axis=2), (1, 2, 0, 3)).reshape(128, 2, C)
    diff = np.arange(N)[None, :] - np.arange(384)[:, None]
    decay = np.where(diff >= 0, np.float64(f(0.99)) ** np.maximum(diff, 0), 0.0) / np.sqrt(float(C))
    p = np.arange(128)
    copy = (p // HD) % 4
    ln = "L0_tok_ln"
    arrays = {
        "patches": T(x["x"].reshape(B, 32, 16, 8, 16, 8), (1, 3, 5, 0, 2, 4)).reshape(2048, B * TOK),
        "conv_w": x["L0_tok_conv_w"].reshape(D, 2048).T,
        "qkv_w": x["L0_tok_qkv_w"], "out_w": x["L0_tok_out_w"], "ff1_w": x["L0_tok_ff1_w"], "ff2_w": x["L0_tok_ff2_w"],
        "head_w": x["L0_tok_head_w"],
        "ret_w": x["L0_attn_W_qkv"].T, "v_w": x["L0_ffn_qkv_w"][2 * C:].T, "proj_w": x["L0_ffn_proj_w"].T,
        "gate_w": pad(np.concatenate([x["L0_ffn_gate_w"].T, x["L1_ffn_gate_w"], x["L1_ffn_v_w"][:, None]], axis=1), 18),
        "q1_w": np.concatenate([pad(wq1[:, :HD1], 32), pad(wq1[:, HD1:], 32)], axis=1),
        "kv1_w": x["L1_attn_Wkv"], "proj1_w": spread, "qk_w": T(qk, (0, 2, 1)),
        "w1": np.stack([T(x["L0_ffn_w1"], (0, 2, 1)), x["L1_ffn_w1"]]),
        "w2": np.stack([T(x["L0_ffn_w2"], (0, 2, 1)), x["L1_ffn_w2"]]),
        "b1": T(np.stack([x["L0_ffn_b1"], x["L1_ffn_b1"]]).reshape(2, EXPERTS, HC, 128), (3, 0, 1, 2)),
        "b2": np.stack([x["L0_ffn_b2"], x["L1_ffn_b2"]]),
        "txt": x["txt"],
        "rows": np.stack([x["L0_tok_head_b"], x["L0_attn_b_qkv"][2 * C:], x["L0_ffn_proj_b"], x["L1_attn_bproj"],
                          x["L1_ffn_out_b"], x["L1_ffn_bk_scale"], bc(x["L1_ffn_v_b"])]),
        "tok_rows": np.concatenate([x["L0_tok_conv_b"][None], x["L0_tok_out_b"], x["L0_tok_ff2_b"]]),
        "tok_cols": np.stack([x[ln + n][l] for l in range(LAYERS) for n in ("1_g", "1_b", "2_g", "2_b")]
                             + [x[ln + "f_g"], x[ln + "f_b"]], axis=1),
        "ff1_b": T(x["L0_tok_ff1_b"].reshape(LAYERS * 4, 128), (1, 0)),
        "ch_cols": np.concatenate([x["L0_attn_b_qkv"][:2 * C].reshape(4, CH).T]
                                  + [halves(x["L0_ffn_" + n]) for n in ("ln1_g", "ln1_b", "ln2_g", "ln2_b")], axis=1),
        "gate_rows": np.stack([x["L0_ffn_gate_b"], x["L1_ffn_gate_b"], np.arange(EXPERTS, dtype=f)]),
        "outw_rows": x["L1_ffn_out_w"][None],
        "ident": np.eye(128, dtype=f),
        "decay": T(decay.reshape(3, 128, N), (1, 0, 2)).astype(f),
        "signs": np.stack([np.where(copy % 2 == 0, -1.0, 1.0) * HD ** -0.5, copy % 2], axis=1).astype(f),
        "sel": np.broadcast_to(-np.eye(HEADS, dtype=f)[:, :, None], (HEADS, HEADS, 128)),
        "gmask": np.broadcast_to((np.arange(CH)[:, None] // HD1 == np.arange(HG)[None, :])[:, :, None],
                                 (CH, HG, HD1)).astype(f),
    }
    arrays = {"in_" + k: np.ascontiguousarray(v) for k, v in arrays.items()}
    nc = bacc.Bacc("TRN2", target_bir_lowering=False, num_devices=1)
    aps = {k[3:]: nc.dram_tensor(k, v.shape, mybir.dt.from_np(v.dtype), kind="ExternalInput").ap() for k, v in arrays.items()}
    out = nc.dram_tensor("out_0", (B, N, C), F32, kind="ExternalOutput").ap()
    fusion_kernel(nc, aps, out)
    return run(nc, [arrays], core_ids=[0]).results[0]["out_0"]
```

```python
import concourse.bass as bass
from concourse import mybir
from contextlib import ExitStack

F32 = mybir.dt.float32
F32R = mybir.dt.float32r
U32 = mybir.dt.uint32
ALU = mybir.AluOpType
ACT = mybir.ActivationFunctionType
AX = mybir.AxisListType

B = 2
TOK = 256
TXT = 77
N = TOK + TXT
NP = N + 1
COLS = B * NP
KP = 2048 // 128
D = 128
INNER = 512
DH = 64
LAYERS = 2
C = 192
CH = 96
ROWS = (128, 128, TXT)
NT = 3 * B
HEADS = 12
HD = 16
PAIRS = HEADS // 2
EXPERTS = 8
HID = 768
HC = HID // 128
EPS = 1e-5
G1 = 2
HG = 4
HD1 = C // (G1 * HG)
CL = 19
CN = 18
SL = CL * CN
CHAINS = 2 * B

LN_TAGS = [("t0ln1", 4), ("t0ln2", 4), ("t1ln1", 4), ("t1ln2", 4), ("tlnf", 4), ("ret", NT), ("ffn0", NT), ("ln1", NT),
           ("ln2", NT), ("att1", NT), ("ffn1", NT)]
LN_ORDER = {tag: n for n, (tag, _) in enumerate(LN_TAGS)}
LN_BASE = {tag: sum(nt for _, nt in LN_TAGS[:n]) for n, (tag, _) in enumerate(LN_TAGS)}
TURN = {tag: n for n, tag in enumerate(("ret", "ln1", "proj", "ln2", "att1", "ffn1"))}


def fusion_kernel(nc, a, out):
    ctx = ExitStack()
    with ctx:
        def sb(name, shape, dt=F32):
            return ctx.enter_context(nc.sbuf_tensor(name, shape, dt))

        def sem(name):
            return ctx.enter_context(nc.semaphore(name))

        P = ctx.enter_context(nc.psum_tensor("P", [128, 8, 512], F32))

        ident = sb("ident", [128, 128])
        neghalf = sb("neghalf", [128, 8])
        stats = sb("stats", [128, NT, 6])
        mv = sb("mv", [128, NT, 2])
        varr = sb("varr", [128, NT])
        rstd = sb("rstd", [128, NT])
        rows = sb("rows", [128, 7, C])
        tokrows = sb("tokrows", [128, 5, D])
        gate_rows = sb("gate_rows", [128, 3, EXPERTS])
        tokcols = sb("tokcols", [128, 2 * (2 * LAYERS + 1)])
        ff1b = sb("ff1b", [128, LAYERS * 4])
        chcols = sb("chcols", [CH, 4 + 4 + 4])
        signs = sb("signs", [128, 2])
        b1s = sb("b1s", [128, 2, EXPERTS, HC])
        b1now = [sb(f"b1now{i}", [128, HC]) for i in range(2)]
        b2s = sb("b2s", [EXPERTS, 2, C])
        gmask = sb("gmask", [CH, HG, HD1])
        outw_rows = sb("outw_rows", [B, 2, B, C])

        region = {"B": sb("regB", [128, 9216]), "C": sb("regC", [128, 10432])}
        used = {"B": 0, "C": 0}
        regB = region["B"]

        def carve(where, parts, *shape):
            size = 1
            for n in shape:
                size *= n
            flat = region[where][0:parts, used[where]:used[where] + size]
            used[where] += size
            names = "abcdef"[:len(shape)]
            return flat.rearrange(f"p ({' '.join(names)}) -> p {' '.join(names)}", **dict(zip(names[1:], shape[1:]))) \
                if len(shape) > 1 else flat

        regA = sb("regA", [128, 2 * HC * COLS + 2 * 2 * PAIRS * 128])
        patches = regA[:, 0:KP * 512].rearrange("p (c n) -> p c n", c=KP)
        convw = regA[:, KP * 512:KP * 512 + KP * D].rearrange("p (c n) -> p c n", c=KP)
        hidT = [regA[:, i * HC * COLS:(i + 1) * HC * COLS].rearrange("p (c n) -> p c n", c=HC) for i in range(2)]
        wqkv = carve("C", 128, LAYERS, 3 * INNER)
        wout = carve("C", 128, LAYERS, 4, D)
        wff1 = carve("C", 128, LAYERS, 512)
        wff2 = carve("C", 128, LAYERS, 4, D)
        whead = carve("C", 128, C)
        xt = carve("C", 128, 4, D)
        yn = sb("yn", [128, NT, C])
        ynt = yn[:, 0:4, 0:D]
        yT = carve("C", 128, 512)
        qs = regB[:, 0:2048].rearrange("p (t c) -> p t c", t=4)
        vt = regB[:, 2048:4096].rearrange("p (t c) -> p t c", t=4)
        kt = regB[:, 4096:6144].rearrange("p (t c) -> p t c", t=4)
        ke = regB[:, 6144:8192].rearrange("p (c n) -> p c n", c=4)
        qT = carve("C", 128, 4, 512)
        hT = qs
        bd = carve("C", 128, B, 4, 128)
        w2 = regB[:, 8192:9216].rearrange("p (b q d) -> p b q d", b=B, q=4)
        segmax = sb("segmax", [128, 4, 8])
        segsum = sb("segsum", [128, 4, 8])
        kmax = sb("kmax", [128, 4, B])
        ksum = sb("ksum", [128, 4, B])

        x2 = region["C"][:, 10432 - NT * C:].rearrange("p (t c) -> p t c", t=NT)
        used["C"] = 0
        wva = carve("C", CH, 2, C)
        wpa = carve("C", CH, 2, C)
        w1q = carve("C", CH, 2, 64)
        w1kv = carve("C", CH, 2, 2 * C)
        w1p = carve("C", 128, 2, C)
        mixed = regB[:, NT * 2 * C + COLS:NT * 2 * C + COLS + B * 2 * N].rearrange("p (b m) -> p b m", b=B)
        cm = carve("C", CH, 4, HG, HD1)
        cc = carve("C", CH, 4, HD1)
        at = carve("C", CH, 4, 32)
        atT = carve("C", 64, B, HG, 4, 32)
        h = sb("h", [128, NT, C])
        tT = sb("tT", [CH, 2, COLS])
        lg = sb("lg", [128, NT, EXPERTS])
        m8 = sb("m8", [128, NT, 8])
        i8 = sb("i8", [128, NT, 8], U32)
        idf = sb("idf", [128, NT, 2])
        s01 = sb("s01", [128, NT, 2])
        gtmp = sb("gtmp", [128, NT])
        cwA = sb("cwA", [128, NT, EXPERTS])
        cw = sb("cw", [128, NT, EXPERTS])
        cwT = sb("cwT", [EXPERTS, COLS])
        w1s = [sb(f"w1s{i}", [CH, 2, HID]) for i in range(2)]
        w2s = [sb(f"w2s{i}", [128, HC, C]) for i in range(2)]
        qkT = regB[0:CH, 0:4 * COLS].rearrange("p (m n) -> p m n", m=4)
        sT = regB[:, 4 * COLS:4 * COLS + B * 3 * N].rearrange("p (t n) -> p t n", t=B * 3)
        decay = regB[:, 5822:5822 + 3 * N].rearrange("p (j n) -> p j n", j=3)
        vtok = regB[:, 4670:4670 + NT * C].rearrange("p (t c) -> p t c", t=NT)
        qst = sb("qst", [128, PAIRS, NP], F32R)
        khi = sb("khi", [128, 2, NP], F32R)
        kst = sb("kst", [128, PAIRS, NP], F32R)
        mx = sb("mx", [128, 3, HEADS])
        mxT = sb("mxT", [HEADS, NP], F32R)
        selw = regB[0:HEADS, 0:HEADS * 128].rearrange("p (h n) -> p h n", h=HEADS)
        selr = sb("selr", [HEADS, HEADS, 128], F32R)
        vaug = regB[:, 0:NT * HEADS * 32].rearrange("p (t h e) -> p t h e", t=NT, h=HEADS)
        pt = regB[:, 2304:2304 + 2 * 3 * N].rearrange("p (u n) -> p u n", u=6)
        ao = regB[:, 4310:4310 + 3 * N].rearrange("p (g n) -> p g n", g=3)
        rden = sb("rden", [128, 4])
        wqa = regA[0:CH, 2 * HC * COLS:].rearrange("p (k m n) -> p k m n", k=2, m=2)
        wret = sb("wret", [CH, 2, 3 * C])
        wgate = sb("wgate", [CH, 2, 2 * EXPERTS + 4 * CHAINS])
        q1T = regB[0:64, NT * 2 * C:NT * 2 * C + COLS]
        kv = regB[:, 0:NT * 2 * C].rearrange("p (t c) -> p t c", t=NT)
        c1 = sb("c1", [CH, 4])
        used["C"] = 0
        sa = carve("C", CHAINS, SL)
        sE = carve("C", CHAINS, CL + 2, 2, 2, CN)
        sprod = carve("C", CHAINS, 2, 2, CN)
        smap = carve("C", CHAINS, CN, 2, 2, 2, 2)
        sy = carve("C", CHAINS, CN, 2, 2)
        ssum = carve("C", CHAINS, 24)
        snorm = carve("C", CHAINS, 6, CN)
        su = carve("C", CHAINS, 2, CN)
        sp_ = carve("C", CHAINS, CL + 1, 2, CN)
        st = [carve("C", CHAINS, CL + 1, 2, CN) for _ in range(2)]
        sd = carve("C", CHAINS, 2, SL)
        se = carve("C", B, 2, SL)
        gf = carve("C", B, 2, N)
        gt = carve("C", B, 3, N)
        powers = carve("C", CHAINS, 2, SL)

        S = {}

        def s(name):
            if name not in S:
                S[name] = sem(name)
            return S[name]

        block = ctx.enter_context(nc.Block())

        def col(i):
            return (i // 3) * NP + (i % 3) * 128

        def vlayernorm_stats(dve, tag, src, nt):
            for t in range(nt):
                nc.vector.bn_stats(stats[:, t, :], src[:, t, :]).then_inc(s("ln_stats"), 1)
            dve.wait_ge(s("ln_stats"), LN_BASE[tag] + nt)
            for t in range(nt):
                nc.vector.bn_aggr(mv[:, t, :], stats[:, t, :]).then_inc(s("ln_mean"), 1)

        def vlayernorm_apply(dve, tag, dst, src, nt):
            dve.wait_ge(s("ln_mean"), LN_BASE[tag] + nt)
            dve.wait_ge(s("ln_rstd"), LN_ORDER[tag] + 1)
            for t in range(nt):
                nc.vector.tensor_scalar(dst[:, t, :], src[:, t, :], mv[:, t, 0:1], rstd[:, t:t + 1],
                                        ALU.subtract, ALU.mult).then_inc(s("ln_norm"), 1)

        def vlayernorm(dve, tag, dst, src, nt):
            vlayernorm_stats(dve, tag, src, nt)
            vlayernorm_apply(dve, tag, dst, src, nt)

        def prstd(pool, tag, nt):
            pool.wait_ge(s("ln_mean"), LN_BASE[tag] + nt)
            nc.gpsimd.tensor_scalar(varr[:, 0:nt], mv[:, 0:nt, 1], EPS, 0.0, ALU.add, ALU.add)\
                .then_inc(s("ln_var"), 1)
            pool.wait_ge(s("ln_var"), LN_ORDER[tag] + 1)
            nc.gpsimd.tensor_tensor(rstd[:, 0:nt], varr[:, 0:nt], neghalf[:, 0:nt], ALU.pow)\
                .then_inc(s("ln_rstd"), 1)

        def reshuffled(u, quarter):
            b, first = u // 8, (u % 8) * N
            skip = (quarter - first) % 4
            n = (N - skip + 3) // 4
            m = (first + skip - quarter) // 4
            part = slice(32 * quarter, 32 * quarter + 32)
            return mixed[part, b, m:m + n], P[part, 4 + u % 4, skip:skip + 4 * (n - 1) + 1:4]

        def ttranspose(pe, tag, src):
            for i in range(NT):
                if tag != "proj":
                    pe.wait_ge(s("ln_norm"), LN_BASE[tag] + i + 1)
                r = ROWS[i % 3]
                for k in range(2):
                    last = nc.tensor.transpose(P[0:CH, (i // 3) * 2 + k, (i % 3) * 128:(i % 3) * 128 + r],
                                               src[0:r, i, k * CH:(k + 1) * CH], ident[0:r, 0:r])
                if i % 3 == 2:
                    last.then_inc(s("turned"), 1)

        def aevacuate(act, tag, cols):
            for b in range(B):
                act.wait_ge(s("turned"), B * TURN[tag] + b + 1)
                for k in range(2):
                    dst, src = tT[:, k, b * NP:b * NP + N], P[0:CH, b * 2 + k, 0:N]
                    if cols is None:
                        last = nc.scalar.activation(dst, src, ACT.Copy)
                    else:
                        last = nc.scalar.activation(dst, src, ACT.Identity, bias=chcols[:, cols + 2 + k:cols + 3 + k],
                                                    scale=chcols[:, cols + k:cols + k + 1])
                    last.then_inc(s("turned_out"), 1)

        def spectral(pool):
            count = [0]
            g = nc.gpsimd

            def step(ins):
                count[0] += 1
                ins.then_inc(s("spec_step"), 1)

            def link(ins):
                step(ins)
                pool.wait_ge(s("spec_step"), count[0])

            def wide(ap, shape):
                return ap.broadcast_to(shape)

            for ap, value in ((powers[:, 0, :], -1.0), (powers[:, 1, :], -0.5), (sE[:, 0:2], 0.0), (sy[:, 0], 0.0)):
                link(g.memset(ap, value))
            link(g.memset(sE[:, 0, 0, 0, :], 1.0))
            link(g.memset(sE[:, 1, 1, 0, :], 1.0))
            link(g.memset(sy[:, 0, 1, 0:1], 1.0))
            pool.wait_ge(s("sa_ready"), 1)
            link(g.tensor_scalar(sa[:, 0:N], sa[:, 0:N], 3.0, -3.0, ALU.min, ALU.max))
            link(g.tensor_scalar(sa[:, 0:N], sa[:, 0:N], -2.0, 0.0, ALU.add, ALU.add))
            av = sa.rearrange("p (n l) -> p l n", l=CL)
            shape = [CHAINS, 2, 2, CN]
            for i in range(CL):
                new, p1, p2 = sE[:, i + 2], sE[:, i + 1], sE[:, i]
                link(g.tensor_tensor(sprod, p1, wide(av[:, i, :].unsqueeze(1).unsqueeze(1), shape), ALU.mult))
                link(g.tensor_tensor(sprod, sprod, p2, ALU.subtract))
                step(g.tensor_tensor(new[:, :, 0], sprod[:, :, 0], p1[:, :, 1], ALU.add))
                link(g.tensor_tensor(new[:, :, 1], sprod[:, :, 1], p1[:, :, 0], ALU.subtract))
            last = sE[:, CL + 1, 1]
            link(g.tensor_tensor(snorm[:, 0:2], last, last, ALU.mult))
            link(g.tensor_tensor(snorm[:, 2], snorm[:, 0], snorm[:, 1], ALU.add))
            link(g.tensor_tensor(snorm[:, 3], snorm[:, 2], powers[:, 1, 0:CN], ALU.pow))
            link(g.tensor_scalar(snorm[:, 4], snorm[:, 3], -1.0, 0.0, ALU.mult, ALU.add))
            for zo in range(2):
                for zi in range(2):
                    scale = snorm[:, 4 if (zo, zi) == (0, 1) else 3]
                    dst = smap[:, :, :, zo, :, zi].rearrange("p n r w -> p r w n")
                    step(g.tensor_tensor(dst, sE[:, CL:CL + 2, :, zo ^ zi, :],
                                         wide(scale.unsqueeze(1).unsqueeze(1), shape), ALU.mult))
            pool.wait_ge(s("spec_step"), count[0])
            for n in range(CN - 1):
                prod = ssum[:, 0:16].rearrange("p (i k) -> p i k", k=4)
                link(g.tensor_tensor(prod, smap[:, n].rearrange("p r o w i -> p (r o) (w i)"),
                                     wide(sy[:, n].rearrange("p w i -> p (w i)").unsqueeze(1), [CHAINS, 4, 4]), ALU.mult))
                half = ssum[:, 16:24].rearrange("p (i k) -> p i k", k=2)
                link(g.tensor_tensor(half, prod[:, :, 0:2], prod[:, :, 2:4], ALU.add))
                link(g.tensor_tensor(sy[:, n + 1].rearrange("p w i -> p (w i)"), half[:, :, 0], half[:, :, 1], ALU.add))
            qr, qi, pr, pi = (sy[:, :, w, z] for w in range(2) for z in range(2))

            def divide(dst_r, dst_i, nr, ni, dr, di, t, power):
                step(g.tensor_tensor(t[0], dr, dr, ALU.mult))
                link(g.tensor_tensor(t[1], di, di, ALU.mult))
                link(g.tensor_tensor(t[0], t[0], t[1], ALU.add))
                step(g.tensor_tensor(t[4], t[0], power, ALU.pow))
                step(g.tensor_tensor(t[2], nr, dr, ALU.mult))
                link(g.tensor_tensor(t[3], ni, di, ALU.mult))
                link(g.tensor_tensor(t[2], t[2], t[3], ALU.add))
                step(g.tensor_tensor(dst_r, t[2], t[4], ALU.mult))
                step(g.tensor_tensor(t[0], ni, dr, ALU.mult))
                link(g.tensor_tensor(t[1], nr, di, ALU.mult))
                link(g.tensor_tensor(t[0], t[0], t[1], ALU.subtract))
                link(g.tensor_tensor(dst_i, t[0], t[4], ALU.mult))

            divide(su[:, 0], su[:, 1], qr, qi, pr, pi, [snorm[:, k] for k in range(5)], powers[:, 0, 0:CN])
            rows_ = slice(1, CL + 2)
            lo, hi = sE[:, rows_, 0], sE[:, rows_, 1]
            big = [CHAINS, CL + 1, 2, CN]
            step(g.tensor_tensor(st[0], lo, wide(su[:, 0].unsqueeze(1).unsqueeze(1), big), ALU.mult))
            link(g.tensor_tensor(st[1], lo, wide(su[:, 1].unsqueeze(1).unsqueeze(1), big), ALU.mult))
            link(g.tensor_tensor(st[0], st[0], hi, ALU.add))
            step(g.tensor_tensor(sp_[:, :, 0], st[0][:, :, 0], st[1][:, :, 1], ALU.subtract))
            link(g.tensor_tensor(sp_[:, :, 1], st[0][:, :, 1], st[1][:, :, 0], ALU.add))
            tmp = [st[0][:, 0:CL, 0], st[0][:, 0:CL, 1], st[1][:, 0:CL, 0], st[1][:, 0:CL, 1],
                   sE[:, 0:CL, 0, 0]]
            order = lambda ap: ap.rearrange("p (n l) -> p l n", l=CL)
            divide(order(sd[:, 0]), order(sd[:, 1]), sp_[:, 1:CL + 1, 0], sp_[:, 1:CL + 1, 1], sp_[:, 0:CL, 0], sp_[:, 0:CL, 1],
                   tmp, powers[:, 0].rearrange("p (l n) -> p l n", n=CN))
            pool.dma_start(se, sd[B:CHAINS]).then_inc(s("backward_moved"), 16)
            pool.wait_ge(s("backward_moved"), 16)
            link(g.tensor_tensor(gf, sd[0:B, :, 0:N], se[:, :, 0:N][:, :, ::-1], ALU.add))
            step(g.tensor_tensor(gf[:, 0], gf[:, 0], sa[0:B, 0:N], ALU.subtract))
            link(g.tensor_scalar(gf[:, 1], gf[:, 1], 1.0, 0.0, ALU.add, ALU.add))
            link(g.tensor_tensor(gt[:, 0:2], gf, gf, ALU.mult))
            link(g.tensor_tensor(gt[:, 2], gt[:, 0], gt[:, 1], ALU.add))
            link(g.tensor_tensor(gt[:, 0], gt[:, 2], powers[0:B, 0, 0:N], ALU.pow))
            link(g.tensor_scalar(gt[:, 1], gt[:, 0], -1.0, 0.0, ALU.mult, ALU.add))
            link(g.tensor_tensor(gf, gf, gt[:, 0:2], ALU.mult))
            g.tensor_scalar(gf, gf, 10.0, -10.0, ALU.min, ALU.max).then_inc(s("feats_ready"), 1)

        def moe_act(act, moe):
            m = f"m{moe}"
            aevacuate(act, "ln2" if moe == 0 else "ffn1", 8 if moe == 0 else None)
            act.wait_ge(s(m + "_gate_in"), 1)
            if moe == 0:
                nc.scalar.activation(gtmp[:, :], gtmp[:, :], ACT.Exp).then_inc(s(m + "_gate_exp"), 1)
            else:
                nc.scalar.activation(lg[:, :, :], lg[:, :, :], ACT.Exp).then_inc(s(m + "_gate_exp"), 1)
            act.wait_ge(s(m + "_cwT"), 1)
            nc.scalar.activation(cwT[:, :].rearrange("e (b n) -> e b n", b=B)[:, :, 0:N], P[0:EXPERTS, 0:2, 0:N],
                                 ACT.Copy).then_inc(s(m + "_cwT_out"), 1)
            with act.Fori(0, EXPERTS // 2) as i:
                for par in range(2):
                    nc.scalar.activation(b1now[par][:, :], b1s[:, moe, bass.ds(i * 2 + par, 1), :], ACT.Copy)\
                        .then_inc(s(m + "_b1"), 1)
                    act.wait_ge(s(m + "_b1"), i * 2 + par + 1)
                    for c in range(HC):
                        for b in range(B):
                            u = c * B + b
                            act.wait_ge(s(m + "_h1"), (i * 2 + par) * (HC * B) + u + 1)
                            nc.scalar.activation(hidT[par][:, c, b * NP:b * NP + N], P[:, u % 4, 0:N],
                                                 ACT.Gelu if moe == 0 else ACT.Gelu_apprx_tanh,
                                                 bias=b1now[par][:, c:c + 1]).then_inc(s(m + "_hid"), 1)

        def moe_vector(dve, moe, acc, link):
            v = nc.vector
            m = f"m{moe}"
            dve.wait_ge(s(m + "_logits"), 1)
            dve.wait_ge(s("pads_zeroed"), 3)
            for i in range(NT):
                r = ROWS[i % 3]
                link(v.tensor_tensor(lg[0:r, i, :], P[0:r, 4, i * 8:i * 8 + 8], gate_rows[0:r, moe, :], ALU.add))
            if moe == 1:
                link(v.tensor_reduce(gtmp[:, :], lg[:, :, :], AX.X, ALU.max))
                v.tensor_tensor(lg[:, :, :], lg[:, :, :], gtmp[:, :].unsqueeze(2).broadcast_to([128, NT, 8]), ALU.subtract)\
                    .then_inc(s(m + "_gate_in"), 1)
                dve.wait_ge(s(m + "_gate_exp"), 1)
                link(v.tensor_reduce(gtmp[:, :], lg[:, :, :], AX.X, ALU.add))
                link(v.reciprocal(gtmp[:, :], gtmp[:, :]))
                link(v.tensor_tensor(lg[:, :, :], lg[:, :, :], gtmp[:, :].unsqueeze(2).broadcast_to([128, NT, 8]), ALU.mult))
            for i in range(NT):
                link(v.max(m8[:, i, :], lg[:, i, :]))
                link(v.max_index(i8[:, i, :], m8[:, i, :], lg[:, i, :]))
            link(v.tensor_copy(idf[:, :, :], i8[:, :, 0:2]))
            if moe == 0:
                v.tensor_tensor(gtmp[:, :], m8[:, :, 1], m8[:, :, 0], ALU.subtract).then_inc(s(m + "_gate_in"), 1)
                dve.wait_ge(s(m + "_gate_exp"), 1)
                link(v.tensor_scalar(s01[:, :, 0], gtmp[:, :], 1.0, None, ALU.add))
                link(v.reciprocal(s01[:, :, 0], s01[:, :, 0]))
                link(v.tensor_tensor(s01[:, :, 1], s01[:, :, 0], gtmp[:, :], ALU.mult))
            else:
                link(v.tensor_tensor(gtmp[:, :], m8[:, :, 0], m8[:, :, 1], ALU.add))
                link(v.reciprocal(gtmp[:, :], gtmp[:, :]))
                link(v.tensor_tensor(s01[:, :, :], m8[:, :, 0:2], gtmp[:, :].unsqueeze(2).broadcast_to([128, NT, 2]), ALU.mult))
            for i in range(NT):
                link(v.tensor_scalar(cwA[:, i, :], gate_rows[:, 2, :], idf[:, i, 0:1], s01[:, i, 0:1], ALU.is_equal, ALU.mult))
                link(v.tensor_scalar(cw[:, i, :], gate_rows[:, 2, :], idf[:, i, 1:2], s01[:, i, 1:2], ALU.is_equal, ALU.mult))
                v.tensor_tensor(cw[:, i, :], cw[:, i, :], cwA[:, i, :], ALU.add).then_inc(s(m + "_cw"), 1)
            for i in range(NT):
                r = ROWS[i % 3]
                dve.wait_ge(s(m + "_b2"), i + 1)
                v.tensor_tensor(acc[0:r, i, :], acc[0:r, i, :], P[0:r, 4 + i % 4, 0:C], ALU.add).then_inc(s(m + "_acc"), 1)
            with dve.Fori(0, EXPERTS) as e:
                for i in range(NT):
                    r = ROWS[i % 3]
                    dve.wait_ge(s(m + "_y"), e * NT + i + 1)
                    dve.wait_ge(s(m + "_acc"), e * NT + i + 1)
                    v.scalar_tensor_tensor(acc[0:r, i, :], P[0:r, 4 + i % 4, 0:C], cw[0:r, i, bass.ds(e, 1)], acc[0:r, i, :],
                                           ALU.mult, ALU.add).then_inc(s(m + "_acc"), 1)
            dve.wait_ge(s(m + "_acc"), NT * (EXPERTS + 1))

        def moe_tensor(pe, moe):
            mm = nc.tensor.matmul
            m = f"m{moe}"
            tag = "ln2" if moe == 0 else "ffn1"
            ttranspose(pe, tag, yn)
            pe.wait_ge(s("turned_out"), 2 * B * TURN[tag] + 2 * B)
            for i in range(NT):
                r = ROWS[i % 3]
                for k in range(2):
                    last = mm(P[0:r, 4, i * 8:i * 8 + 8], tT[:, k, col(i):col(i) + r], wgate[:, k, 8 * moe:8 * moe + 8],
                              start=(k == 0), stop=(k == 1))
            last.then_inc(s(m + "_logits"), 1)
            if moe == 1:
                for chain in range(CHAINS):
                    for k in range(2):
                        seq = tT[:, k, chain % B * NP:chain % B * NP + N]
                        last = mm(P[0:CHAINS, 6, 0:N], wgate[:, k, 16 + 4 * chain:20 + 4 * chain], seq[:, ::-1] if chain >= B else seq,
                                  start=(chain == 0 and k == 0), stop=(chain == CHAINS - 1 and k == 1))
                last.then_inc(s("spec_v"), 1)
            for i in range(NT):
                r = ROWS[i % 3]
                pe.wait_ge(s(m + "_cw"), i + 1)
                last = nc.tensor.transpose(P[0:EXPERTS, i // 3, (i % 3) * 128:(i % 3) * 128 + r], cw[0:r, i, :], ident[0:r, 0:r])
            last.then_inc(s(m + "_cwT"), 1)
            pe.wait_ge(s(m + "_cwT_out"), 1)
            if moe == 1:
                pe.wait_ge(s("sa_ready"), 1)
            for i in range(NT):
                r = ROWS[i % 3]
                if i >= 4:
                    pe.wait_ge(s(m + "_acc"), i - 3)
                mm(P[0:r, 4 + i % 4, 0:C], cwT[:, col(i):col(i) + r], b2s[:, moe, :], start=True, stop=True)\
                    .then_inc(s(m + "_b2"), 1)
            with pe.Fori(0, EXPERTS // 2) as e2:
                for par in range(2):
                    e = e2 * 2 + par
                    pe.wait_ge(s(f"w1_in{par}"), (e2 + 1 + moe * (EXPERTS // 2)) * 16)
                    pe.wait_ge(s(f"w2_in{par}"), (e2 + 1 + moe * (EXPERTS // 2)) * 16)
                    for c in range(HC):
                        for b in range(B):
                            u = c * B + b
                            if u >= 4:
                                pe.wait_ge(s(m + "_hid"), e * (HC * B) + u - 3)
                            for k in range(2):
                                last = mm(P[:, u % 4, 0:N], w1s[par][:, k, c * 128:(c + 1) * 128],
                                          tT[:, k, b * NP:b * NP + N], start=(k == 0), stop=(k == 1))
                            last.then_inc(s(m + "_h1"), 1)
                    pe.wait_ge(s(m + "_hid"), (e + 1) * (HC * B))
                    for i in range(NT):
                        r = ROWS[i % 3]
                        pe.wait_ge(s(m + "_acc"), e * NT + i + (5 if i < 2 else 1 if i < 4 else 3))
                        for c in range(HC):
                            last = mm(P[0:r, 4 + i % 4, 0:C], hidT[par][:, c, col(i):col(i) + r], w2s[par][:, c, :],
                                      start=(c == 0), stop=(c == HC - 1))
                        last.then_inc(s(m + "_y"), 1)

        @block.sync
        def _(sp):
            pat = a["patches"].rearrange("(c p) n -> p c n", p=128)
            cwv = a["conv_w"].rearrange("(c p) n -> p c n", p=128)
            for g in range(4):
                sp.dma_start(convw[:, 4 * g:4 * g + 4, :], cwv[:, 4 * g:4 * g + 4, :]).then_inc(s(f"patches_in{g}"), 16)
                sp.dma_start(patches[:, 4 * g:4 * g + 4, :], pat[:, 4 * g:4 * g + 4, :]).then_inc(s(f"patches_in{g}"), 16)
            for n, (dst, name, pat_) in enumerate([
                    (wqkv[:, :, :], "qkv_w", "l p n -> p l n"), (wout[:, :, :, :], "out_w", "l (q p) n -> p l q n"),
                    (wff1[:, :, :], "ff1_w", "l p n -> p l n"), (wff2[:, :, :, :], "ff2_w", "l (q p) n -> p l q n")]):
                kw = {"p": 128} if "q" in pat_ else {}
                src = a[name].rearrange(pat_, **kw)
                if n in (1, 3):
                    for l in range(LAYERS):
                        sp.dma_start(dst[:, l, :, :], src[:, l, :, :]).then_inc(s("tok_weights_in"), 16)
                else:
                    sp.dma_start(dst, src).then_inc(s("tok_weights_in"), 16)
            sp.dma_start(whead[:, :], a["head_w"]).then_inc(s("tok_weights_in"), 16)
            for dst, name in ((wret, "ret_w"), (wgate, "gate_w")):
                sp.dma_start(dst[:, :, :], a[name].rearrange("(k p) n -> p k n", p=CH)).then_inc(s("weights_in"), 16)
            sp.wait_ge(s("conv"), 4)
            for m in range(2):
                sp.dma_start(wqa[:, :, m, :], a["qk_w"][m].rearrange("(k p) n -> p k n", p=CH)).then_inc(s("weights_in"), 16)
            sp.wait_ge(s("head"), 4)
            sp.dma_start(decay, a["decay"]).then_inc(s("decay_in"), 16)
            for dst, name in ((wva, "v_w"), (wpa, "proj_w"), (w1q, "q1_w"), (w1kv, "kv1_w")):
                sp.dma_start(dst[:, :, :], a[name].rearrange("(k p) n -> p k n", p=CH)).then_inc(s("attention_weights_in"), 16)
            sp.dma_start(w1p[:, :, :], a["proj1_w"]).then_inc(s("attention_weights_in"), 16)
            for moe in range(2):
                for e in range(EXPERTS):
                    par, turn = e % 2, moe * EXPERTS + e
                    if turn >= 2:
                        sp.wait_ge(s(f"m{(turn - 2) // EXPERTS}_y"), ((turn - 2) % EXPERTS + 1) * NT)
                    sp.dma_start(w1s[par][:, :, :], a["w1"][moe, e].rearrange("(k p) n -> p k n", p=CH))\
                        .then_inc(s(f"w1_in{par}"), 16)
                    sp.dma_start(w2s[par][:, :, :], a["w2"][moe, e].rearrange("(k p) n -> p k n", p=128))\
                        .then_inc(s(f"w2_in{par}"), 16)
            ov = out
            for b in range(B):
                for j in range(3):
                    sp.wait_ge(s("out_ready"), b * 3 + j + 1)
                    sp.dma_start(ov[b, j * 128:j * 128 + ROWS[j], :], h[0:ROWS[j], b * 3 + j, :]).then_inc(s("out_stored"), 16)
            sp.wait_ge(s("out_stored"), 16 * NT)

        @block.gpsimd
        def _(pool):
            nc.gpsimd.memset(neghalf[:, :], -0.5).then_inc(s("neghalf_set"), 1)
            nc.gpsimd.memset(h[:, :, :], 0.0).then_inc(s("h_zeroed"), 1)
            nc.gpsimd.memset(bd[:, :, :, :], 0.0).then_inc(s("bd_zeroed"), 1)
            nc.gpsimd.memset(tT[:, :, :], 0.0).then_inc(s("pads_zeroed"), 1)
            nc.gpsimd.memset(mx[:, :, :], 0.0).then_inc(s("pads_zeroed"), 1)
            nc.gpsimd.memset(yn[:, :, :], 0.0).then_inc(s("yn_zeroed"), 1)
            nc.gpsimd.memset(lg[:, :, :], 0.0).then_inc(s("pads_zeroed"), 1)
            pool.wait_ge(s("neghalf_set"), 1)
            pool.wait_ge(s("consts_in"), 16 * 11)
            nc.gpsimd.tensor_copy(selr[:, :, :], selw[:, :, :]).then_inc(s("selr_set"), 1)
            for l in range(LAYERS):
                prstd(pool, f"t{l}ln1", 4)
                prstd(pool, f"t{l}ln2", 4)
            prstd(pool, "tlnf", 4)
            for tag in ("ret", "ffn0", "ln1", "ln2", "att1", "ffn1"):
                prstd(pool, tag, NT)
            nc.gpsimd.memset(sa[:, N:SL], 0.0).then_inc(s("sa_zeroed"), 1)
            spectral(pool)

        @block.scalar
        def _(act):
            one = lambda x: x.rearrange("(o n) -> o n", o=1)
            for dst, src in ((ident[:, :], a["ident"]), (tokrows[:, :, :], a["tok_rows"].partition_broadcast(128)),
                             (tokcols[:, :], a["tok_cols"]), (ff1b[:, :], a["ff1_b"]), (chcols[:, :], a["ch_cols"]),
                             (signs[:, :], a["signs"]), (selw[:, :, :], a["sel"]), (rows[:, :, :], a["rows"].partition_broadcast(128)),
                             (gate_rows[:, :, :], a["gate_rows"].partition_broadcast(128)),
                             (b1s[:, :, :, :], a["b1"]), (b2s[:, :, :], a["b2"].rearrange("m e c -> e m c"))):
                act.dma_start(dst, src).then_inc(s("consts_in"), 16)
            act.dma_start(gmask[:, :, :], a["gmask"]).then_inc(s("late_in"), 16)
            act.dma_start(outw_rows[:, :, :, :], a["outw_rows"]).then_inc(s("late_in"), 16)
            act.wait_ge(s("h_zeroed"), 1)
            for b in range(B):
                act.dma_start(h[0:TXT, b * 3 + 2, :], a["txt"][b]).then_inc(s("txt_in"), 16)
            act.wait_ge(s("consts_in"), 16 * 11)
            for l in range(LAYERS):
                t = f"t{l}"
                act.wait_ge(s("tok_turned"), 2 * l + 1)
                nc.scalar.activation(yT[:, :], P[:, 0, :], ACT.Identity, bias=tokcols[:, 4 * l + 1:4 * l + 2],
                                     scale=tokcols[:, 4 * l:4 * l + 1]).then_inc(s("tok_y"), 1)
                for q in range(4):
                    act.wait_ge(s("tok_kmax"), 4 * l + q + 1)
                    for b in range(B):
                        nc.scalar.activation(ke[:, q, b * TOK:(b + 1) * TOK], P[:, 4 + q, b * TOK:(b + 1) * TOK], ACT.Exp,
                                             bias=kmax[:, q, b:b + 1], accum_out=ksum[:, q, b:b + 1]).then_inc(s("tok_kexp"), 1)
                for q in range(4):
                    act.wait_ge(s("tok_qsub"), 4 * l + q + 1)
                    nc.scalar.activation(qs[:, q, :], qs[:, q, :], ACT.Exp).then_inc(s("tok_qexp"), 1)
                for q in range(4):
                    act.wait_ge(s("tok_v"), 4 * l + q + 1)
                    nc.scalar.activation(vt[:, q, :], P[:, q, :], ACT.Copy).then_inc(s("tok_vout"), 1)
                for q in range(4):
                    act.wait_ge(s("tok_kturned"), 4 * l + q + 1)
                    nc.scalar.activation(kt[:, :, q * 128:(q + 1) * 128], P[:, 4 + q, :].rearrange("p (t c) -> p t c", t=4),
                                         ACT.Copy).then_inc(s("tok_kt"), 1)
                for q in range(4):
                    act.wait_ge(s("tok_qturned"), 4 * l + q + 1)
                    nc.scalar.activation(qT[:, :, q * 128:(q + 1) * 128], P[:, q, :].rearrange("p (c n) -> p c n", c=4),
                                         ACT.Copy).then_inc(s("tok_qT"), 1)
                act.wait_ge(s("tok_turned"), 2 * l + 2)
                nc.scalar.activation(yT[:, :], P[:, 0, :], ACT.Identity, bias=tokcols[:, 4 * l + 3:4 * l + 4],
                                     scale=tokcols[:, 4 * l + 2:4 * l + 3]).then_inc(s("tok_y"), 1)
                for q in range(4):
                    act.wait_ge(s("tok_ff1"), 4 * l + q + 1)
                    nc.scalar.activation(hT[:, q, :], P[:, 4 + q, :], ACT.Gelu, bias=ff1b[:, 4 * l + q:4 * l + q + 1])\
                        .then_inc(s("tok_gelu"), 1)
            act.wait_ge(s("tok_turned"), 2 * LAYERS + 1)
            nc.scalar.activation(yT[:, :], P[:, 0, :], ACT.Identity, bias=tokcols[:, 9:10],
                                 scale=tokcols[:, 8:9]).then_inc(s("tok_y"), 1)
            act.wait_ge(s("pads_zeroed"), 3)
            aevacuate(act, "ret", None)
            for m in range(4):
                for b in range(B):
                    u = m * B + b
                    act.wait_ge(s("ret_qk"), u + 1)
                    nc.scalar.activation(qkT[:, m, b * NP:b * NP + N], P[0:CH, 4 + u % 4, 0:N], ACT.Identity,
                                         bias=chcols[:, m:m + 1]).then_inc(s("ret_qk_out"), 1)
            aevacuate(act, "ln1", 4)
            for b in range(B):
                for p in range(PAIRS):
                    u = b * PAIRS + p
                    act.wait_ge(s("qk_stack"), u + 1)
                    if u >= 2:
                        act.wait_ge(s("k_lo"), u - 1)
                    if b == 1 and p == 0:
                        act.wait_ge(s("att_scoresT"), 3 * HEADS)
                    nc.scalar.activation(qst[:, p, :], P[:, 2 * (u % 2), 0:NP], ACT.Identity,
                                         scale=signs[:, 0:1]).then_inc(s("q_hi"), 1)
                    nc.scalar.activation(khi[:, u % 2, :], P[:, 2 * (u % 2) + 1, 0:NP], ACT.Copy).then_inc(s("k_hi"), 1)
                act.wait_ge(s("att_maxT"), b + 1)
                nc.scalar.activation(mxT[:, 0:N], P[0:HEADS, 0, 0:N], ACT.Copy).then_inc(s("att_max_out"), 1)
                if b == 0:
                    nc.scalar.activation(mxT[:, N:NP], ident[0:HEADS, 127:128], ACT.Copy).then_inc(s("att_max_pad"), 1)
                for hh in range(HEADS):
                    for j in range(3):
                        u = (b * HEADS + hh) * 3 + j
                        r = ROWS[j]
                        act.wait_ge(s("att_scoresT"), u + 1)
                        if u >= 6:
                            act.wait_ge(s("att_pv"), u - 5)
                        nc.scalar.activation(pt[0:r, u % 6, :], P[0:r, 4 + u % 2, 0:N], ACT.Exp).then_inc(s("att_exp"), 1)
                    if hh % 4 == 3:
                        grp = b * 3 + hh // 4
                        act.wait_ge(s("att_pv"), (b * HEADS + hh + 1) * 3)
                        if grp >= 3:
                            act.wait_ge(s("att_o_turned"), 3 * (grp - 2))
                        nc.scalar.activation(ao[:, grp % 3, :], P[:, 6, 0:N], ACT.Copy).then_inc(s("att_ao"), 1)
            aevacuate(act, "proj", None)
            moe_act(act, 0)
            aevacuate(act, "att1", None)
            for b in range(B):
                act.wait_ge(s("q1"), b + 1)
                nc.scalar.activation(q1T[:, b * NP:b * NP + N], P[0:64, 4 + b, 0:N], ACT.Copy).then_inc(s("q1_out"), 1)
            for i in range(NT):
                act.wait_ge(s("kv1"), i + 1)
                r = ROWS[i % 3]
                nc.scalar.activation(kv[0:r, i, :], P[0:r, i % 4, 0:2 * C], ACT.Copy).then_inc(s("kv1_out"), 1)
            act.wait_ge(s("ctx_sub"), 1)
            nc.scalar.activation(cc[:, :, :], cc[:, :, :], ACT.Exp, scale=float(HD1) ** -0.5).then_inc(s("ctx_exp"), 1)
            for u in range(0, 2 * HG * G1, 2):
                act.wait_ge(s("heads1"), u + 1)
                for quarter in range(4):
                    dst, src = reshuffled(u, quarter)
                    last = nc.scalar.activation(dst, src, ACT.Copy)
                last.then_inc(s("heads1_even"), 1)
            moe_act(act, 1)

        @block.vector
        def _(dve):
            count = [0]

            def link(ins):
                count[0] += 1
                ins.then_inc(s("dve_step"), 1)
                dve.wait_ge(s("dve_step"), count[0])

            v = nc.vector
            dve.wait_ge(s("consts_in"), 16 * 11)
            dve.wait_ge(s("yn_zeroed"), 1)
            for t in range(4):
                dve.wait_ge(s("conv"), t + 1)
                link(v.tensor_tensor(xt[:, t, :], P[:, t, 0:D], tokrows[:, 0, :], ALU.add))

            for l in range(LAYERS):
                t = f"t{l}"
                vlayernorm(dve, t + "ln1", ynt, xt, 4)
                for q in range(4):
                    dve.wait_ge(s("tok_k"), 4 * l + q + 1)
                    link(v.tensor_reduce(kmax[:, q, :], P[:, 4 + q, :].rearrange("p (b n) -> p b n", b=B), AX.X, ALU.max))
                    v.tensor_scalar(kmax[:, q, :], kmax[:, q, :], -1.0, None, ALU.mult).then_inc(s("tok_kmax"), 1)
                for q in range(4):
                    dve.wait_ge(s("tok_q"), 4 * l + q + 1)
                    dve.wait_ge(s("selr_set"), 1)
                    seg = P[:, q, :].rearrange("p (h d) -> p h d", d=DH)
                    link(v.tensor_reduce(segmax[:, q, :], seg, AX.X, ALU.max))
                    v.tensor_tensor(qs[:, q, :].rearrange("p (h d) -> p h d", d=DH), seg,
                                    segmax[:, q, :].unsqueeze(2).broadcast_to([128, 8, DH]), ALU.subtract)\
                        .then_inc(s("tok_qsub"), 1)
                for q in range(4):
                    dve.wait_ge(s("tok_qexp"), 4 * l + q + 1)
                    seg = qs[:, q, :].rearrange("p (h d) -> p h d", d=DH)
                    link(v.tensor_reduce(segsum[:, q, :], seg, AX.X, ALU.add))
                    link(v.reciprocal(segsum[:, q, :], segsum[:, q, :]))
                    link(v.tensor_scalar(segsum[:, q, :], segsum[:, q, :], DH ** -0.5, None, ALU.mult))
                    v.tensor_tensor(seg, seg, segsum[:, q, :].unsqueeze(2).broadcast_to([128, 8, DH]), ALU.mult)\
                        .then_inc(s("tok_qsoft"), 1)
                dve.wait_ge(s("tok_kexp"), 8 * l + 8)
                v.reciprocal(ksum[:, :, :], ksum[:, :, :]).then_inc(s("tok_kinv"), 1)
                for b in range(B):
                    dve.wait_ge(s("tok_ctx"), 2 * l + b + 1)
                    if l == 0 and b == 0:
                        dve.wait_ge(s("bd_zeroed"), 1)
                    for z in range(2):
                        r = slice(64 * z, 64 * z + 64)
                        v.tensor_copy(bd[r, b, :, 64 * z:64 * z + 64],
                                      P[r, 4 + b, :].rearrange("p (q d) -> p q d", q=4)[:, :, 64 * z:64 * z + 64])\
                            .then_inc(s("tok_bd"), 1)
                dve.wait_ge(s("tok_kinv"), 1 * l + 1)
                for b in range(B):
                    dve.wait_ge(s("tok_w2"), 2 * l + b + 1)
                    v.tensor_tensor(w2[:, b, :, :], P[:, 6 + b, :].rearrange("p (q d) -> p q d", q=4),
                                    ksum[:, :, b].unsqueeze(2).broadcast_to([128, 4, D]), ALU.mult).then_inc(s("tok_w2_out"), 1)
                for i in range(4):
                    dve.wait_ge(s("tok_att"), 4 * l + i + 1)
                    link(v.tensor_tensor(xt[:, i, :], xt[:, i, :], P[:, 4 + i, 0:D], ALU.add))
                    link(v.tensor_tensor(xt[:, i, :], xt[:, i, :], tokrows[:, 1 + l, :], ALU.add))
                vlayernorm(dve, t + "ln2", ynt, xt, 4)
                for i in range(4):
                    dve.wait_ge(s("tok_ff2"), 4 * l + i + 1)
                    link(v.tensor_tensor(xt[:, i, :], xt[:, i, :], P[:, i, 0:D], ALU.add))
                    link(v.tensor_tensor(xt[:, i, :], xt[:, i, :], tokrows[:, 3 + l, :], ALU.add))
            vlayernorm(dve, "tlnf", ynt, xt, 4)
            dve.wait_ge(s("h_zeroed"), 1)
            for i in range(4):
                dve.wait_ge(s("head"), i + 1)
                link(v.tensor_tensor(h[:, (i // 2) * 3 + i % 2, :], P[:, 4 + i, 0:C], rows[:, 0, :], ALU.add))
            dve.wait_ge(s("txt_in"), 32)

            vlayernorm(dve, "ret", yn, h, NT)
            for i in range(NT):
                dve.wait_ge(s("ret_v"), i + 1)
                r = ROWS[i % 3]
                v.tensor_tensor(vtok[0:r, i, :], P[0:r, i % 4, 0:C], rows[0:r, 1, :], ALU.add).then_inc(s("ret_v_out"), 1)
            dve.wait_ge(s("decay_in"), 16)
            for b in range(B):
                for j in range(3):
                    u = b * 3 + j
                    r = ROWS[j]
                    dve.wait_ge(s("ret_scores"), u + 1)
                    v.tensor_tensor(sT[0:r, u, j * 128:N], P[0:r, 4 + u % 4, j * 128:N], decay[0:r, j, j * 128:N], ALU.mult)\
                        .then_inc(s("ret_scores_out"), 1)
            for i in range(NT):
                dve.wait_ge(s("ret_o"), i + 1)
                r = ROWS[i % 3]
                v.tensor_tensor(h[0:r, i, :], h[0:r, i, :], P[0:r, i % 4, 0:C], ALU.add).then_inc(s("ret_o_out"), 1)
            dve.wait_ge(s("ret_o_out"), NT)

            vlayernorm(dve, "ffn0", x2, h, NT)
            dve.wait_ge(s("ln_norm"), LN_BASE["ffn0"] + NT)
            dve.wait_ge(s("turned"), B * TURN["ret"] + B)
            vlayernorm(dve, "ln1", yn, x2, NT)
            v.memset(vaug, 0.0).then_inc(s("vaug_zeroed"), 1)
            dve.wait_ge(s("vaug_zeroed"), 1)
            v.memset(vaug[:, :, :, HD:HD + 1], 1.0).then_inc(s("vaug_ones"), 1)
            for i in range(NT):
                dve.wait_ge(s("att_v"), i + 1)
                r = ROWS[i % 3]
                v.tensor_copy(vaug[0:r, i, :, 0:HD], P[0:r, 4 + i % 4, 0:C].rearrange("p (h d) -> p h d", d=HD))\
                    .then_inc(s("att_v_out"), 1)
            for b in range(B):
                for p in range(PAIRS):
                    u = b * PAIRS + p
                    dve.wait_ge(s("q_hi"), u + 1)
                    for z in range(2):
                        r = slice(32 + 64 * z, 64 + 64 * z)
                        v.scalar_tensor_tensor(qst[r, p, :], P[r, 2 * (u % 2), 0:NP], signs[r, 0:1], qst[r, p, :].bitcast(F32),
                                               ALU.mult, ALU.subtract).then_inc(s("q_lo"), 1)
                    dve.wait_ge(s("k_hi"), u + 1)
                    v.scalar_tensor_tensor(kst[:, p, :], P[:, 2 * (u % 2) + 1, 0:NP], signs[:, 1:2], khi[:, u % 2, :].bitcast(F32),
                                           ALU.mult, ALU.subtract).then_inc(s("k_lo"), 1)
                    for z in range(2):
                        w = (u * 2 + z)
                        dve.wait_ge(s("att_scores"), 3 * (w + 1))
                        for i in range(3):
                            r = ROWS[i]
                            v.tensor_reduce(mx[0:r, i, 2 * p + z:2 * p + z + 1], P[0:r, 4 + (w * 3 + i) % 4, 0:N], AX.X, ALU.max)\
                                .then_inc(s("att_max"), 1)
                for g in range(3):
                    grp = b * 3 + g
                    for i in range(3):
                        r = ROWS[i]
                        dve.wait_ge(s("att_o_turned"), grp * 3 + 3)
                        o = P[0:r, 7, i * 128:(i + 1) * 128].rearrange("p (h e) -> p h e", e=32)
                        link(v.reciprocal(rden[0:r, :], o[:, :, HD]))
                        v.tensor_tensor(yn[0:r, b * 3 + i, g * 64:(g + 1) * 64].rearrange("p (h e) -> p h e", e=HD), o[:, :, 0:HD],
                                        rden[0:r, :].unsqueeze(2).broadcast_to([r, 4, HD]), ALU.mult).then_inc(s("att_o"), 1)
                        dve.wait_ge(s("att_o"), grp * 3 + i + 1)
            for i in range(NT):
                dve.wait_ge(s("att_proj"), i + 1)
                r = ROWS[i % 3]
                v.tensor_tensor(x2[0:r, i, :], x2[0:r, i, :], P[0:r, i % 4, 0:C], ALU.add).then_inc(s("att_proj_out"), 1)
                dve.wait_ge(s("att_proj_out"), i + 1)
                link(v.tensor_tensor(x2[0:r, i, :], x2[0:r, i, :], rows[0:r, 2, :], ALU.add))
            vlayernorm(dve, "ln2", yn, x2, NT)
            moe_vector(dve, 0, x2, link)
            for i in range(NT):
                r = ROWS[i % 3]
                link(v.tensor_tensor(h[0:r, i, :], h[0:r, i, :], x2[0:r, i, :], ALU.add))

            dve.wait_ge(s("turned"), B * TURN["ln2"] + B)
            vlayernorm(dve, "att1", yn, h, NT)
            dve.wait_ge(s("late_in"), 32)
            dve.wait_ge(s("ctx1"), 4)
            link(v.memset(at[:, :, :], 0.0))
            for g in range(4):
                link(v.tensor_tensor(cm[:, g, :, :], P[0:CH, 4 + g, 0:CH].rearrange("p (h e) -> p h e", e=HD1), gmask[:, :, :], ALU.mult))
            link(v.tensor_reduce(cc[:, :, :], cm[:, :, :, :].rearrange("p g h e -> p g e h"), AX.X, ALU.add))
            link(v.tensor_reduce(c1[:, :], cc[:, :, :], AX.X, ALU.max))
            v.tensor_tensor(cc[:, :, :], cc[:, :, :], c1[:, :].unsqueeze(2).broadcast_to([CH, 4, HD1]), ALU.subtract)\
                .then_inc(s("ctx_sub"), 1)
            dve.wait_ge(s("ctx_exp"), 1)
            link(v.tensor_reduce(c1[:, :], cc[:, :, :], AX.X, ALU.add))
            link(v.reciprocal(c1[:, :], c1[:, :]))
            v.tensor_tensor(at[:, :, 0:HD1], cc[:, :, :], c1[:, :].unsqueeze(2).broadcast_to([CH, 4, HD1]), ALU.mult)\
                .then_inc(s("ctx_soft"), 1)
            link(v.memset(atT[:, :, :, :, :], 0.0))
            dve.wait_ge(s("at_turned"), 1)
            for b in range(B):
                v.tensor_copy(atT[:, b, :, :, 0:HD1], P[0:64, b, 0:CH].rearrange("p (h o d) -> p h o d", h=HG, o=1)
                              .broadcast_to([64, HG, 4, HD1])).then_inc(s("at_spread"), 1)
            for u in range(1, 2 * HG * G1, 2):
                dve.wait_ge(s("heads1"), u + 1)
                for quarter in range(4):
                    dst, src = reshuffled(u, quarter)
                    last = v.tensor_copy(dst, src)
                last.then_inc(s("heads1_odd"), 1)
            for i in range(NT):
                dve.wait_ge(s("att1_o"), i + 1)
                r = ROWS[i % 3]
                v.tensor_tensor(h[0:r, i, :], h[0:r, i, :], P[0:r, i % 4, 0:C], ALU.add).then_inc(s("att1_o_out"), 1)
                dve.wait_ge(s("att1_o_out"), i + 1)
                link(v.tensor_tensor(h[0:r, i, :], h[0:r, i, :], rows[0:r, 3, :], ALU.add))

            dve.wait_ge(s("turned"), B * TURN["att1"] + B)
            vlayernorm(dve, "ffn1", yn, h, NT)
            dve.wait_ge(s("sa_zeroed"), 1)
            dve.wait_ge(s("spec_v"), 1)
            v.tensor_scalar(sa[:, 0:N], P[0:CHAINS, 6, 0:N], rows[0:CHAINS, 6, 0:1], None, ALU.add).then_inc(s("sa_ready"), 1)
            moe_vector(dve, 1, h, link)
            for i in range(NT):
                r = ROWS[i % 3]
                dve.wait_ge(s("spec_o"), i + 1)
                link(v.tensor_tensor(x2[0:r, i, :], P[0:r, i % 4, 0:C], rows[0:r, 4, :], ALU.add))
                link(v.tensor_tensor(x2[0:r, i, :], x2[0:r, i, :], rows[0:r, 5, :], ALU.mult))
                v.tensor_tensor(h[0:r, i, :], h[0:r, i, :], x2[0:r, i, :], ALU.add).then_inc(s("out_ready"), 1)

        @block.tensor
        def _(pe):
            mm = nc.tensor.matmul
            for g in range(4):
                pe.wait_ge(s(f"patches_in{g}"), 32)
                for t in range(4):
                    for c in range(4 * g, 4 * g + 4):
                        last = mm(P[:, t, 0:D], patches[:, c, t * 128:(t + 1) * 128], convw[:, c, :],
                                  start=(c == 0), stop=(c == KP - 1))
                    if g == 3:
                        last.then_inc(s("conv"), 1)
            pe.wait_ge(s("consts_in"), 16 * 11)
            pe.wait_ge(s("tok_weights_in"), 16 * 7)

            def turn4(tag):
                for t in range(4):
                    pe.wait_ge(s("ln_norm"), LN_BASE[tag] + t + 1)
                    last = nc.tensor.transpose(P[:, 0, t * 128:(t + 1) * 128], ynt[:, t, :], ident[:, :])
                last.then_inc(s("tok_turned"), 1)

            for l in range(LAYERS):
                t = f"t{l}"
                turn4(t + "ln1")
                pe.wait_ge(s("tok_y"), 2 * l + 1)
                for q in range(4):
                    mm(P[:, 4 + q, :], wqkv[:, l, INNER + q * 128:INNER + (q + 1) * 128], yT[:, :], start=True, stop=True)\
                        .then_inc(s("tok_k"), 1)
                for q in range(4):
                    mm(P[:, q, :], yT[:, q * 128:(q + 1) * 128], wqkv[:, l, 0:INNER], start=True, stop=True)\
                        .then_inc(s("tok_q"), 1)
                for q in range(4):
                    pe.wait_ge(s("tok_qsub"), 4 * l + q + 1)
                    mm(P[:, q, :], yT[:, q * 128:(q + 1) * 128], wqkv[:, l, 2 * INNER:3 * INNER], start=True, stop=True)\
                        .then_inc(s("tok_v"), 1)
                for q in range(4):
                    pe.wait_ge(s("tok_kexp"), 8 * l + 2 * (q + 1))
                    for i in range(4):
                        last = nc.tensor.transpose(P[:, 4 + q, i * 128:(i + 1) * 128], ke[:, q, i * 128:(i + 1) * 128], ident[:, :])
                    last.then_inc(s("tok_kturned"), 1)
                for q in range(4):
                    pe.wait_ge(s("tok_qsoft"), 4 * l + q + 1)
                    pe.wait_ge(s("tok_vout"), 4 * l + q + 1)
                    for c in range(4):
                        last = nc.tensor.transpose(P[:, q, c * 128:(c + 1) * 128], qs[:, q, c * 128:(c + 1) * 128], ident[:, :])
                    last.then_inc(s("tok_qturned"), 1)
                pe.wait_ge(s("tok_kt"), 4 * l + 4)
                for b in range(B):
                    for q in range(4):
                        for z in range(2):
                            last = mm(P[:, 4 + b, q * 128:(q + 1) * 128], vt[:, 2 * b + z, q * 128:(q + 1) * 128],
                                      kt[:, 2 * b + z, q * 128:(q + 1) * 128], start=(z == 0), stop=(z == 1))
                    last.then_inc(s("tok_ctx"), 1)
                for b in range(B):
                    pe.wait_ge(s("tok_bd"), 4 * l + 2 * (b + 1))
                    for q in range(4):
                        last = mm(P[:, 6 + b, q * 128:(q + 1) * 128], bd[:, b, q, :], wout[:, l, q, :], start=True, stop=True)
                    last.then_inc(s("tok_w2"), 1)
                pe.wait_ge(s("tok_qT"), 4 * l + 4)
                pe.wait_ge(s("tok_w2_out"), 2 * l + 2)
                for i in range(4):
                    for q in range(4):
                        last = mm(P[:, 4 + i, 0:D], qT[:, q, i * 128:(i + 1) * 128], w2[:, i // 2, q, :],
                                  start=(q == 0), stop=(q == 3))
                    last.then_inc(s("tok_att"), 1)
                turn4(t + "ln2")
                pe.wait_ge(s("tok_y"), 2 * l + 2)
                for q in range(4):
                    mm(P[:, 4 + q, :], wff1[:, l, q * 128:(q + 1) * 128], yT[:, :], start=True, stop=True)\
                        .then_inc(s("tok_ff1"), 1)
                pe.wait_ge(s("tok_gelu"), 4 * l + 4)
                for i in range(4):
                    for q in range(4):
                        last = mm(P[:, i, 0:D], hT[:, q, i * 128:(i + 1) * 128], wff2[:, l, q, :], start=(q == 0), stop=(q == 3))
                    last.then_inc(s("tok_ff2"), 1)
            turn4("tlnf")
            pe.wait_ge(s("tok_y"), 2 * LAYERS + 1)
            for i in range(4):
                mm(P[:, 4 + i, 0:C], yT[:, i * 128:(i + 1) * 128], whead[:, :], start=True, stop=True).then_inc(s("head"), 1)

            pe.wait_ge(s("weights_in"), 16 * 4)
            ttranspose(pe, "ret", yn)
            pe.wait_ge(s("turned_out"), 2 * B * TURN["ret"] + 2 * B)
            for i in range(NT):
                r = ROWS[i % 3]
                if i >= 4:
                    pe.wait_ge(s("ret_v_out"), i - 3)
                for k in range(2):
                    last = mm(P[0:r, i % 4, 0:C], tT[:, k, col(i):col(i) + r], wret[:, k, 2 * C:3 * C], start=(k == 0), stop=(k == 1))
                last.then_inc(s("ret_v"), 1)
            for m in range(4):
                for b in range(B):
                    u = m * B + b
                    if u >= 4:
                        pe.wait_ge(s("ret_qk_out"), u - 3)
                    for k in range(2):
                        last = mm(P[0:CH, 4 + u % 4, 0:N], wret[:, k, m * CH:(m + 1) * CH], tT[:, k, b * NP:b * NP + N],
                                  start=(k == 0), stop=(k == 1))
                    last.then_inc(s("ret_qk"), 1)
            pe.wait_ge(s("ret_qk_out"), 8)
            for b in range(B):
                for j in range(3):
                    u = b * 3 + j
                    r = ROWS[j]
                    if u >= 4:
                        pe.wait_ge(s("ret_scores_out"), u - 3)
                    for k in range(2):
                        last = mm(P[0:r, 4 + u % 4, j * 128:N], qkT[:, 2 + k, b * NP + j * 128:b * NP + j * 128 + r],
                                  qkT[:, k, b * NP + j * 128:b * NP + N], start=(k == 0), stop=(k == 1))
                    last.then_inc(s("ret_scores"), 1)
            pe.wait_ge(s("ret_scores_out"), NT)
            pe.wait_ge(s("ret_v_out"), NT)
            for b in range(B):
                for i in range(3):
                    if b * 3 + i >= 4:
                        pe.wait_ge(s("ret_o_out"), b * 3 + i - 3)
                    r = ROWS[i]
                    for j in range(i + 1):
                        last = mm(P[0:r, (b * 3 + i) % 4, 0:C], sT[0:ROWS[j], b * 3 + j, i * 128:i * 128 + r],
                                  vtok[0:ROWS[j], b * 3 + j, :], start=(j == 0), stop=(j == i))
                    last.then_inc(s("ret_o"), 1)

            pe.wait_ge(s("attention_weights_in"), 16 * 5)
            ttranspose(pe, "ln1", yn)
            pe.wait_ge(s("turned_out"), 2 * B * TURN["ln1"] + 2 * B)
            for i in range(NT):
                r = ROWS[i % 3]
                if i >= 4:
                    pe.wait_ge(s("att_v_out"), i - 3)
                for k in range(2):
                    last = mm(P[0:r, 4 + i % 4, 0:C], tT[:, k, col(i):col(i) + r], wva[:, k, :], start=(k == 0), stop=(k == 1))
                last.then_inc(s("att_v"), 1)
            pe.wait_ge(s("att_v_out"), NT)
            pe.wait_ge(s("vaug_ones"), 1)
            pe.wait_ge(s("selr_set"), 1)
            for b in range(B):
                if b == 1:
                    pe.wait_ge(s("att_exp"), 3 * HEADS)
                    pe.wait_ge(s("att_o"), 9)
                for p in range(PAIRS):
                    u = b * PAIRS + p
                    if u >= 2:
                        pe.wait_ge(s("k_lo"), u - 1)
                    for m in range(2):
                        for k in range(2):
                            last = mm(P[:, 2 * (u % 2) + m, 0:NP], wqa[:, k, m, p * 128:(p + 1) * 128], tT[:, k, b * NP:(b + 1) * NP],
                                      start=(k == 0), stop=(k == 1))
                    last.then_inc(s("qk_stack"), 1)
                    pe.wait_ge(s("q_lo"), 2 * (u + 1))
                    pe.wait_ge(s("k_lo"), u + 1)
                    for z in range(2):
                        for i in range(3):
                            w = (u * 2 + z) * 3 + i
                            if w >= 4:
                                pe.wait_ge(s("att_max"), w - 3)
                            rows_ = slice(64 * z, 64 * z + 64)
                            mm(P[0:ROWS[i], 4 + w % 4, 0:NP], qst[rows_, p, i * 128:i * 128 + ROWS[i]], kst[rows_, p, :],
                               start=True, stop=True).then_inc(s("att_scores"), 1)
                pe.wait_ge(s("att_max"), (b + 1) * HEADS * 3)
                for i in range(3):
                    r = ROWS[i]
                    last = nc.tensor.transpose(P[0:HEADS, 0, i * 128:i * 128 + r], mx[0:r, i, :], ident[0:r, 0:r])
                last.then_inc(s("att_maxT"), 1)
                pe.wait_ge(s("att_max_out"), b + 1)
                pe.wait_ge(s("att_max_pad"), 1)

                def pv(u):
                    hh, j = (u // 3) % HEADS, u % 3
                    r = ROWS[j]
                    if hh % 4 == 0 and j == 0 and u >= 12:
                        pe.wait_ge(s("att_ao"), u // 12)
                    pe.wait_ge(s("att_exp"), u + 1)
                    mm(P[32 * (hh % 4):32 * (hh % 4) + 32, 6, 0:N], vaug[0:r, (u // (3 * HEADS)) * 3 + j, hh, :], pt[0:r, u % 6, :],
                       start=(j == 0), stop=(j == 2), tile_position=None).then_inc(s("att_pv"), 1)
                    if hh % 4 == 3 and j == 2:
                        grp = u // 12
                        pe.wait_ge(s("att_ao"), grp + 1)
                        if grp >= 1:
                            pe.wait_ge(s("att_o"), 3 * grp)
                        for i in range(3):
                            nc.tensor.transpose(P[0:ROWS[i], 7, i * 128:(i + 1) * 128], ao[:, grp % 3, i * 128:i * 128 + ROWS[i]],
                                                ident[:, :]).then_inc(s("att_o_turned"), 1)

                base = b * HEADS * 3
                for hh in range(HEADS):
                    for j in range(3):
                        u = base + hh * 3 + j
                        r = ROWS[j]
                        if u >= 2:
                            pe.wait_ge(s("att_exp"), u - 1)
                        rows_ = slice(64 * (hh % 2), 64 * (hh % 2) + 64)
                        mm(P[0:r, 4 + u % 2, 0:NP], kst[rows_, hh // 2, j * 128:j * 128 + r], qst[rows_, hh // 2, :],
                           start=True, stop=False)
                        mm(P[0:r, 4 + u % 2, 0:NP], selr[:, hh, 0:r], mxT[:, :], start=False, stop=True).then_inc(s("att_scoresT"), 1)
                        if u > base:
                            pv(u - 1)
                pv(base + HEADS * 3 - 1)
            pe.wait_ge(s("att_o"), 3 * B * 3)
            ttranspose(pe, "proj", yn)
            pe.wait_ge(s("turned_out"), 2 * B * TURN["proj"] + 2 * B)
            for i in range(NT):
                r = ROWS[i % 3]
                if i >= 4:
                    pe.wait_ge(s("att_proj_out"), i - 3)
                for k in range(2):
                    last = mm(P[0:r, i % 4, 0:C], tT[:, k, col(i):col(i) + r], wpa[:, k, :], start=(k == 0), stop=(k == 1))
                last.then_inc(s("att_proj"), 1)
            moe_tensor(pe, 0)

            ttranspose(pe, "att1", yn)
            pe.wait_ge(s("turned_out"), 2 * B * TURN["att1"] + 2 * B)
            for b in range(B):
                for k in range(2):
                    last = mm(P[0:64, 4 + b, 0:N], w1q[:, k, :], tT[:, k, b * NP:b * NP + N], start=(k == 0), stop=(k == 1))
                last.then_inc(s("q1"), 1)
            for i in range(NT):
                r = ROWS[i % 3]
                if i >= 4:
                    pe.wait_ge(s("kv1_out"), i - 3)
                for k in range(2):
                    last = mm(P[0:r, i % 4, 0:2 * C], tT[:, k, col(i):col(i) + r], w1kv[:, k, :], start=(k == 0), stop=(k == 1))
                last.then_inc(s("kv1"), 1)
            pe.wait_ge(s("kv1_out"), NT)
            for b in range(B):
                for g in range(G1):
                    for j in range(3):
                        r = ROWS[j]
                        last = mm(P[0:CH, 4 + b * 2 + g, 0:CH], kv[0:r, b * 3 + j, g * CH:(g + 1) * CH],
                                  kv[0:r, b * 3 + j, C + g * CH:C + (g + 1) * CH], start=(j == 0), stop=(j == 2))
                    last.then_inc(s("ctx1"), 1)
            pe.wait_ge(s("ctx_soft"), 1)
            for b in range(B):
                last = nc.tensor.transpose(P[0:64, b, 0:CH], at[:, 2 * b:2 * b + 2, :].rearrange("p g e -> p (g e)"), ident[0:CH, 0:CH])
            last.then_inc(s("at_turned"), 1)
            pe.wait_ge(s("at_spread"), B)
            for u in range(2 * HG * G1):
                if u >= 4:
                    pe.wait_ge(s("heads1_odd" if u % 2 else "heads1_even"), (u - 4) // 2 + 1)
                b, hh, g = u // 8, u % 8 // G1, u % G1
                mm(P[:, 4 + u % 4, 0:N], atT[32 * g:32 * g + 32, b, hh, :, :].rearrange("p q d -> p (q d)"),
                   q1T[32 * g:32 * g + 32, b * NP:b * NP + N], start=True, stop=True).then_inc(s("heads1"), 1)
            pe.wait_ge(s("heads1_even"), 8)
            pe.wait_ge(s("heads1_odd"), 8)
            for i in range(NT):
                r = ROWS[i % 3]
                if i >= 4:
                    pe.wait_ge(s("att1_o_out"), i - 3)
                first = (i % 3) * 256
                for half in range(2):
                    last = mm(P[0:r, i % 4, 0:C], mixed[:, i // 3, first + half:first + half + 2 * r - 1:2], w1p[:, half, :],
                              start=(half == 0), stop=(half == 1))
                last.then_inc(s("att1_o"), 1)
            moe_tensor(pe, 1)
            for i in range(NT):
                r = ROWS[i % 3]
                pe.wait_ge(s("feats_ready"), 1)
                if i >= 4:
                    pe.wait_ge(s("out_ready"), i - 3)
                for z in range(2):
                    last = mm(P[0:r, i % 4, 0:C], gf[:, z, (i % 3) * 128:(i % 3) * 128 + r], outw_rows[:, z, i // 3, :],
                              start=(z == 0), stop=(z == 1))
                last.then_inc(s("spec_o"), 1)


def kernel(**inputs):
    import numpy as np
    import concourse.bacc as bacc
    from concourse.bass_utils import run_bass_kernel_spmd as run

    x = {k: np.asarray(v) for k, v in inputs.items()}
    f = np.float32
    T = np.transpose
    pad = lambda w, n: np.concatenate([w, np.zeros((w.shape[0], n - w.shape[1]), w.dtype)], axis=1)
    halves = lambda v_: v_.reshape(2, CH).T
    vw = x["L1_ffn_v_w"][:, None]
    own = [np.concatenate([vw if m == n else np.zeros_like(vw) for m in range(CHAINS)], axis=1) for n in range(CHAINS)]
    bc = lambda v_: np.broadcast_to(v_, (C,))
    heads = x["L0_ffn_qkv_w"][:2 * C].reshape(2, HEADS, 1, HD, C)
    qk = np.broadcast_to(heads, (2, HEADS, 4, HD, C)).reshape(2, HEADS * 4 * HD, C)
    wq1 = x["L1_attn_Wq"]
    wp1 = x["L1_attn_Wproj"].reshape(2, 4, HD1, C)
    spread = T(np.concatenate([wp1, np.zeros((2, 4, 32 - HD1, C), f)], axis=2), (1, 2, 0, 3)).reshape(128, 2, C)
    diff = np.arange(N)[None, :] - np.arange(384)[:, None]
    decay = np.where(diff >= 0, np.float64(f(0.99)) ** np.maximum(diff, 0), 0.0) / np.sqrt(float(C))
    p = np.arange(128)
    copy = (p // HD) % 4
    ln = "L0_tok_ln"
    arrays = {
        "patches": T(x["x"].reshape(B, 32, 16, 8, 16, 8), (1, 3, 5, 0, 2, 4)).reshape(2048, B * TOK),
        "conv_w": x["L0_tok_conv_w"].reshape(D, 2048).T,
        "qkv_w": x["L0_tok_qkv_w"], "out_w": x["L0_tok_out_w"], "ff1_w": x["L0_tok_ff1_w"], "ff2_w": x["L0_tok_ff2_w"],
        "head_w": x["L0_tok_head_w"],
        "ret_w": x["L0_attn_W_qkv"].T, "v_w": x["L0_ffn_qkv_w"][2 * C:].T, "proj_w": x["L0_ffn_proj_w"].T,
        "gate_w": np.concatenate([x["L0_ffn_gate_w"].T, x["L1_ffn_gate_w"], *own], axis=1),
        "q1_w": np.concatenate([pad(wq1[:, :HD1], 32), pad(wq1[:, HD1:], 32)], axis=1),
        "kv1_w": x["L1_attn_Wkv"], "proj1_w": spread, "qk_w": T(qk, (0, 2, 1)),
        "w1": np.stack([T(x["L0_ffn_w1"], (0, 2, 1)), x["L1_ffn_w1"]]),
        "w2": np.stack([T(x["L0_ffn_w2"], (0, 2, 1)), x["L1_ffn_w2"]]),
        "b1": T(np.stack([x["L0_ffn_b1"], x["L1_ffn_b1"]]).reshape(2, EXPERTS, HC, 128), (3, 0, 1, 2)),
        "b2": np.stack([x["L0_ffn_b2"], x["L1_ffn_b2"]]),
        "txt": x["txt"],
        "rows": np.stack([x["L0_tok_head_b"], x["L0_attn_b_qkv"][2 * C:], x["L0_ffn_proj_b"], x["L1_attn_bproj"],
                          x["L1_ffn_out_b"], x["L1_ffn_bk_scale"], bc(x["L1_ffn_v_b"])]),
        "tok_rows": np.concatenate([x["L0_tok_conv_b"][None], x["L0_tok_out_b"], x["L0_tok_ff2_b"]]),
        "tok_cols": np.stack([x[ln + n][l] for l in range(LAYERS) for n in ("1_g", "1_b", "2_g", "2_b")]
                             + [x[ln + "f_g"], x[ln + "f_b"]], axis=1),
        "ff1_b": T(x["L0_tok_ff1_b"].reshape(LAYERS * 4, 128), (1, 0)),
        "ch_cols": np.concatenate([x["L0_attn_b_qkv"][:2 * C].reshape(4, CH).T]
                                  + [halves(x["L0_ffn_" + n]) for n in ("ln1_g", "ln1_b", "ln2_g", "ln2_b")], axis=1),
        "gate_rows": np.stack([x["L0_ffn_gate_b"], x["L1_ffn_gate_b"], np.arange(EXPERTS, dtype=f)]),
        "outw_rows": np.stack([np.concatenate([x["L1_ffn_out_w"][:, None], np.zeros((2, 1, C), f)][::1 - 2 * b], axis=1)
                               for b in range(B)]),
        "ident": np.eye(128, dtype=f),
        "decay": T(decay.reshape(3, 128, N), (1, 0, 2)).astype(f),
        "signs": np.stack([np.where(copy % 2 == 0, -1.0, 1.0) * HD ** -0.5, copy % 2], axis=1).astype(f),
        "sel": np.broadcast_to(-np.eye(HEADS, dtype=f)[:, :, None], (HEADS, HEADS, 128)),
        "gmask": np.broadcast_to((np.arange(CH)[:, None] // HD1 == np.arange(HG)[None, :])[:, :, None],
                                 (CH, HG, HD1)).astype(f),
    }
    arrays = {"in_" + k: np.ascontiguousarray(v) for k, v in arrays.items()}
    nc = bacc.Bacc("TRN2", target_bir_lowering=False, num_devices=1)
    aps = {k[3:]: nc.dram_tensor(k, v.shape, mybir.dt.from_np(v.dtype), kind="ExternalInput").ap() for k, v in arrays.items()}
    out = nc.dram_tensor("out_0", (B, N, C), F32, kind="ExternalOutput").ap()
    fusion_kernel(nc, aps, out)
    return run(nc, [arrays], core_ids=[0]).results[0]["out_0"]
```

```python
import concourse.bass as bass
from concourse import mybir
from contextlib import ExitStack

F32 = mybir.dt.float32
F32R = mybir.dt.float32r
U32 = mybir.dt.uint32
ALU = mybir.AluOpType
ACT = mybir.ActivationFunctionType
AX = mybir.AxisListType

B = 2
TOK = 256
TXT = 77
N = TOK + TXT
NP = N + 1
COLS = B * NP
KP = 2048 // 128
D = 128
INNER = 512
DH = 64
LAYERS = 2
C = 192
CH = 96
ROWS = (128, 128, TXT)
NT = 3 * B
HEADS = 12
HD = 16
PAIRS = HEADS // 2
EXPERTS = 8
HID = 768
HC = HID // 128
EPS = 1e-5
G1 = 2
HG = 4
PROJ_BANKS = (2, 3, 0, 6, 7, 4)
LOGIT_BANKS = ((2, 7), (4, 5))
HD1 = C // (G1 * HG)
TURN_AT, PROJECT_AT, MIX_AT, GATE_AT = 5, 8, 17, 22
CL = 19
CN = 18
SL = CL * CN
CHAINS = 2 * B
ARENA = 36480

IMAGE = ((0, 1, 2), (3, 4, 5))
LN_TAGS = [(f"t{l}{name}_{b}", (3 * b, 3 * b + 1)) for l in range(LAYERS) for name in ("ln1", "ln2") for b in range(B)]
LN_TAGS += [(f"tlnf_{b}", (3 * b, 3 * b + 1)) for b in range(B)]
LN_TAGS += [("ret_0", IMAGE[0]), ("ret_1", IMAGE[1]), ("ffn0_0", IMAGE[0]), ("ln1_0", IMAGE[0]), ("ffn0_1", IMAGE[1]),
            ("ln1_1", IMAGE[1]), ("ln2_0", IMAGE[0]), ("ln2_1", IMAGE[1]),
            ("att1_0", IMAGE[0]), ("att1_1", IMAGE[1]), ("ffn1_0", IMAGE[0]), ("ffn1_1", IMAGE[1])]
LN_TILES = dict(LN_TAGS)
LN_ORDER = {tag: n for n, (tag, _) in enumerate(LN_TAGS)}
LN_BASE = {tag: sum(len(tiles) for _, tiles in LN_TAGS[:n]) for n, (tag, _) in enumerate(LN_TAGS)}
TURN = {tag: n for n, tag in enumerate(("ret", "proj", "att1"))}
X_TURN = {tag: n for n, tag in enumerate(("ln1", "ln2", "ffn1"))}


def fusion_kernel(nc, a, out):
    ctx = ExitStack()
    with ctx:
        def sb(name, shape, dt=F32):
            return ctx.enter_context(nc.sbuf_tensor(name, shape, dt))

        def sem(name):
            return ctx.enter_context(nc.semaphore(name))

        P = ctx.enter_context(nc.psum_tensor("P", [128, 8, 512], F32))

        ident = sb("ident", [128, 128])
        neghalf = sb("neghalf", [128, 8])
        stats = sb("stats", [128, NT, 6])
        mv = sb("mv", [128, NT, 2])
        varr = sb("varr", [128, NT])
        rstd = sb("rstd", [128, NT])
        rows = sb("rows", [128, 7, C])
        tokrows = sb("tokrows", [128, 5, D])
        gate_rows = sb("gate_rows", [128, 3, EXPERTS])
        tokcols = sb("tokcols", [128, 2 * (2 * LAYERS + 1)])
        ff1b = sb("ff1b", [128, LAYERS * 4])
        chcols = sb("chcols", [CH, 4])
        signs = sb("signs", [128, 3])
        b1s = sb("b1s", [128, 2, EXPERTS, HC])
        b1now = [sb(f"b1now{i}", [128, HC]) for i in range(2)]
        b2s = sb("b2s", [32 + EXPERTS, 2, C])
        gmask = sb("gmask", [CH, HG, HD1])
        outw_rows = sb("outw_rows", [B, 2, B, C])

        yn = sb("yn", [128, NT, C + 64])
        ynt = yn[:, :, 0:D]
        h = sb("h", [128, NT, C])
        tT = sb("tT", [CH, 2, COLS])
        segmax = sb("segmax", [128, 4, 8])
        segsum = sb("segsum", [128, 4, 8])
        kmax = sb("kmax", [128, 4, B])
        ksum = sb("ksum", [128, 4, B])
        lg = sb("lg", [128, NT, EXPERTS])
        m8 = sb("m8", [128, NT, 8])
        i8 = sb("i8", [128, NT, 8], U32)
        idf = sb("idf", [128, NT, 2])
        s01 = sb("s01", [128, NT, 2])
        gtmp = sb("gtmp", [128, NT])
        cwA = sb("cwA", [128, NT, EXPERTS])
        cw = sb("cw", [128, NT, 32])
        cwT = sb("cwT", [32 + EXPERTS, NP])
        raw1 = [sb(f"raw1_{i}", [128, 2, HID]) for i in range(2)]
        raw2 = [sb(f"raw2_{i}", [128, HC, C]) for i in range(2)]
        mx = sb("mx", [128, B, 3, HEADS])
        rden = sb("rden", [128, 3, 4])
        c1 = sb("c1", [CH, 4])
        wret = sb("wret", [CH, 2, 3 * C])
        wgate = sb("wgate", [128, 2, 2 * EXPERTS + 4 * CHAINS])
        mcols = sb("mcols", [128, 8])

        arena = sb("arena", [128, ARENA])
        base = nc.lookup_mloc(arena).addr
        assert base % 32 == 0
        cursor = [0]

        def place(name, parts, *shape, dt=F32, col=None):
            if col is not None:
                cursor[0] = col
            t = nc.alloc_sbuf_tensor_at(name, [parts, *shape], dt, offset=base + 4 * cursor[0])
            size = 1
            for n in shape:
                size *= n
            cursor[0] += (size + 7) // 8 * 8
            assert cursor[0] <= ARENA
            return t[(slice(None),) * (1 + len(shape))]

        patches = place("patches", 128, KP, 512, col=0)
        convw = place("convw", 128, KP, D)
        qs = place("qs", 128, 4, 512)
        vt = place("vt", 128, 4, 512)
        kt = place("kt", 128, 4, 512)
        ke = place("ke", 128, 4, 512)
        w2 = place("w2", 128, B, 4, D)
        hT = qs
        wqkv = place("wqkv", 128, LAYERS, 3 * INNER)
        wout = place("wout", 128, LAYERS, 4, D)
        wff1 = place("wff1", 128, LAYERS, 512)
        wff2 = place("wff2", 128, LAYERS, 4, D)
        whead = place("whead", 128, C)
        xt = place("xt", 128, NT, D)
        yT = place("yT", 128, 512)
        qT = place("qT", 128, 4, 512)
        bd = place("bd", 128, B, 4, 128)
        tok_end = cursor[0]

        hid_hi = [place(f"hid_hi{b}", 128, HC, NP, dt=F32R, col=0 if b == 0 else None) for b in range(B)]
        hid_lo = [place(f"hid_lo{b}", 128, HC, NP, dt=F32R) for b in range(B)]
        gelus = place("gelus", 128, 3, 2, NP)
        weights_col = cursor[0]
        w1a_hi, w1a_lo, w1b, w2_parts = [], [], [], []
        for i in range(2):
            expert_col = cursor[0]
            for parts, n, sh in ((w1a_hi, "w1a_hi", [HID]), (w1a_lo, "w1a_lo", [HID]), (w1b, "w1b", [HID]),
                                 (w2_parts, "w2_parts", [HC, 2, C])):
                parts.append(place(f"{n}{i}", 128, *sh, dt=F32R))
        xf = place("xf", 128, 2, COLS)
        x_hi = place("x_hi", 128, 2, COLS, dt=F32R)
        x_lo = place("x_lo", 128, 2, COLS, dt=F32R)
        shared = cursor[0]

        qkT = place("qkT", CH, 4, COLS, col=0)
        sT = place("sT", 128, B * 3, N)
        vtok = place("vtok", 128, NT, C)
        decay = place("decay", 128, 3, N)
        wq_raw = place("wq_raw", 128, 2, 2 * PAIRS * 128)
        vaug = place("vaug", 128, NT, HEADS, 32, col=0)
        pt = place("pt", 128, 6, N)
        ao = place("ao", 128, 3, N)
        mxT = place("mxT", HEADS, B, NP, dt=F32R)
        qst1 = place("qst1", 128, PAIRS, NP, dt=F32R)
        kst1 = place("kst1", 128, PAIRS, NP, dt=F32R)
        assert cursor[0] <= weights_col
        wq_hi = place("wq_hi", 128, 2 * PAIRS * 128, dt=F32R, col=expert_col)
        wq_lo = place("wq_lo", 128, 2 * PAIRS * 128, dt=F32R)
        wq_b = place("wq_b", 128, 2 * PAIRS * 128, dt=F32R)
        qst0 = place("qst0", 128, PAIRS, NP, dt=F32R, col=shared)
        kst0 = place("kst0", 128, PAIRS, NP, dt=F32R)
        khi = place("khi", 128, 2, NP, dt=F32R)
        qhi = place("qhi", 128, 2, NP, dt=F32R)
        qst, kst = (qst0, qst1), (kst0, kst1)
        kv = place("kv", 128, NT, 2 * C, col=0)
        q1s = place("q1s", 128, G1, COLS, dt=F32R)
        mixed = place("mixed", 128, B, 2 * N)
        atS = place("atS", 128, B, G1, HG, 4, 32, dt=F32R)
        cm = place("cm", CH, 4, HG, HD1, col=shared + 5040)
        cc = place("cc", CH, 4, HD1)
        at = place("at", CH, B * G1, 4, 32)
        selr = place("selr", HEADS, HEADS, 128, dt=F32R, col=max(tok_end, cursor[0]))
        selw = place("selw", HEADS, HEADS, 128)
        wva = place("wva", 128, 2, C, col=cursor[0] - HEADS * 128)
        wpa = place("wpa", CH, 2, C)
        w1q = place("w1q", CH, 2, G1 * 128)
        w1kv = place("w1kv", CH, 2, 2 * C)
        w1p = place("w1p", 128, 2, C)
        sums = place("sums", 128, NT, 2, C)
        x2 = sums[:, :, 0, :]
        sa = place("sa", CHAINS, SL, col=shared)
        sE = place("sE", CHAINS, CL + 2, 2, 2, CN)
        sprod = place("sprod", CHAINS, 2, 2, CN)
        smap = place("smap", CHAINS, CN, 2, 2, 2, 2)
        sy = place("sy", CHAINS, CN, 2, 2)
        ssum = place("ssum", CHAINS, 24)
        snorm = place("snorm", CHAINS, 6, CN)
        su = place("su", CHAINS, 2, CN)
        sp_ = place("sp_", CHAINS, CL + 1, 2, CN)
        st = [place(f"st{k}", CHAINS, CL + 1, 2, CN) for k in range(2)]
        sd = place("sd", CHAINS, 2, SL)
        se = place("se", B, 2, SL)
        gf = place("gf", B, 2, N)
        gt = place("gt", B, 3, N)
        spec_squares, spec_inverses = st[0][:, 0:CL, 0], sE[:, 0:CL, 0, 0]
        powers = place("powers", CHAINS, 2, CN)
        assert cursor[0] <= ARENA - NT * C

        S = {}

        def s(name):
            if name not in S:
                S[name] = sem(name)
            return S[name]

        block = ctx.enter_context(nc.Block())

        def col(i):
            return (i // 3) * NP + (i % 3) * 128

        def layernorm_stats(dve, tag, src):
            tiles = LN_TILES[tag]
            for t in tiles:
                nc.vector.bn_stats(stats[:, t, :], src[:, t, :]).then_inc(s("ln_stats"), 1)
            dve.wait_ge(s("ln_stats"), LN_BASE[tag] + len(tiles))
            for t in tiles:
                nc.vector.bn_aggr(mv[:, t, :], stats[:, t, :]).then_inc(s("ln_mean"), 1)

        def layernorm_apply(dve, tag, dst, src):
            tiles = LN_TILES[tag]
            dve.wait_ge(s("ln_mean"), LN_BASE[tag] + len(tiles))
            dve.wait_ge(s("ln_rstd"), LN_ORDER[tag] + 1)
            for t in tiles:
                if tag in ("ln1_0", "ln1_1", "ln2_0", "ln2_1", "ffn1_0", "ffn1_1"):
                    nc.vector.tensor_scalar(dst[:, t, C:], src[:, t, 128:C], mv[:, t, 0:1], rstd[:, t:t + 1],
                                            ALU.subtract, ALU.mult)
                nc.vector.tensor_scalar(dst[:, t, 0:src.shape[-1]], src[:, t, :], mv[:, t, 0:1], rstd[:, t:t + 1],
                                        ALU.subtract, ALU.mult).then_inc(s("ln_norm"), 1)

        def layernorm(dve, tag, dst, src):
            layernorm_stats(dve, tag, src)
            layernorm_apply(dve, tag, dst, src)

        def prstd(pool, tag):
            tiles = LN_TILES[tag]
            t = slice(tiles[0], tiles[-1] + 1)
            pool.wait_ge(s("ln_mean"), LN_BASE[tag] + len(tiles))
            nc.gpsimd.tensor_scalar(varr[:, t], mv[:, t, 1], EPS, 0.0, ALU.add, ALU.add).then_inc(s("ln_var"), 1)
            pool.wait_ge(s("ln_var"), LN_ORDER[tag] + 1)
            nc.gpsimd.tensor_tensor(rstd[:, t], varr[:, t], neghalf[:, t], ALU.pow).then_inc(s("ln_rstd"), 1)

        def reshuffled(u, quarter):
            b, first = u // 8, (u % 8) * N
            skip = (quarter - first) % 4
            n = (N - skip + 3) // 4
            m = (first + skip - quarter) // 4
            part = slice(32 * quarter, 32 * quarter + 32)
            return mixed[part, b, m:m + n], P[part, 4 + u % 4, skip:skip + 4 * (n - 1) + 1:4]

        def ttranspose(pe, tag, images=range(B)):
            for b in images:
                for i in IMAGE[b]:
                    if tag == "ret":
                        pe.wait_ge(s("ln_norm"), LN_BASE["ret_0"] + i + 1)
                    elif tag == "att1":
                        pe.wait_ge(s("ln_norm"), LN_BASE["att1_0"] + i + 1)
                    r = ROWS[i % 3]
                    for k in range(2):
                        last = nc.tensor.transpose(P[0:CH, turn_banks(tag, b) + k, (i % 3) * 128:(i % 3) * 128 + r],
                                                   yn[0:r, i, k * CH:(k + 1) * CH], ident[0:r, 0:r])
                last.then_inc(s("turned"), 1)

        def aevacuate(act, tag, images=range(B)):
            for b in images:
                act.wait_ge(s("turned"), B * TURN[tag] + b + 1)
                for k in range(2):
                    nc.scalar.activation(tT[:, k, b * NP:b * NP + N], P[0:CH, turn_banks(tag, b) + k, 0:N], ACT.Copy)\
                        .then_inc(s("turned_out"), 1)

        def turn_banks(tag, b):
            return 0 if tag in ("ret", "att1") else 4 if (tag, b) == ("proj", 1) else 2 * b

        def stack_bank(u):
            return 2 * (u % 2) if u < PAIRS else 0

        def score_bank(w):
            return 4 + w % 3 if w < 6 * PAIRS else 2 + w % 2

        def xevacuate(act, tag, b, banks, cols, halves=(0, 1)):
            for k in halves:
                src = P[:, banks + k, 0:N]
                for dst, sem_ in ((xf, "xf"), (x_hi, "x_hi")):
                    dst = dst[:, k, b * NP:b * NP + N]
                    if cols is None:
                        last = nc.scalar.activation(dst, src, ACT.Copy)
                    else:
                        last = nc.scalar.activation(dst, src, ACT.Identity, bias=mcols[:, cols + 2 + k:cols + 3 + k],
                                                    scale=mcols[:, cols + k:cols + k + 1])
                    last.then_inc(s(sem_), 1)

        def xlo(dve, tag, b):
            n = 2 * (B * X_TURN[tag] + b + 1)
            dve.wait_ge(s("xf"), n)
            dve.wait_ge(s("x_hi"), n)
            cols = slice(b * NP, (b + 1) * NP)
            nc.vector.tensor_tensor(x_lo[:, :, cols], xf[:, :, cols], x_hi[:, :, cols].bitcast(F32), ALU.subtract)\
                .then_inc(s("x_lo"), 1)

        def xturn(pe, tag, tiles, bank):
            for k in range(2):
                last = xturn_half(pe, tag, tiles, bank + k, k)
            last.then_inc(s("x_turned"), 1)

        def xturn_half(pe, tag, tiles, bank, k):
            for n, i in enumerate(tiles):
                pe.wait_ge(s("ln_norm"), LN_BASE[tag] + LN_TILES[tag].index(i) + 1)
                r = ROWS[i % 3]
                src = yn[0:r, i, 128:C + 64] if k else yn[0:r, i, 0:128]
                last = nc.tensor.transpose(P[:, bank, n * 128:n * 128 + r], src, ident[0:r, 0:r])
            return last

        def spectral(pool):
            count = [0]
            g = nc.gpsimd

            def step(ins):
                count[0] += 1
                ins.then_inc(s("spec_step"), 1)

            def link(ins):
                step(ins)
                pool.wait_ge(s("spec_step"), count[0])

            def wide(ap, shape):
                return ap.broadcast_to(shape)

            for ap, value in ((powers[:, 0, :], -1.0), (powers[:, 1, :], -0.5), (sE[:, 0:2], 0.0), (sy[:, 0], 0.0)):
                link(g.memset(ap, value))
            link(g.memset(sE[:, 0, 0, 0, :], 1.0))
            link(g.memset(sE[:, 1, 1, 0, :], 1.0))
            link(g.memset(sy[:, 0, 1, 0:1], 1.0))
            pool.wait_ge(s("sa_ready"), 1)
            link(g.tensor_scalar(sa[:, 0:N], sa[:, 0:N], 3.0, -3.0, ALU.min, ALU.max))
            link(g.tensor_scalar(sa[:, 0:N], sa[:, 0:N], -2.0, 0.0, ALU.add, ALU.add))
            av = sa.rearrange("p (n l) -> p l n", l=CL)
            shape = [CHAINS, 2, 2, CN]
            for i in range(CL):
                new, p1, p2 = sE[:, i + 2], sE[:, i + 1], sE[:, i]
                link(g.tensor_tensor(sprod, p1, wide(av[:, i, :].unsqueeze(1).unsqueeze(1), shape), ALU.mult))
                link(g.tensor_tensor(sprod, sprod, p2, ALU.subtract))
                step(g.tensor_tensor(new[:, :, 0], sprod[:, :, 0], p1[:, :, 1], ALU.add))
                link(g.tensor_tensor(new[:, :, 1], sprod[:, :, 1], p1[:, :, 0], ALU.subtract))
            last = sE[:, CL + 1, 1]
            link(g.tensor_tensor(snorm[:, 0:2], last, last, ALU.mult))
            link(g.tensor_tensor(snorm[:, 2], snorm[:, 0], snorm[:, 1], ALU.add))
            link(g.tensor_tensor(snorm[:, 3], snorm[:, 2], powers[:, 1, :], ALU.pow))
            link(g.tensor_scalar(snorm[:, 4], snorm[:, 3], -1.0, 0.0, ALU.mult, ALU.add))
            for zo in range(2):
                for zi in range(2):
                    scale = snorm[:, 4 if (zo, zi) == (0, 1) else 3]
                    dst = smap[:, :, :, zo, :, zi].rearrange("p n r w -> p r w n")
                    step(g.tensor_tensor(dst, sE[:, CL:CL + 2, :, zo ^ zi, :],
                                         wide(scale.unsqueeze(1).unsqueeze(1), shape), ALU.mult))
            pool.wait_ge(s("spec_step"), count[0])
            for n in range(CN - 1):
                prod = ssum[:, 0:16].rearrange("p (i k) -> p i k", k=4)
                link(g.tensor_tensor(prod, smap[:, n].rearrange("p r o w i -> p (r o) (w i)"),
                                     wide(sy[:, n].rearrange("p w i -> p (w i)").unsqueeze(1), [CHAINS, 4, 4]), ALU.mult))
                half = ssum[:, 16:24].rearrange("p (i k) -> p i k", k=2)
                link(g.tensor_tensor(half, prod[:, :, 0:2], prod[:, :, 2:4], ALU.add))
                link(g.tensor_tensor(sy[:, n + 1].rearrange("p w i -> p (w i)"), half[:, :, 0], half[:, :, 1], ALU.add))
            qr, qi, pr, pi = (sy[:, :, w, z] for w in range(2) for z in range(2))

            def divide(dst_r, dst_i, nr, ni, dr, di, t, power=None):
                step(g.tensor_tensor(t[0], dr, dr, ALU.mult))
                link(g.tensor_tensor(t[1], di, di, ALU.mult))
                if power is None:
                    g.tensor_tensor(t[0], t[0], t[1], ALU.add).then_inc(s("spec_square"), 1)
                else:
                    link(g.tensor_tensor(t[0], t[0], t[1], ALU.add))
                    step(g.tensor_tensor(t[4], t[0], power, ALU.pow))
                step(g.tensor_tensor(t[2], nr, dr, ALU.mult))
                link(g.tensor_tensor(t[3], ni, di, ALU.mult))
                link(g.tensor_tensor(t[2], t[2], t[3], ALU.add))
                if power is None:
                    pool.wait_ge(s("spec_inverse"), 1)
                step(g.tensor_tensor(dst_r, t[2], t[4], ALU.mult))
                step(g.tensor_tensor(t[0], ni, dr, ALU.mult))
                link(g.tensor_tensor(t[1], nr, di, ALU.mult))
                link(g.tensor_tensor(t[0], t[0], t[1], ALU.subtract))
                link(g.tensor_tensor(dst_i, t[0], t[4], ALU.mult))

            divide(su[:, 0], su[:, 1], qr, qi, pr, pi, [snorm[:, k] for k in range(5)], powers[:, 0, :])
            rows_ = slice(1, CL + 2)
            lo, hi = sE[:, rows_, 0], sE[:, rows_, 1]
            big = [CHAINS, CL + 1, 2, CN]
            step(g.tensor_tensor(st[0], lo, wide(su[:, 0].unsqueeze(1).unsqueeze(1), big), ALU.mult))
            link(g.tensor_tensor(st[1], lo, wide(su[:, 1].unsqueeze(1).unsqueeze(1), big), ALU.mult))
            link(g.tensor_tensor(st[0], st[0], hi, ALU.add))
            step(g.tensor_tensor(sp_[:, :, 0], st[0][:, :, 0], st[1][:, :, 1], ALU.subtract))
            link(g.tensor_tensor(sp_[:, :, 1], st[0][:, :, 1], st[1][:, :, 0], ALU.add))
            order = lambda ap: ap.rearrange("p (n l) -> p l n", l=CL)
            divide(order(sd[:, 0]), order(sd[:, 1]), sp_[:, 1:CL + 1, 0], sp_[:, 1:CL + 1, 1], sp_[:, 0:CL, 0], sp_[:, 0:CL, 1],
                   [spec_squares, st[0][:, 0:CL, 1], st[1][:, 0:CL, 0], st[1][:, 0:CL, 1], spec_inverses])
            pool.dma_start(se, sd[B:CHAINS]).then_inc(s("backward_moved"), 16)
            pool.wait_ge(s("backward_moved"), 16)
            link(g.tensor_tensor(gf, sd[0:B, :, 0:N], se[:, :, 0:N][:, :, ::-1], ALU.add))
            step(g.tensor_tensor(gf[:, 0], gf[:, 0], sa[0:B, 0:N], ALU.subtract))
            link(g.tensor_scalar(gf[:, 1], gf[:, 1], 1.0, 0.0, ALU.add, ALU.add))
            link(g.tensor_tensor(gt[:, 0:2], gf, gf, ALU.mult))
            g.tensor_tensor(gt[:, 2], gt[:, 0], gt[:, 1], ALU.add).then_inc(s("spec_square"), 1)
            pool.wait_ge(s("spec_inverse"), 2)
            link(g.tensor_scalar(gt[:, 1], gt[:, 0], -1.0, 0.0, ALU.mult, ALU.add))
            link(g.tensor_tensor(gf, gf, gt[:, 0:2], ALU.mult))
            g.tensor_scalar(gf, gf, 10.0, -10.0, ALU.min, ALU.max).then_inc(s("feats_ready"), 1)

        def gate_exp(act, moe, b):
            m, tiles = f"m{moe}", slice(3 * b, 3 * b + 3)
            act.wait_ge(s(m + "_gate_in"), b + 1)
            values = gtmp[:, tiles] if moe == 0 else lg[:, tiles, :]
            nc.scalar.activation(values, values, ACT.Exp).then_inc(s(m + "_gate_exp"), 1)

        def gelu(act, moe, e, par, b, c):
            m = f"m{moe}"
            unit, pair = (2 * e + b) * HC + c, (2 * e + b) * (HC // 2) + c // 2
            act.wait_ge(s(m + "_h1"), unit + 1)
            if c % 2 == 0 and not (isinstance(e, int) and pair < 3):
                act.wait_ge(s(m + "_hid_lo"), pair - 2)
            nc.scalar.activation(gelus[:, c // 2, c % 2, 0:N], P[:, (6 * b + c) % 4, 0:N],
                                 ACT.Gelu if moe == 0 else ACT.Gelu_apprx_tanh, bias=b1now[par][:, c:c + 1])\
                .then_inc(s(m + "_gelu"), 1)

        def hidden_bias(act, moe, e, par):
            nc.scalar.activation(b1now[par][:, :], b1s[:, moe, bass.ds(e, 1), :], ACT.Copy).then_inc(s(f"m{moe}_b1"), 1)
            act.wait_ge(s(f"m{moe}_b1"), e + 1)

        def moe_act(act, moe):
            m = f"m{moe}"
            if moe == 1:
                for b in range(B):
                    act.wait_ge(s("x_turned"), B * X_TURN["ffn1"] + b + 1)
                    xevacuate(act, "ffn1", b, 2 * b, None)
                for b in range(B):
                    gate_exp(act, moe, b)
                hidden_bias(act, moe, 0, 0)
                for c in range(HC):
                    gelu(act, moe, 0, 0, 0, c)
            weights_hi(act, moe, 1, 1)
            for c in range(HC):
                gelu(act, moe, 0, 0, 1, c)
            act.wait_ge(s(m + "_cwT"), 1)
            for b in range(B):
                part = slice(32 * b, 32 * b + EXPERTS)
                nc.scalar.activation(cwT[part, 0:N], P[part, 7, 0:N], ACT.Copy).then_inc(s(m + "_cwT_out"), 1)

            def expert(e, par, last):
                hidden_bias(act, moe, e, par)
                for b in range(B):
                    for c in range(HC):
                        gelu(act, moe, e, par, b, c)
                    if not last:
                        act.wait_ge(s(m + "_y"), 6 * e)
                        weights_hi(act, moe, e + 1, 1 - par, (2,) if b else (0, 1))

            expert(1, 1, False)
            with act.Fori(1, EXPERTS // 2 - 1) as i:
                for par in range(2):
                    expert(i * 2 + par, par, False)
            expert(EXPERTS - 2, 0, False)
            expert(EXPERTS - 1, 1, True)

        def weights_hi(act, moe, e, par, which=(0, 1, 2)):
            act.wait_ge(s(f"w_in{par}"), ((e // 2 if isinstance(e, int) else (e - par) // 2) + 1 + moe * (EXPERTS // 2)) * 64)
            pairs = ((w1a_hi[par][:, :], raw1[par][:, 0, :]), (w1b[par][:, :], raw1[par][:, 1, :]),
                     (w2_parts[par][:, :, 0, :], raw2[par][:, :, :]))
            for n in which:
                nc.scalar.activation(*pairs[n], ACT.Copy).then_inc(s("w_hi"), 1)

        def weights_lo(dve, moe, e, par, which=(0, 1, 2)):
            triples = ((w1a_lo[par][:, :], raw1[par][:, 0, :], w1a_hi[par][:, :]),
                       (w1b[par][64:128, :], raw1[par][64:128, 1, :], w1b[par][64:128, :]),
                       (w2_parts[par][:, :, 1, :], raw2[par][:, :, :], w2_parts[par][:, :, 0, :]))
            for n in which:
                dst, src, hi = triples[n]
                dve.wait_ge(s("w_hi"), 3 * (moe * EXPERTS + e) + n + 1)
                nc.vector.tensor_tensor(dst, src, hi.bitcast(F32), ALU.subtract).then_inc(s("w_lo"), 1)

        def gate_scores(dve, moe, b, step, settle):
            v, m = nc.vector, f"m{moe}"
            t = slice(3 * b, 3 * b + 3)
            bank, first = LOGIT_BANKS[moe][b], 24 * b
            dve.wait_ge(s(m + "_logits"), b + 1)
            dve.wait_ge(s("pads_zeroed"), 5)
            full = P[:, bank, first:first + 16].rearrange("p (t e) -> p t e", e=EXPERTS)
            v.tensor_tensor(lg[:, 3 * b:3 * b + 2, :], full, gate_rows[:, moe, :].unsqueeze(1).broadcast_to([128, 2, EXPERTS]), ALU.add)\
                .then_inc(s(m + "_logits_out"), 1)
            v.tensor_tensor(lg[0:TXT, 3 * b + 2, :], P[0:TXT, bank, first + 16:first + 24], gate_rows[0:TXT, moe, :], ALU.add)\
                .then_inc(s(m + "_logits_out"), 1)
            dve.wait_ge(s(m + "_logits_out"), 2 * (b + 1))
            if moe == 0:
                for i in IMAGE[b]:
                    step(v.max(m8[:, i, :], lg[:, i, :]))
                settle()
                v.tensor_tensor(gtmp[:, t], m8[:, t, 1], m8[:, t, 0], ALU.subtract).then_inc(s(m + "_gate_in"), 1)
            else:
                step(v.tensor_reduce(gtmp[:, t], lg[:, t, :], AX.X, ALU.max))
                settle()
                v.tensor_tensor(lg[:, t, :], lg[:, t, :], gtmp[:, t].unsqueeze(2).broadcast_to([128, 3, 8]), ALU.subtract)\
                    .then_inc(s(m + "_gate_in"), 1)

        def gate_weights(dve, moe, b, step, settle):
            v, m = nc.vector, f"m{moe}"
            t = slice(3 * b, 3 * b + 3)
            wide = lambda ap: ap.broadcast_to([128, 3, EXPERTS])
            if moe == 1:
                dve.wait_ge(s(m + "_gate_exp"), b + 1)
                step(v.tensor_reduce(gtmp[:, t], lg[:, t, :], AX.X, ALU.add))
                settle()
                step(v.reciprocal(gtmp[:, t], gtmp[:, t]))
                settle()
                step(v.tensor_tensor(lg[:, t, :], lg[:, t, :], wide(gtmp[:, t].unsqueeze(2)), ALU.mult))
                settle()
                for i in IMAGE[b]:
                    step(v.max(m8[:, i, :], lg[:, i, :]))
                settle()
            for i in IMAGE[b]:
                step(v.max_index(i8[:, i, :], m8[:, i, :], lg[:, i, :]))
            settle()
            step(v.tensor_copy(idf[:, t, :], i8[:, t, 0:2]))
            if moe == 0:
                dve.wait_ge(s(m + "_gate_exp"), b + 1)
                step(v.tensor_scalar(s01[:, t, 0], gtmp[:, t], 1.0, None, ALU.add))
                settle()
                step(v.reciprocal(s01[:, t, 0], s01[:, t, 0]))
                settle()
                step(v.tensor_tensor(s01[:, t, 1], s01[:, t, 0], gtmp[:, t], ALU.mult))
            else:
                step(v.tensor_tensor(gtmp[:, t], m8[:, t, 0], m8[:, t, 1], ALU.add))
                settle()
                step(v.reciprocal(gtmp[:, t], gtmp[:, t]))
                settle()
                step(v.tensor_tensor(s01[:, t, :], m8[:, t, 0:2], gtmp[:, t].unsqueeze(2).broadcast_to([128, 3, 2]), ALU.mult))
            numbers = wide(gate_rows[:, 2, :].unsqueeze(1))
            step(v.tensor_tensor(cwA[:, t, :], numbers, wide(idf[:, t, 0:1]), ALU.is_equal))
            step(v.tensor_tensor(cw[:, t, 0:EXPERTS], numbers, wide(idf[:, t, 1:2]), ALU.is_equal))
            settle()
            step(v.tensor_tensor(cwA[:, t, :], cwA[:, t, :], wide(s01[:, t, 0:1]), ALU.mult))
            step(v.tensor_tensor(cw[:, t, 0:EXPERTS], cw[:, t, 0:EXPERTS], wide(s01[:, t, 1:2]), ALU.mult))
            settle()
            v.tensor_tensor(cw[:, t, 0:EXPERTS], cw[:, t, 0:EXPERTS], cwA[:, t, :], ALU.add).then_inc(s(m + "_cw"), 1)

        def hidden_parts(dve, moe, e, b, q):
            m = f"m{moe}"
            pair = (2 * e + b) * (HC // 2) + q
            src, dst_hi = gelus[:, q, :, 0:N], hid_hi[b][:, 2 * q:2 * q + 2, 0:N]
            dve.wait_ge(s(m + "_gelu"), 2 * pair + 2)
            nc.vector.tensor_copy(dst_hi, src).then_inc(s(m + "_hid_hi"), 1)
            dve.wait_ge(s(m + "_hid_hi"), pair + 1)
            nc.vector.tensor_tensor(hid_lo[b][:, 2 * q:2 * q + 2, 0:N], src, dst_hi.bitcast(F32), ALU.subtract)\
                .then_inc(s(m + "_hid_lo"), 1)

        def moe_vector(dve, moe, before_last):
            v = nc.vector
            m = f"m{moe}"

            def add_up(e, par, b):
                for j in range(3):
                    i, r, n = b * 3 + j, ROWS[j], 6 * e + 3 * b + j
                    dve.wait_ge(s(m + "_y"), n + 1)
                    if not (isinstance(e, int) and n < 3):
                        dve.wait_ge(s(m + "_acc"), n + 4 if isinstance(e, int) and n < 6 else n + 1)
                    scale = cw[0:r, i, e:e + 1] if isinstance(e, int) else cw[0:r, i, bass.ds(e, 1)]
                    both = sums[0:r, i, :, :]
                    v.scalar_tensor_tensor(both, P[0:r, output_bank(e, par, i), 0:2 * C].rearrange("p (z c) -> p z c", z=2), scale, both,
                                           ALU.mult, ALU.add).then_inc(s(m + "_acc"), 1)

            def expert(e, par, last):
                for b in range(B):
                    if moe == 1 and isinstance(e, int) and (e, b) == (EXPERTS - 2, 0):
                        dve.wait_ge(s("spec_square"), 1)
                        v.reciprocal(spec_inverses, spec_squares).then_inc(s("spec_inverse"), 1)
                    for q in range(HC // 2):
                        hidden_parts(dve, moe, e, b, q)
                    if moe == 1 and isinstance(e, int) and (e, b) == (EXPERTS - 1, 0):
                        dve.wait_ge(s("spec_square"), 2)
                        v.reciprocal(gt[:, 0], gt[:, 2]).then_inc(s("spec_inverse"), 1)
                    if b == 1:
                        if not last:
                            weights_lo(dve, moe, e + 1, 1 - par, (2,))
                        add_up(e, par, 0)
                    else:
                        add_up(e - 1, 1 - par, 1)
                        if not last:
                            weights_lo(dve, moe, e + 1, 1 - par, (0, 1))

            dve.wait_ge(s(m + "_cw"), 1)
            dve.wait_ge(s("sums_zeroed"), moe + 1)
            add_up(0, 0, 0)
            weights_lo(dve, moe, 1, 1)
            for q in range(HC // 2):
                hidden_parts(dve, moe, 0, 1, q)
            dve.wait_ge(s(m + "_acc"), 3)
            for i in range(NT):
                r = ROWS[i % 3]
                dve.wait_ge(s(m + "_b2"), i + 1)
                v.tensor_tensor(x2[0:r, i, :], x2[0:r, i, :], P[0:r, 4 + (i + 3) % 4, 0:C], ALU.add).then_inc(s(m + "_acc"), 1)
            expert(1, 1, False)
            with dve.Fori(1, EXPERTS // 2 - 1) as i2:
                for par in range(2):
                    expert(i2 * 2 + par, par, False)
            expert(EXPERTS - 2, 0, False)
            expert(EXPERTS - 1, 1, True)
            dve.wait_ge(s(m + "_acc"), NT * (EXPERTS + 1) - 3)
            before_last()
            add_up(EXPERTS - 1, 1, 1)
            dve.wait_ge(s(m + "_acc"), NT * (EXPERTS + 1))

        def output_bank(e, par, i):
            return 4 + i if isinstance(e, int) and e == 0 and i < 3 else 4 + (6 * par + i + 2) % 4

        def hidden(pe, moe, e, par, b, chunks=range(HC)):
            m = f"m{moe}"
            cols = slice(b * NP, (b + 1) * NP)
            if b == 0:
                pe.wait_ge(s("w_lo"), 3 * (moe * EXPERTS + e) + 2)
            for c in chunks:
                unit = (2 * e + b) * HC + c
                if not (isinstance(e, int) and unit < 4):
                    pe.wait_ge(s(m + "_gelu"), unit - 3)
                f = slice(c * 128, (c + 1) * 128)
                terms = ((w1a_hi, x_hi, 0), (w1a_hi, x_lo, 0), (w1a_lo, x_hi, 0), (w1b, x_hi, 1), (w1b, x_lo, 1))
                for n, (w, x_, k) in enumerate(terms):
                    last = nc.tensor.matmul(P[:, (6 * b + c) % 4, 0:NP], w[par][:, f], x_[:, k, cols], start=(n == 0), stop=(n == 4))
                last.then_inc(s(m + "_h1"), 1)

        def gate_logits(pe, moe, b):
            pe.wait_ge(s("xf"), 2 * B * X_TURN["ffn1" if moe else "ln2"] + 2 * (b + 1))
            for i in IMAGE[b]:
                r = ROWS[i % 3]
                for p, k in ((slice(0, 128), 0), (slice(0, 64), 1)):
                    last = nc.tensor.matmul(P[0:r, LOGIT_BANKS[moe][b], i * 8:i * 8 + 8], xf[p, k, col(i):col(i) + r],
                                            wgate[p, k, 8 * moe:8 * moe + 8], start=(k == 0), stop=(k == 1))
            last.then_inc(s(f"m{moe}_logits"), 1)

        def moe_tensor(pe, moe):
            mm = nc.tensor.matmul
            m = f"m{moe}"

            def outputs(e, par, b):
                if b == 0:
                    pe.wait_ge(s("w_lo"), 3 * (moe * EXPERTS + e + 1))
                for j in range(3):
                    r = ROWS[j]
                    n = (2 * e + b) * 3 + j
                    if not (isinstance(e, int) and n < 3):
                        pe.wait_ge(s(m + "_acc"), n + 3)
                    tok = slice(j * 128, j * 128 + r)
                    for c in range(HC):
                        if j == 0 and c % 2 == 0:
                            pe.wait_ge(s(m + "_hid_lo"), (2 * e + b) * (HC // 2) + c // 2 + 1)
                        products = [(hid_hi, 2 * C), (hid_lo, C)]
                        if c == HC - 1:
                            products.reverse()
                        for hid, n_cols in products:
                            last = mm(P[0:r, output_bank(e, par, 3 * b + j), 0:n_cols], hid[b][:, c, tok],
                                      w2_parts[par][:, c, :, :].rearrange("p z c -> p (z c)")[:, 0:n_cols],
                                      start=(c == 0 and hid is hid_hi), stop=(c == HC - 1 and hid is hid_hi))
                    last.then_inc(s(m + "_y"), 1)

            def expert(e, par):
                hidden(pe, moe, e, par, 0)
                outputs(e - 1, 1 - par, 1)
                hidden(pe, moe, e, par, 1)
                outputs(e, par, 0)

            if moe == 0:
                outputs(0, 0, 0)
                pe.wait_ge(s("m0_gelu"), 4)
                xturn(pe, "ln2_1", IMAGE[1], 2)
                gate_logits(pe, moe, 1)
            else:
                pe.wait_ge(s("sa_ready"), 1)
                outputs(0, 0, 0)
            pe.wait_ge(s("x_lo"), B * (X_TURN["ffn1" if moe else "ln2"] + 1))
            pe.wait_ge(s("x_hi"), 2 * B * (X_TURN["ffn1" if moe else "ln2"] + 1))
            hidden(pe, moe, 0, 0, 1)
            pe.wait_ge(s(m + "_cw"), B)
            for i in range(NT):
                r, b = ROWS[i % 3], i // 3
                last = mm(P[32 * b:32 * b + 32, 7, (i % 3) * 128:(i % 3) * 128 + r], cw[0:r, i, :], ident[0:r, 0:r],
                          start=True, stop=True)
            last.then_inc(s(m + "_cwT"), 1)
            hidden(pe, moe, 1, 1, 0)
            pe.wait_ge(s(m + "_cwT_out"), B)
            for i in range(NT):
                r, part = ROWS[i % 3], slice(32 * (i // 3), 32 * (i // 3) + EXPERTS)
                if i >= 1:
                    pe.wait_ge(s(m + "_acc"), i)
                mm(P[0:r, 4 + (i + 3) % 4, 0:C], cwT[part, (i % 3) * 128:(i % 3) * 128 + r], b2s[part, moe, :],
                   start=True, stop=True)\
                    .then_inc(s(m + "_b2"), 1)
            outputs(0, 0, 1)
            hidden(pe, moe, 1, 1, 1)
            outputs(1, 1, 0)
            with pe.Fori(1, EXPERTS // 2) as e2:
                for par in range(2):
                    expert(e2 * 2 + par, par)
            if moe == 1:
                pe.wait_ge(s("feats_ready"), 1)
                pe.wait_ge(s("m1_gelu"), 2 * EXPERTS * HC)
                for i in range(NT):
                    r = ROWS[i % 3]
                    for z in range(2):
                        last = mm(P[0:r, i // 2, i % 2 * C:(i % 2 + 1) * C], gf[:, z, (i % 3) * 128:(i % 3) * 128 + r],
                                  outw_rows[:, z, i // 3, :], start=(z == 0), stop=(z == 1))
                    last.then_inc(s("spec_o"), 1)
            outputs(EXPERTS - 1, 1, 1)

        @block.sync
        def _(sp):
            pat = a["patches"].rearrange("(c p) n -> p c n", p=128)
            cwv = a["conv_w"].rearrange("(c p) n -> p c n", p=128)
            for g in range(4):
                sp.dma_start(convw[:, 4 * g:4 * g + 4, :], cwv[:, 4 * g:4 * g + 4, :]).then_inc(s(f"patches_in{g}"), 16)
                sp.dma_start(patches[:, 4 * g:4 * g + 4, :], pat[:, 4 * g:4 * g + 4, :]).then_inc(s(f"patches_in{g}"), 16)
            for n, (dst, name, pat_) in enumerate([
                    (wqkv[:, :, :], "qkv_w", "l p n -> p l n"), (wout[:, :, :, :], "out_w", "l (q p) n -> p l q n"),
                    (wff1[:, :, :], "ff1_w", "l p n -> p l n"), (wff2[:, :, :, :], "ff2_w", "l (q p) n -> p l q n")]):
                kw = {"p": 128} if "q" in pat_ else {}
                src = a[name].rearrange(pat_, **kw)
                if n in (1, 3):
                    for l in range(LAYERS):
                        sp.dma_start(dst[:, l, :, :], src[:, l, :, :]).then_inc(s("tok_weights_in"), 16)
                else:
                    sp.dma_start(dst, src).then_inc(s("qkv_weights_in" if n == 0 else "tok_weights_in"), 16)
            sp.dma_start(whead[:, :], a["head_w"]).then_inc(s("tok_weights_in"), 16)
            sp.dma_start(wret[:, :, :], a["ret_w"].rearrange("(k p) n -> p k n", p=CH)).then_inc(s("weights_in"), 16)
            sp.dma_start(wgate[:, :, :], a["gate_w"]).then_inc(s("weights_in"), 16)
            sp.wait_ge(s("conv"), B)
            for m in range(2):
                dst = wq_raw[:, :, m * PAIRS * 128:(m + 1) * PAIRS * 128]
                for part, k, src in ((slice(0, 128), 0, slice(0, 128)), (slice(0, 64), 1, slice(128, C)), (slice(64, 128), 1, slice(128, C))):
                    sp.dma_start(dst[part, k, :], a["qk_w"][m, src]).then_inc(s("qk_weights_in"), 16)
            sp.wait_ge(s("head"), 4)
            sp.dma_start(decay, a["decay"]).then_inc(s("decay_in"), 16)
            sp.wait_ge(s("selr_set"), 1)
            sp.dma_start(wva[:, :, :], a["v_w"]).then_inc(s("attention_weights_in"), 16)
            for dst, name in ((wpa, "proj_w"), (w1q, "q1_w"), (w1kv, "kv1_w")):
                sp.dma_start(dst[:, :, :], a[name].rearrange("(k p) n -> p k n", p=CH)).then_inc(s("attention_weights_in"), 16)
            sp.dma_start(w1p[:, :, :], a["proj1_w"]).then_inc(s("attention_weights_in"), 16)
            for moe in range(2):
                for e in range(EXPERTS):
                    par, turn = e % 2, moe * EXPERTS + e
                    if turn >= 2:
                        sp.wait_ge(s("w_lo"), 3 * (turn - 1))
                    w1v = a["w1"][moe, e]
                    for dst, src in ((raw1[par][:, 0, :], w1v[0:128]), (raw1[par][0:64, 1, :], w1v[128:C]),
                                     (raw1[par][64:128, 1, :], w1v[128:C]),
                                     (raw2[par][:, :, :], a["w2"][moe, e].rearrange("(k p) n -> p k n", p=128))):
                        sp.dma_start(dst, src).then_inc(s(f"w_in{par}"), 16)
            ov = out
            for b in range(B):
                for j in range(3):
                    sp.wait_ge(s("out_ready"), b * 3 + j + 1)
                    sp.dma_start(ov[b, j * 128:j * 128 + ROWS[j], :], h[0:ROWS[j], b * 3 + j, :]).then_inc(s("out_stored"), 16)
            sp.wait_ge(s("out_stored"), 16 * NT)

        @block.gpsimd
        def _(pool):
            nc.gpsimd.memset(neghalf[:, :], -0.5).then_inc(s("neghalf_set"), 1)
            nc.gpsimd.memset(h[:, :, :], 0.0).then_inc(s("h_zeroed"), 1)
            nc.gpsimd.memset(bd[:, :, :, :], 0.0).then_inc(s("bd_zeroed"), 1)
            nc.gpsimd.memset(tT[:, :, :], 0.0).then_inc(s("pads_zeroed"), 1)
            nc.gpsimd.memset(mx[:, :, :, :], 0.0).then_inc(s("pads_zeroed"), 1)
            nc.gpsimd.memset(yn[:, :, :], 0.0).then_inc(s("pads_zeroed"), 1)
            nc.gpsimd.memset(lg[:, :, :], 0.0).then_inc(s("pads_zeroed"), 1)
            nc.gpsimd.memset(cw[:, :, :], 0.0).then_inc(s("pads_zeroed"), 1)
            pool.wait_ge(s("neghalf_set"), 1)
            for tag, _ in LN_TAGS:
                if tag.startswith("t"):
                    prstd(pool, tag)
                if tag == "t0ln1_1":
                    pool.wait_ge(s("consts_in"), 16 * 9)
                    nc.gpsimd.tensor_copy(selr[:, :, :], selw[:, :, :]).then_inc(s("selr_set"), 1)
                    pool.wait_ge(s("selr_set"), 1)
            nc.gpsimd.memset(xf[:, :, N::NP], 0.0).then_inc(s("xf_zeroed"), 1)
            pool.wait_ge(s("xf_zeroed"), 1)
            nc.gpsimd.tensor_copy(x_hi[:, :, N::NP], xf[:, :, N::NP]).then_inc(s("xf_zeroed"), 1)
            pool.wait_ge(s("xf_zeroed"), 2)
            for tag in ("ret_0", "ret_1", "ffn0_0", "ln1_0", "ffn0_1", "ln1_1"):
                prstd(pool, tag)
            pool.wait_ge(s("ret_o"), NT)
            nc.gpsimd.memset(vaug, 0.0).then_inc(s("vaug_zeroed"), 1)
            pool.wait_ge(s("vaug_zeroed"), 1)
            nc.gpsimd.memset(vaug[:, :, :, HD:HD + 1], 1.0).then_inc(s("vaug_ones"), 1)
            nc.gpsimd.memset(sums[:, :, 1, :], 0.0).then_inc(s("sums_zeroed"), 1)
            for tag in ("ln2_0", "ln2_1", "att1_0", "att1_1", "ffn1_0", "ffn1_1"):
                prstd(pool, tag)
                if tag == "att1_1":
                    pool.wait_ge(s("m0_y"), NT * EXPERTS)
                    nc.gpsimd.memset(at, 0.0).then_inc(s("at_zeroed"), 1)
                    pad_columns = atS.rearrange("p b g h q d -> p (b g h q) d")[:, :, HD1:32]
                    nc.gpsimd.tensor_copy(pad_columns, xf[:, 0, N:NP].unsqueeze(1).broadcast_to([128, B * G1 * HG * 4, 32 - HD1]))\
                        .then_inc(s("at_zeroed"), 1)
                    pool.wait_ge(s("mixed_in"), B)
                    nc.gpsimd.memset(sums[:, :, 1, :], 0.0).then_inc(s("sums_zeroed"), 1)
            nc.gpsimd.memset(sa[:, N:SL], 0.0).then_inc(s("sa_zeroed"), 1)
            spectral(pool)

        @block.scalar
        def _(act):
            one = lambda x: x.rearrange("(o n) -> o n", o=1)
            for dst, src in ((tokrows[:, :, :], a["tok_rows"].partition_broadcast(128)), (ident[:, :], a["ident"]),
                             (tokcols[:, :], a["tok_cols"]), (ff1b[:, :], a["ff1_b"])):
                act.dma_start(dst, src).then_inc(s("tok_consts_in"), 16)
            act.wait_ge(s("h_zeroed"), 1)
            for b in range(B):
                act.dma_start(h[0:TXT, b * 3 + 2, :], a["txt"][b]).then_inc(s("txt_in"), 16)
            for dst, src in ((chcols[:, :], a["ch_cols"]), (signs[:, :], a["signs"]), (mcols[:, :], a["mix_cols"]),
                             (selw[:, :, :], a["sel"]), (rows[:, :, :], a["rows"].partition_broadcast(128)),
                             (gate_rows[:, :, :], a["gate_rows"].partition_broadcast(128)),
                             (b1s[:, :, :, :], a["b1"]), (b2s[0:EXPERTS, :, :], a["b2"].rearrange("m e c -> e m c")),
                             (b2s[32:32 + EXPERTS, :, :], a["b2"].rearrange("m e c -> e m c"))):
                act.dma_start(dst, src).then_inc(s("consts_in"), 16)
            act.dma_start(gmask[:, :, :], a["gmask"]).then_inc(s("late_in"), 16)
            act.dma_start(outw_rows[:, :, :, :], a["outw_rows"]).then_inc(s("late_in"), 16)
            act.wait_ge(s("tok_consts_in"), 16 * 4)

            def tok_y(turn, column, b):
                act.wait_ge(s("tok_turned"), turn * B + b + 1)
                nc.scalar.activation(yT[:, b * TOK:(b + 1) * TOK], P[:, 4 * b + 3, 0:TOK], ACT.Identity,
                                     bias=tokcols[:, column + 1:column + 2], scale=tokcols[:, column:column + 1]).then_inc(s("tok_y"), 1)

            def tok_exps(l, b):
                n = l * B + b
                for q in range(4):
                    act.wait_ge(s("tok_kmax"), 2 * n + q // 2 + 1)
                    nc.scalar.activation(ke[:, q, b * TOK:(b + 1) * TOK], P[:, 4 * b + q // 2, q % 2 * TOK:(q % 2 + 1) * TOK], ACT.Exp,
                                         bias=kmax[:, q, b:b + 1], accum_out=ksum[:, q, b:b + 1]).then_inc(s("tok_kexp"), 1)
                for i in range(2):
                    act.wait_ge(s("tok_qsub"), 2 * n + i + 1)
                    nc.scalar.activation(qs[:, 2 * b + i, :], qs[:, 2 * b + i, :], ACT.Exp).then_inc(s("tok_qexp"), 1)

            def tok_out(l, b):
                n = l * B + b
                for i in range(2):
                    act.wait_ge(s("tok_v"), 2 * n + i + 1)
                    nc.scalar.activation(vt[:, 2 * b + i, :], P[:, 4 * b + 2 + i, :], ACT.Copy).then_inc(s("tok_vout"), 1)
                for i in range(2):
                    act.wait_ge(s("tok_kturned"), 2 * n + i + 1)
                    nc.scalar.activation(kt[:, 2 * b + i, :], P[:, 4 * b + i, :], ACT.Copy).then_inc(s("tok_kt"), 1)
                for i in range(2):
                    act.wait_ge(s("tok_qturned"), 2 * n + i + 1)
                    nc.scalar.activation(qT[:, :, (2 * b + i) * 128:(2 * b + i + 1) * 128],
                                         P[:, 4 * b + 2 + i, :].rearrange("p (c n) -> p c n", c=4), ACT.Identity,
                                         scale=DH ** -0.5).then_inc(s("tok_qT"), 1)

            def tok_gelu(l, b):
                n = l * B + b
                for q in range(4):
                    act.wait_ge(s("tok_ff1"), 2 * n + q // 2 + 1)
                    nc.scalar.activation(hT[:, q, b * TOK:(b + 1) * TOK], P[:, 4 * b + q // 2, q % 2 * TOK:(q % 2 + 1) * TOK], ACT.Gelu,
                                         bias=ff1b[:, 4 * l + q:4 * l + q + 1]).then_inc(s("tok_gelu"), 1)

            for l in range(LAYERS):
                for b in range(B):
                    tok_y(2 * l, 4 * l, b)
                for b in range(B):
                    tok_exps(l, b)
                for b in range(B):
                    tok_out(l, b)
                for b in range(B):
                    tok_y(2 * l + 1, 4 * l + 2, b)
                    tok_gelu(l, b)
            for b in range(B):
                tok_y(2 * LAYERS, 4 * LAYERS, b)
            act.wait_ge(s("consts_in"), 16 * 9)
            act.wait_ge(s("pads_zeroed"), 5)
            aevacuate(act, "ret", (0,))
            for b in range(B):
                for m in range(4):
                    u = 4 * b + m
                    act.wait_ge(s("ret_qk"), u + 1)
                    nc.scalar.activation(qkT[:, m, b * NP:b * NP + N], P[0:CH, 4 + u % 2, 0:N], ACT.Identity,
                                         bias=chcols[:, m:m + 1]).then_inc(s("ret_qk_out"), 1)
                if b == 0:
                    aevacuate(act, "ret", (1,))
                    act.wait_ge(s("qk_weights_in"), 16 * 6)
                    nc.scalar.activation(wq_hi, wq_raw[:, 0, :], ACT.Copy).then_inc(s("wq_hi"), 1)
                    nc.scalar.activation(wq_b, wq_raw[:, 1, :], ACT.Copy).then_inc(s("wq_hi"), 1)
            act.wait_ge(s("xf_zeroed"), 2)
            act.wait_ge(s("x_turned"), 1)
            xevacuate(act, "ln1", 0, 0, 0)

            def q_high(u):
                act.wait_ge(s("q_stack"), u + 1)
                if u >= 2:
                    act.wait_ge(s("q_lo"), u - 1)
                nc.scalar.activation(qhi[:, u % 2, :], P[:, stack_bank(u), 0:NP], ACT.Identity,
                                     scale=signs[:, 0:1]).then_inc(s("q_hi"), 1)

            def k_high(u):
                act.wait_ge(s("k_stack"), u + 1)
                if u >= 2:
                    act.wait_ge(s("k_lo"), u - 1)
                nc.scalar.activation(khi[:, u % 2, :], P[:, stack_bank(u) + 1, 0:NP], ACT.Copy).then_inc(s("k_hi"), 1)

            def max_out(b):
                act.wait_ge(s("att_maxT"), b + 1)
                nc.scalar.activation(mxT[:, b, 0:N], P[0:HEADS, 7 if b == 0 else 0, 0:N], ACT.Copy).then_inc(s("att_max_out"), 1)
                nc.scalar.activation(mxT[:, b, N:NP], ident[0:HEADS, 127:128], ACT.Copy).then_inc(s("att_max_out"), 1)

            q_high(0)
            k_high(0)
            q_high(1)
            k_high(1)
            for u in range(PAIRS):
                if u + 2 <= PAIRS:
                    q_high(u + 2)
                    k_high(u + 2)
                if u == 1:
                    act.wait_ge(s("x_half_turned"), 1)
                    xevacuate(act, "ln1", 1, 7, 0, (0,))
                    act.wait_ge(s("x_turned"), 2)
                    xevacuate(act, "ln1", 1, 6, 0, (1,))
                if 2 <= u <= 4:
                    act.wait_ge(s("vaug_ones"), 1)
                    for i in (2 * u - 4, 2 * u - 3):
                        act.wait_ge(s("att_v"), i + 1)
                        r = ROWS[i % 3]
                        nc.scalar.activation(vaug[0:r, i, :, 0:HD], P[0:r, 7, 0:C].rearrange("p (h d) -> p h d", d=HD), ACT.Copy)\
                            .then_inc(s("att_v_out"), 1)
                    weights_hi(act, 0, 0, 0, (u - 2,))
            max_out(0)
            for b in range(B):
                if b == 1:
                    max_out(1)
                for t in range(3 * HEADS):
                    u = b * 3 * HEADS + t
                    r = ROWS[t % 3]
                    act.wait_ge(s("att_scoresT"), u + 1)
                    if u >= 6:
                        act.wait_ge(s("att_pv"), u - 5)
                    nc.scalar.activation(pt[0:r, u % 6, :], P[0:r, 4 + u % 2, 0:N], ACT.Exp).then_inc(s("att_exp"), 1)
                    if b == 0 and t % 6 == 2 and t < 3 * HEADS - 6:
                        q_high(PAIRS + t // 6 + 1)
                    if b == 0 and t % 6 == 3 and t < 3 * HEADS - 6:
                        k_high(PAIRS + t // 6 + 1)
                    if b == 1 and t == TURN_AT + 1:
                        aevacuate(act, "proj", (0,))
                    if b == 1 and t == MIX_AT + 1:
                        act.wait_ge(s("x_turned"), B * X_TURN["ln2"] + 1)
                        xevacuate(act, "ln2", 0, 0, 4)
                    if b == 1 and t == GATE_AT + 5:
                        gate_exp(act, 0, 0)
                    if t % 12 == 11:
                        grp = u // 12
                        act.wait_ge(s("att_pv"), u + 1)
                        if grp >= 3:
                            act.wait_ge(s("att_o_turned"), 3 * (grp - 2))
                        nc.scalar.activation(ao[:, grp % 3, :], P[:, 6, 0:N], ACT.Copy).then_inc(s("att_ao"), 1)
            hidden_bias(act, 0, 0, 0)
            gelu(act, 0, 0, 0, 0, 0)
            gelu(act, 0, 0, 0, 0, 1)
            aevacuate(act, "proj", (1,))
            for c in range(2, HC):
                gelu(act, 0, 0, 0, 0, c)
            act.wait_ge(s("x_turned"), B * X_TURN["ln2"] + 2)
            xevacuate(act, "ln2", 1, 2, 4)
            gate_exp(act, 0, 1)
            moe_act(act, 0)
            weights_hi(act, 1, 0, 0)
            def key_values(b):
                for i in IMAGE[b]:
                    act.wait_ge(s("kv1"), i + 1)
                    r = ROWS[i % 3]
                    nc.scalar.activation(kv[0:r, i, :], P[0:r, 4 + i % 3, 0:2 * C], ACT.Copy).then_inc(s("kv1_out"), 1)

            def queries(b):
                for g in range(G1):
                    act.wait_ge(s("q1"), G1 * b + g + 1)
                    nc.scalar.activation(q1s[:, g, b * NP:(b + 1) * NP], P[:, 2 + g, 0:NP], ACT.Copy).then_inc(s("q1_hi"), 1)

            def context_exp(b):
                act.wait_ge(s("ctx_sub"), b + 1)
                c = cc[:, 2 * b:2 * b + 2, :]
                nc.scalar.activation(c, c, ACT.Exp, scale=float(HD1) ** -0.5).then_inc(s("ctx_exp"), 1)

            def heads(b):
                for u in range(8 * b, 8 * b + 8, 2):
                    act.wait_ge(s("heads1"), u + 1)
                    for quarter in range(4):
                        dst, src = reshuffled(u, quarter)
                        last = nc.scalar.activation(dst, src, ACT.Copy)
                    last.then_inc(s("heads1_even"), 1)

            aevacuate(act, "att1", (0,))
            queries(0)
            key_values(0)
            aevacuate(act, "att1", (1,))
            key_values(1)
            context_exp(0)
            queries(1)
            context_exp(1)
            heads(0)
            heads(1)
            moe_act(act, 1)

        @block.vector
        def _(dve):
            count = [0]

            def step(ins):
                count[0] += 1
                ins.then_inc(s("dve_step"), 1)

            def settle():
                dve.wait_ge(s("dve_step"), count[0])

            def link(ins):
                step(ins)
                settle()

            v = nc.vector
            dve.wait_ge(s("tok_consts_in"), 16 * 4)
            dve.wait_ge(s("pads_zeroed"), 5)
            def tok_normalise(tag, b, row=None):
                layernorm(dve, f"{tag}_{b}", ynt, xt)
                if row is not None:
                    dve.wait_ge(s("ln_norm"), LN_BASE[f"{tag}_{b}"] + 2)
                    step(v.tensor_tensor(xt[:, 3 * b:3 * b + 2, :], xt[:, 3 * b:3 * b + 2, :],
                                         tokrows[:, row, :].unsqueeze(1).broadcast_to([128, 2, D]), ALU.add))

            def tok_add(name, l, b, bank):
                settle()
                dve.wait_ge(s(name), l * B + b + 1)
                link(v.tensor_tensor(xt[:, 3 * b:3 * b + 2, :], xt[:, 3 * b:3 * b + 2, :],
                                     P[:, bank, 0:2 * D].rearrange("p (t d) -> p t d", t=2), ALU.add))

            def tok_maxima(l, b):
                n = l * B + b
                for m in range(2):
                    dve.wait_ge(s("tok_k"), 2 * n + m + 1)
                    link(v.tensor_reduce(kmax[:, 2 * m:2 * m + 2, b], P[:, 4 * b + m, :].rearrange("p (q n) -> p q n", q=2), AX.X, ALU.max))
                    v.tensor_scalar(kmax[:, 2 * m:2 * m + 2, b], kmax[:, 2 * m:2 * m + 2, b], -1.0, None, ALU.mult).then_inc(s("tok_kmax"), 1)
                for i in range(2):
                    dve.wait_ge(s("tok_q"), 2 * n + i + 1)
                    seg = P[:, 4 * b + 2 + i, :].rearrange("p (h d) -> p h d", d=DH)
                    t = 2 * b + i
                    link(v.tensor_reduce(segmax[:, t, :], seg, AX.X, ALU.max))
                    v.tensor_tensor(qs[:, t, :].rearrange("p (h d) -> p h d", d=DH), seg,
                                    segmax[:, t, :].unsqueeze(2).broadcast_to([128, 8, DH]), ALU.subtract).then_inc(s("tok_qsub"), 1)

            def tok_softmax(l, b):
                n = l * B + b
                segs = [qs[:, 2 * b + i, :].rearrange("p (h d) -> p h d", d=DH) for i in range(2)]
                for i in range(2):
                    dve.wait_ge(s("tok_qexp"), 2 * n + i + 1)
                    step(v.tensor_reduce(segsum[:, 2 * b + i, :], segs[i], AX.X, ALU.add))
                settle()
                link(v.reciprocal(segsum[:, 2 * b:2 * b + 2, :], segsum[:, 2 * b:2 * b + 2, :]))
                for i in range(2):
                    v.tensor_tensor(segs[i], segs[i], segsum[:, 2 * b + i, :].unsqueeze(2).broadcast_to([128, 8, DH]), ALU.mult)\
                        .then_inc(s("tok_qsoft"), 1)
                dve.wait_ge(s("tok_kexp"), 4 * n + 4)
                step(v.reciprocal(ksum[:, :, b], ksum[:, :, b]))

            def tok_context(l, b):
                n = l * B + b
                dve.wait_ge(s("tok_ctx"), n + 1)
                if n == 0:
                    dve.wait_ge(s("bd_zeroed"), 1)
                for z in range(2):
                    r = slice(64 * z, 64 * z + 64)
                    v.tensor_copy(bd[r, b, :, 64 * z:64 * z + 64],
                                  P[r, 4 * b, :].rearrange("p (q d) -> p q d", q=4)[:, :, 64 * z:64 * z + 64]).then_inc(s("tok_bd"), 1)
                settle()
                dve.wait_ge(s("tok_w2"), n + 1)
                v.tensor_tensor(w2[:, b, :, :], P[:, 4 * b + 1, :].rearrange("p (q d) -> p q d", q=4),
                                ksum[:, :, b].unsqueeze(2).broadcast_to([128, 4, D]), ALU.mult).then_inc(s("tok_w2_out"), 1)

            for b in range(B):
                dve.wait_ge(s("conv"), b + 1)
                link(v.tensor_tensor(xt[:, 3 * b:3 * b + 2, :], P[:, 4 * b:4 * b + 2, 0:D],
                                     tokrows[:, 0, :].unsqueeze(1).broadcast_to([128, 2, D]), ALU.add))
                tok_normalise("t0ln1", b, 1)
            for l in range(LAYERS):
                for b in range(B):
                    tok_maxima(l, b)
                for b in range(B):
                    tok_softmax(l, b)
                for b in range(B):
                    tok_context(l, b)
                    tok_add("tok_att", l, b, 4 * b)
                    tok_normalise(f"t{l}ln2", b, 3 + l)
                for b in range(B):
                    tok_add("tok_ff2", l, b, 4 * b + 2)
                    if l + 1 < LAYERS:
                        tok_normalise(f"t{l + 1}ln1", b, 2 + l)
                    else:
                        tok_normalise("tlnf", b)
            dve.wait_ge(s("h_zeroed"), 1)
            dve.wait_ge(s("consts_in"), 16 * 9)
            dve.wait_ge(s("txt_in"), 32)

            for b in range(B):
                for i in range(2):
                    dve.wait_ge(s("head"), 2 * b + i + 1)
                    v.tensor_tensor(h[:, 3 * b + i, :], P[:, 4 * b + i, 0:C], rows[:, 0, :], ALU.add).then_inc(s("head_out"), 1)
                dve.wait_ge(s("head_out"), 2 * (b + 1))
                layernorm(dve, f"ret_{b}", yn, h)

            def ret_values(b):
                for i in IMAGE[b]:
                    dve.wait_ge(s("ret_v"), i + 1)
                    r = ROWS[i % 3]
                    v.tensor_tensor(vtok[0:r, i, :], P[0:r, 2 + i % 3 % 2, 0:C], rows[0:r, 1, :], ALU.add).then_inc(s("ret_vo_out"), 1)

            def ret_decayed(b):
                dve.wait_ge(s("decay_in"), 16)
                for j in range(3):
                    u, r = b * 3 + j, ROWS[j]
                    dve.wait_ge(s("ret_scores"), u + 1)
                    v.tensor_tensor(sT[0:r, u, j * 128:N], P[0:r, 6 + u % 2, j * 128:N], decay[0:r, j, j * 128:N], ALU.mult)\
                        .then_inc(s("ret_scores_out"), 1)

            def ret_added(b):
                for i in IMAGE[b]:
                    dve.wait_ge(s("ret_o"), i + 1)
                    r = ROWS[i % 3]
                    v.tensor_tensor(h[0:r, i, :], h[0:r, i, :], P[0:r, 2 + (i % 3 + 1) % 2, 0:C], ALU.add).then_inc(s("ret_vo_out"), 1)
                dve.wait_ge(s("ret_vo_out"), 6 * (b + 1))

            ret_values(0)
            ret_decayed(0)
            ret_added(0)
            layernorm_stats(dve, "ffn0_0", h)
            dve.wait_ge(s("wq_hi"), 2)
            v.tensor_tensor(wq_b[64:128], wq_raw[64:128, 1, :], wq_b[64:128].bitcast(F32), ALU.subtract).then_inc(s("wq_lo"), 1)
            layernorm_apply(dve, "ffn0_0", x2, h)
            dve.wait_ge(s("ln_norm"), LN_BASE["ffn0_0"] + 3)
            layernorm_stats(dve, "ln1_0", x2)
            ret_values(1)
            dve.wait_ge(s("turned"), B * TURN["ret"] + B)
            layernorm_apply(dve, "ln1_0", yn, x2)
            v.tensor_tensor(wq_lo, wq_raw[:, 0, :], wq_hi.bitcast(F32), ALU.subtract).then_inc(s("wq_lo"), 1)
            ret_decayed(1)

            xlo(dve, "ln1", 0)
            ret_added(1)
            layernorm_stats(dve, "ffn0_1", h)

            def low(u):
                b, p, bank = u // PAIRS, u % PAIRS, stack_bank(u)
                dve.wait_ge(s("q_hi"), u + 1)
                v.scalar_tensor_tensor(qst[b][:, p, :], P[:, bank, 0:NP], signs[:, 2:3], qhi[:, u % 2, :].bitcast(F32),
                                       ALU.mult, ALU.subtract).then_inc(s("q_lo"), 1)
                dve.wait_ge(s("k_hi"), u + 1)
                v.scalar_tensor_tensor(kst[b][:, p, :], P[:, bank + 1, 0:NP], signs[:, 1:2], khi[:, u % 2, :].bitcast(F32),
                                       ALU.mult, ALU.subtract).then_inc(s("k_lo"), 1)

            def maxima(u, tiles):
                for t in tiles:
                    w, r, head = 6 * u + t, ROWS[t % 3], 2 * (u % PAIRS) + t // 3
                    dve.wait_ge(s("att_scores"), w + 1)
                    v.tensor_reduce(mx[0:r, u // PAIRS, t % 3, head:head + 1], P[0:r, score_bank(w), 0:N], AX.X, ALU.max)\
                        .then_inc(s("att_max"), 1)

            def normalise(grp):
                b, g = grp // 3, grp % 3
                dve.wait_ge(s("att_o_turned"), grp * 3 + 3)
                o = [P[0:ROWS[i], 7, i * 128:(i + 1) * 128].rearrange("p (h e) -> p h e", e=32) for i in range(3)]
                for i in range(3):
                    v.reciprocal(rden[0:ROWS[i], i, :], o[i][:, :, HD]).then_inc(s("att_inverse"), 1)
                for i in range(3):
                    r = ROWS[i]
                    dve.wait_ge(s("att_inverse"), grp * 3 + i + 1)
                    v.tensor_tensor(yn[0:r, b * 3 + i, g * 64:(g + 1) * 64].rearrange("p (h e) -> p h e", e=HD), o[i][:, :, 0:HD],
                                    rden[0:r, i, :].unsqueeze(2).broadcast_to([r, 4, HD]), ALU.mult).then_inc(s("att_o"), 1)

            def add_projected(b):
                for i in IMAGE[b]:
                    dve.wait_ge(s("att_proj"), i + 1)
                    r = ROWS[i % 3]
                    v.tensor_tensor(x2[0:r, i, :], x2[0:r, i, :], P[0:r, PROJ_BANKS[i], 0:C], ALU.add)\
                        .then_inc(s("att_proj_out"), 1)

            low(0)
            layernorm_apply(dve, "ffn0_1", x2, h)
            dve.wait_ge(s("ln_norm"), LN_BASE["ffn0_1"] + 3)
            layernorm_stats(dve, "ln1_1", x2)
            for u in range(2 * PAIRS):
                maxima(u, range(4))
                if u + 1 < 2 * PAIRS:
                    low(u + 1)
                if u == 0:
                    layernorm_apply(dve, "ln1_1", yn, x2)
                if u == 2:
                    xlo(dve, "ln1", 1)
                maxima(u, (4, 5))
                if u == 1:
                    dve.wait_ge(s("ln_norm"), LN_BASE["ln1_1"] + 3)
                    v.tensor_tensor(x2[:, :, :], x2[:, :, :], rows[:, 2, :].unsqueeze(1).broadcast_to([128, NT, C]), ALU.add)\
                        .then_inc(s("proj_bias"), 1)
                if u in (PAIRS + 2, PAIRS + 4):
                    normalise((u - PAIRS) // 2 - 1)
            normalise(2)
            weights_lo(dve, 0, 0, 0)
            dve.wait_ge(s("proj_bias"), 1)
            add_projected(0)
            dve.wait_ge(s("att_proj_out"), 3)
            layernorm_stats(dve, "ln2_0", x2)
            normalise(3)
            layernorm_apply(dve, "ln2_0", yn, x2)
            xlo(dve, "ln2", 0)
            gate_scores(dve, 0, 0, step, settle)
            normalise(4)
            gate_weights(dve, 0, 0, step, settle)
            normalise(5)
            hidden_parts(dve, 0, 0, 0, 0)
            add_projected(1)
            dve.wait_ge(s("att_proj_out"), NT)
            layernorm_stats(dve, "ln2_1", x2)
            hidden_parts(dve, 0, 0, 0, 1)
            layernorm_apply(dve, "ln2_1", yn, x2)
            hidden_parts(dve, 0, 0, 0, 2)
            xlo(dve, "ln2", 1)
            gate_scores(dve, 0, 1, step, settle)
            gate_weights(dve, 0, 1, step, settle)

            def mixed_in(b):
                t = slice(3 * b, 3 * b + 3)
                link(v.tensor_tensor(h[:, t, :], h[:, t, :], sums[:, t, 0, :], ALU.add))
                v.tensor_tensor(h[:, t, :], h[:, t, :], sums[:, t, 1, :], ALU.add).then_inc(s("mixed_in"), 1)
                dve.wait_ge(s("mixed_in"), b + 1)

            def first_image_on():
                mixed_in(0)
                layernorm(dve, "att1_0", yn, h)

            moe_vector(dve, 0, first_image_on)
            mixed_in(1)
            layernorm(dve, "att1_1", yn, h)

            weights_lo(dve, 1, 0, 0)
            dve.wait_ge(s("ln_norm"), LN_BASE["att1_1"] + 3)
            link(v.tensor_tensor(h[:, :, :], h[:, :, :], rows[:, 3, :].unsqueeze(1).broadcast_to([128, NT, C]), ALU.add))
            dve.wait_ge(s("late_in"), 32)
            dve.wait_ge(s("at_zeroed"), 2)

            def query_lows(b):
                for g in range(G1):
                    dve.wait_ge(s("q1_hi"), G1 * b + g + 1)
                    dst = q1s[64:128, g, b * NP:(b + 1) * NP]
                    v.tensor_tensor(dst, P[64:128, 2 + g, 0:NP], dst.bitcast(F32), ALU.subtract).then_inc(s("q1_lo"), 1)

            def context_scores(b):
                t = slice(2 * b, 2 * b + 2)
                dve.wait_ge(s("ctx1"), b + 1)
                link(v.tensor_tensor(cm[:, t, :, :], P[0:CH, 7 if b == 0 else 0, 0:2 * CH].rearrange("p (g h e) -> p g h e", g=G1, e=HD1),
                                     gmask[:, :, :].unsqueeze(1).broadcast_to([CH, G1, HG, HD1]), ALU.mult))
                link(v.tensor_reduce(cc[:, t, :], cm[:, t, :, :].rearrange("p g h e -> p g e h"), AX.X, ALU.add))
                link(v.tensor_reduce(c1[:, t], cc[:, t, :], AX.X, ALU.max))
                v.tensor_tensor(cc[:, t, :], cc[:, t, :], c1[:, t].unsqueeze(2).broadcast_to([CH, 2, HD1]), ALU.subtract)\
                    .then_inc(s("ctx_sub"), 1)

            def context_softmax(b):
                t = slice(2 * b, 2 * b + 2)
                dve.wait_ge(s("ctx_exp"), b + 1)
                link(v.tensor_reduce(c1[:, t], cc[:, t, :], AX.X, ALU.add))
                link(v.reciprocal(c1[:, t], c1[:, t]))
                link(v.tensor_tensor(cc[:, t, :], cc[:, t, :], c1[:, t].unsqueeze(2).broadcast_to([CH, 2, HD1]), ALU.mult))
                v.tensor_copy(at[:, t, :, 0:HD1], cc[:, t, :].unsqueeze(2).broadcast_to([CH, 2, 4, HD1])).then_inc(s("ctx_soft"), 1)

            def context_spread(b):
                dve.wait_ge(s("at_turned"), b + 1)
                srcs = [P[:, 1, g * CH:(g + 1) * CH].rearrange("p (h o d) -> p h o d", h=HG, o=1).broadcast_to([128, HG, 4, HD1])
                        for g in range(G1)]
                for g in range(G1):
                    v.tensor_copy(atS[:, b, g, :, :, 0:HD1], srcs[g]).then_inc(s("at_hi"), 1)
                for g in range(G1):
                    dve.wait_ge(s("at_hi"), G1 * b + g + 1)
                    for r in (slice(32, 64), slice(96, 128)):
                        dst = atS[r, b, g, :, :, 0:HD1]
                        v.tensor_tensor(dst, srcs[g][r], dst.bitcast(F32), ALU.subtract).then_inc(s("at_spread"), 1)

            def heads_out(b):
                for u in range(8 * b + 1, 8 * b + 8, 2):
                    dve.wait_ge(s("heads1"), u + 1)
                    for quarter in range(4):
                        dst, src = reshuffled(u, quarter)
                        last = v.tensor_copy(dst, src)
                    last.then_inc(s("heads1_odd"), 1)

            def attended(b):
                for i in IMAGE[b]:
                    dve.wait_ge(s("att1_o"), i + 1)
                    r = ROWS[i % 3]
                    v.tensor_tensor(x2[0:r, i, :], h[0:r, i, :], P[0:r, 2 + i % 2, 0:C], ALU.add).then_inc(s("att1_o_out"), 1)
                dve.wait_ge(s("att1_o_out"), 3 * (b + 1))
                layernorm_stats(dve, f"ffn1_{b}", x2)

            query_lows(0)
            context_scores(0)
            context_softmax(0)
            query_lows(1)
            context_scores(1)
            context_spread(0)
            context_softmax(1)
            heads_out(0)
            context_spread(1)
            heads_out(1)
            attended(0)
            dve.wait_ge(s("turned"), B * TURN["att1"] + B)
            layernorm_apply(dve, "ffn1_0", yn, x2)
            attended(1)
            xlo(dve, "ffn1", 0)
            layernorm_apply(dve, "ffn1_1", yn, x2)

            gate_scores(dve, 1, 0, step, settle)
            xlo(dve, "ffn1", 1)
            gate_scores(dve, 1, 1, step, settle)
            for q in range(HC // 2):
                hidden_parts(dve, 1, 0, 0, q)
            dve.wait_ge(s("sa_zeroed"), 1)
            dve.wait_ge(s("spec_v"), 1)
            v.tensor_scalar(sa[:, 0:N], P[0:CHAINS, 6, 0:N], rows[0:CHAINS, 6, 0:1], None, ALU.add).then_inc(s("sa_ready"), 1)
            for b in range(B):
                gate_weights(dve, 1, b, step, settle)

            def spectral_in():
                for i in range(NT):
                    r = ROWS[i % 3]
                    dve.wait_ge(s("spec_o"), i // 2 * 2 + 2)
                    step(v.tensor_tensor(yn[0:r, i, 0:C], P[0:r, i // 2, i % 2 * C:(i % 2 + 1) * C], rows[0:r, 5, :], ALU.mult))
                settle()
                finish(0)

            def finish(b):
                for i in IMAGE[b]:
                    r = ROWS[i % 3]
                    step(v.tensor_tensor(yn[0:r, i, 0:C], yn[0:r, i, 0:C], sums[0:r, i, 1, :], ALU.add))
                settle()
                for i in IMAGE[b]:
                    r = ROWS[i % 3]
                    v.tensor_tensor(h[0:r, i, :], yn[0:r, i, 0:C], x2[0:r, i, :], ALU.add).then_inc(s("out_ready"), 1)

            dve.wait_ge(s("ln_norm"), LN_BASE["ffn1_1"] + 3)
            link(v.tensor_tensor(rows[:, 4, :], rows[:, 4, :], rows[:, 5, :], ALU.mult))
            link(v.tensor_tensor(x2[:, :, :], x2[:, :, :], rows[:, 4, :].unsqueeze(1).broadcast_to([128, NT, C]), ALU.add))
            moe_vector(dve, 1, spectral_in)
            finish(1)

        @block.tensor
        def _(pe):
            mm = nc.tensor.matmul
            for g in range(4):
                pe.wait_ge(s(f"patches_in{g}"), 32)
                for t in range(4):
                    for c in range(4 * g, 4 * g + 4):
                        last = mm(P[:, 4 * (t // 2) + t % 2, 0:D], patches[:, c, t * 128:(t + 1) * 128], convw[:, c, :],
                                  start=(c == 0), stop=(c == KP - 1))
                    if g == 3 and t % 2 == 1:
                        last.then_inc(s("conv"), 1)
            pe.wait_ge(s("tok_consts_in"), 16 * 4)
            pe.wait_ge(s("qkv_weights_in"), 16)

            def tok_turn(tag, b):
                for i in range(2):
                    pe.wait_ge(s("ln_norm"), LN_BASE[f"{tag}_{b}"] + i + 1)
                    last = nc.tensor.transpose(P[:, 4 * b + 3, i * 128:(i + 1) * 128], ynt[:, 3 * b + i, :], ident[:, :])
                last.then_inc(s("tok_turned"), 1)

            def tok_tile(b, i):
                return slice((2 * b + i) * 128, (2 * b + i + 1) * 128)

            def tok_keys(l, b):
                pe.wait_ge(s("tok_y"), 2 * l * B + b + 1)
                for q in range(4):
                    last = mm(P[:, 4 * b + q // 2, q % 2 * TOK:(q % 2 + 1) * TOK], wqkv[:, l, INNER + q * 128:INNER + (q + 1) * 128],
                              yT[:, b * TOK:(b + 1) * TOK], start=True, stop=True)
                    if q % 2 == 1:
                        last.then_inc(s("tok_k"), 1)

            def tok_queries(l, b):
                for i in range(2):
                    mm(P[:, 4 * b + 2 + i, :], yT[:, tok_tile(b, i)], wqkv[:, l, 0:INNER], start=True, stop=True).then_inc(s("tok_q"), 1)

            def tok_values(l, b):
                for i in range(2):
                    pe.wait_ge(s("tok_qsub"), 2 * (l * B + b) + i + 1)
                    mm(P[:, 4 * b + 2 + i, :], yT[:, tok_tile(b, i)], wqkv[:, l, 2 * INNER:3 * INNER], start=True, stop=True)\
                        .then_inc(s("tok_v"), 1)

            def tok_turn_keys(l, b):
                pe.wait_ge(s("tok_kexp"), 4 * (l * B + b) + 4)
                for i in range(2):
                    for q in range(4):
                        last = nc.tensor.transpose(P[:, 4 * b + i, q * 128:(q + 1) * 128], ke[:, q, tok_tile(b, i)], ident[:, :])
                    last.then_inc(s("tok_kturned"), 1)

            def tok_turn_queries(l, b):
                n = l * B + b
                for i in range(2):
                    pe.wait_ge(s("tok_qsoft"), 2 * n + i + 1)
                    pe.wait_ge(s("tok_vout"), 2 * n + i + 1)
                    for c in range(4):
                        last = nc.tensor.transpose(P[:, 4 * b + 2 + i, c * 128:(c + 1) * 128], qs[:, 2 * b + i, c * 128:(c + 1) * 128],
                                                   ident[:, :])
                    last.then_inc(s("tok_qturned"), 1)

            def tok_contexts(l, b):
                pe.wait_ge(s("tok_kt"), 2 * (l * B + b) + 2)
                pe.wait_ge(s("tok_vout"), 2 * (l * B + b) + 2)
                for q in range(4):
                    for i in range(2):
                        last = mm(P[:, 4 * b, q * 128:(q + 1) * 128], vt[:, 2 * b + i, q * 128:(q + 1) * 128],
                                  kt[:, 2 * b + i, q * 128:(q + 1) * 128], start=(i == 0), stop=(i == 1))
                last.then_inc(s("tok_ctx"), 1)

            def tok_weighted(l, b):
                pe.wait_ge(s("tok_weights_in"), 16 * 6)
                pe.wait_ge(s("tok_bd"), 2 * (l * B + b) + 2)
                for q in range(4):
                    last = mm(P[:, 4 * b + 1, q * 128:(q + 1) * 128], bd[:, b, q, :], wout[:, l, q, :], start=True, stop=True)
                last.then_inc(s("tok_w2"), 1)

            def tok_attention(l, b):
                pe.wait_ge(s("tok_qT"), 2 * (l * B + b) + 2)
                pe.wait_ge(s("tok_w2_out"), l * B + b + 1)
                for i in range(2):
                    for q in range(4):
                        last = mm(P[:, 4 * b, i * D:(i + 1) * D], qT[:, q, tok_tile(b, i)], w2[:, b, q, :], start=(q == 0), stop=(q == 3))
                last.then_inc(s("tok_att"), 1)

            def tok_ff1(l, b):
                pe.wait_ge(s("tok_y"), (2 * l + 1) * B + b + 1)
                for q in range(4):
                    last = mm(P[:, 4 * b + q // 2, q % 2 * TOK:(q % 2 + 1) * TOK], wff1[:, l, q * 128:(q + 1) * 128],
                              yT[:, b * TOK:(b + 1) * TOK], start=True, stop=True)
                    if q % 2 == 1:
                        last.then_inc(s("tok_ff1"), 1)

            def tok_ff2(l, b):
                pe.wait_ge(s("tok_gelu"), 4 * (l * B + b) + 4)
                for i in range(2):
                    for q in range(4):
                        last = mm(P[:, 4 * b + 2, i * D:(i + 1) * D], hT[:, q, tok_tile(b, i)], wff2[:, l, q, :],
                                  start=(q == 0), stop=(q == 3))
                last.then_inc(s("tok_ff2"), 1)

            for l in range(LAYERS):
                tok_turn(f"t{l}ln1", 0)
                tok_keys(l, 0)
                tok_turn(f"t{l}ln1", 1)
                tok_queries(l, 0)
                tok_keys(l, 1)
                tok_queries(l, 1)
                tok_values(l, 0)
                tok_turn_keys(l, 0)
                tok_values(l, 1)
                tok_turn_queries(l, 0)
                tok_contexts(l, 0)
                tok_turn_keys(l, 1)
                tok_weighted(l, 0)
                tok_turn_queries(l, 1)
                tok_attention(l, 0)
                tok_contexts(l, 1)
                tok_turn(f"t{l}ln2", 0)
                tok_weighted(l, 1)
                tok_ff1(l, 0)
                tok_attention(l, 1)
                tok_ff2(l, 0)
                tok_turn(f"t{l}ln2", 1)
                tok_ff1(l, 1)
                tok_ff2(l, 1)
            for b in range(B):
                tok_turn("tlnf", b)
                pe.wait_ge(s("tok_y"), 2 * LAYERS * B + b + 1)
                for i in range(2):
                    mm(P[:, 4 * b + i, 0:C], yT[:, tok_tile(b, i)], whead[:, :], start=True, stop=True).then_inc(s("head"), 1)

            pe.wait_ge(s("consts_in"), 16 * 9)
            pe.wait_ge(s("weights_in"), 16 * 2)
            def ret_turned(b):
                ttranspose(pe, "ret", (b,))

            def ret_values(b):
                pe.wait_ge(s("turned_out"), 2 * (b + 1))
                for i in IMAGE[b]:
                    r, n = ROWS[i % 3], 6 * b + i % 3
                    if n >= 2:
                        pe.wait_ge(s("ret_vo_out"), n - 1)
                    for k in range(2):
                        last = mm(P[0:r, 2 + n % 2, 0:C], tT[:, k, col(i):col(i) + r], wret[:, k, 2 * C:3 * C], start=(k == 0), stop=(k == 1))
                    last.then_inc(s("ret_v"), 1)

            def ret_queries_keys(b):
                pe.wait_ge(s("turned_out"), 2 * (b + 1))
                for m in range(4):
                    u = 4 * b + m
                    if u >= 2:
                        pe.wait_ge(s("ret_qk_out"), u - 1)
                    for k in range(2):
                        last = mm(P[0:CH, 4 + u % 2, 0:N], wret[:, k, m * CH:(m + 1) * CH], tT[:, k, b * NP:b * NP + N],
                                  start=(k == 0), stop=(k == 1))
                    last.then_inc(s("ret_qk"), 1)

            def ret_scores(b):
                pe.wait_ge(s("ret_qk_out"), 4 * (b + 1))
                for j in range(3):
                    u, r = b * 3 + j, ROWS[j]
                    if u >= 2:
                        pe.wait_ge(s("ret_scores_out"), u - 1)
                    for k in range(2):
                        last = mm(P[0:r, 6 + u % 2, j * 128:N], qkT[:, 2 + k, b * NP + j * 128:b * NP + j * 128 + r],
                                  qkT[:, k, b * NP + j * 128:b * NP + N], start=(k == 0), stop=(k == 1))
                    last.then_inc(s("ret_scores"), 1)

            def ret_outputs(b):
                for i in range(3):
                    r, n = ROWS[i], 6 * b + 3 + i
                    pe.wait_ge(s("ret_vo_out"), max(n - 1, 6 * b + 3))
                    pe.wait_ge(s("ret_scores_out"), 3 * b + i + 1)
                    for j in range(i + 1):
                        last = mm(P[0:r, 2 + n % 2, 0:C], sT[0:ROWS[j], b * 3 + j, i * 128:i * 128 + r],
                                  vtok[0:ROWS[j], b * 3 + j, :], start=(j == 0), stop=(j == i))
                    last.then_inc(s("ret_o"), 1)

            ret_turned(0)
            ret_values(0)
            pe.wait_ge(s("head_out"), 4)
            ret_queries_keys(0)
            ret_turned(1)
            ret_scores(0)
            ret_outputs(0)
            ret_queries_keys(1)
            ret_values(1)
            xturn(pe, "ln1_0", IMAGE[0], 0)
            ret_scores(1)
            ret_outputs(1)

            pe.wait_ge(s("attention_weights_in"), 16 * 5)

            def stack(u, m):
                before = u - 2 if u < PAIRS else PAIRS - 2 if u == PAIRS else u - 1
                if before >= 0:
                    pe.wait_ge(s("k_lo" if m else "q_lo"), before + 1)
                f = slice((m * PAIRS + u % PAIRS) * 128, (m * PAIRS + u % PAIRS + 1) * 128)
                cols = slice((u // PAIRS) * NP, (u // PAIRS + 1) * NP)
                for n, (w, x_, k) in enumerate(((wq_hi, x_hi, 0), (wq_hi, x_lo, 0), (wq_lo, x_hi, 0), (wq_b, x_hi, 1), (wq_b, x_lo, 1))):
                    last = mm(P[:, stack_bank(u) + m, 0:NP], w[:, f], x_[:, k, cols], start=(n == 0), stop=(n == 4))
                last.then_inc(s("k_stack" if m else "q_stack"), 1)

            def score(u, t):
                w, i = 6 * u + t, t % 3
                if t == 0:
                    pe.wait_ge(s("q_lo"), u + 1)
                    pe.wait_ge(s("k_lo"), u + 1)
                if w < 6 * PAIRS:
                    if w >= 3:
                        pe.wait_ge(s("att_max"), w - 2)
                elif w >= 6 * PAIRS + 2:
                    pe.wait_ge(s("att_max"), w - 1)
                part, b, p = slice(64 * (t // 3), 64 * (t // 3) + 64), u // PAIRS, u % PAIRS
                mm(P[0:ROWS[i], score_bank(w), 0:NP], qst[b][part, p, i * 128:i * 128 + ROWS[i]], kst[b][part, p, :],
                   start=True, stop=True).then_inc(s("att_scores"), 1)

            def turn_maxima(b):
                pe.wait_ge(s("att_max"), (b + 1) * 6 * PAIRS)
                for i in range(3):
                    r = ROWS[i]
                    last = nc.tensor.transpose(P[0:HEADS, 7 if b == 0 else 0, i * 128:i * 128 + r], mx[0:r, b, i, :], ident[0:r, 0:r])
                last.then_inc(s("att_maxT"), 1)

            def score_turned(u):
                b, t = u // (3 * HEADS), u % (3 * HEADS)
                hh, j = t // 3, t % 3
                r = ROWS[j]
                if u >= 2:
                    pe.wait_ge(s("att_exp"), u - 1)
                part = slice(64 * (hh % 2), 64 * (hh % 2) + 64)
                mm(P[0:r, 4 + u % 2, 0:NP], kst[b][part, hh // 2, j * 128:j * 128 + r], qst[b][part, hh // 2, :], start=True, stop=False)
                mm(P[0:r, 4 + u % 2, 0:NP], selr[:, hh, 0:r], mxT[:, b, :], start=False, stop=True).then_inc(s("att_scoresT"), 1)

            def pv(u):
                hh, j = (u // 3) % HEADS, u % 3
                r = ROWS[j]
                if u % 12 == 0 and u >= 12:
                    pe.wait_ge(s("att_ao"), u // 12)
                pe.wait_ge(s("att_exp"), u + 1)
                mm(P[32 * (hh % 4):32 * (hh % 4) + 32, 6, 0:N], vaug[0:r, (u // (3 * HEADS)) * 3 + j, hh, :], pt[0:r, u % 6, :],
                   start=(j == 0), stop=(j == 2)).then_inc(s("att_pv"), 1)

            def turn_outputs(grp):
                pe.wait_ge(s("att_ao"), grp + 1)
                if grp >= 1:
                    pe.wait_ge(s("att_o"), 3 * grp)
                if grp == 0:
                    pe.wait_ge(s("att_max_out"), 1)
                for i in range(3):
                    nc.tensor.transpose(P[0:ROWS[i], 7, i * 128:(i + 1) * 128], ao[:, grp % 3, i * 128:i * 128 + ROWS[i]],
                                        ident[:, :]).then_inc(s("att_o_turned"), 1)

            def project(b):
                pe.wait_ge(s("turned_out"), 2 * B * TURN["proj"] + 2 * (b + 1))
                for i in IMAGE[b]:
                    r = ROWS[i % 3]
                    for k in range(2):
                        last = mm(P[0:r, PROJ_BANKS[i], 0:C], tT[:, k, col(i):col(i) + r], wpa[:, k, :], start=(k == 0), stop=(k == 1))
                    last.then_inc(s("att_proj"), 1)

            def att_value(i):
                r = ROWS[i % 3]
                if i >= 1:
                    pe.wait_ge(s("att_v_out"), i)
                for p, k in ((slice(0, 128), 0), (slice(0, 64), 1)):
                    last = mm(P[0:r, 7, 0:C], xf[p, k, col(i):col(i) + r], wva[p, k, :], start=(k == 0), stop=(k == 1))
                last.then_inc(s("att_v"), 1)

            pe.wait_ge(s("x_lo"), 1)
            pe.wait_ge(s("wq_lo"), 2)
            pe.wait_ge(s("ret_vo_out"), 2 * NT)
            for u in range(2):
                for m in range(2):
                    stack(u, m)
            for u in range(PAIRS):
                for t in range(6):
                    score(u, t)
                    if t in (1, 2) and u + 2 <= PAIRS:
                        if u + 2 == PAIRS:
                            pe.wait_ge(s("x_lo"), 2)
                        stack(u + 2, t - 1)
                    if t == 3 and u == 1:
                        xturn_half(pe, "ln1_1", IMAGE[1], 7, 0).then_inc(s("x_half_turned"), 1)
                    if t == 5 and u == 1:
                        pe.wait_ge(s("xf"), 3)
                        pe.wait_ge(s("x_hi"), 3)
                        xturn_half(pe, "ln1_1", IMAGE[1], 7, 1).then_inc(s("x_turned"), 1)
                    if t in (3, 4) and 2 <= u <= 4:
                        pe.wait_ge(s("xf"), 2 * B)
                        pe.wait_ge(s("x_hi"), 2 * B)
                        att_value(2 * u - 7 + t)
            pe.wait_ge(s("att_v_out"), NT)
            pe.wait_ge(s("selr_set"), 1)
            turn_maxima(0)
            for u in range(2 * 3 * HEADS):
                b, t = u // (3 * HEADS), u % (3 * HEADS)
                if t == 0:
                    if b == 1:
                        pv(u - 1)
                        turn_maxima(1)
                    pe.wait_ge(s("att_max_out"), 2 * (b + 1))
                score_turned(u)
                if b == 0:
                    pair = PAIRS + t // 6
                    score(pair, t % 6)
                    if t % 6 in (1, 2) and pair + 1 < 2 * PAIRS:
                        stack(pair + 1, t % 6 - 1)
                if t > 0:
                    pv(u - 1)
                if u % 12 == 1 and u >= 12:
                    turn_outputs(u // 12 - 1)
                if b == 1 and t == TURN_AT:
                    pe.wait_ge(s("att_o"), 9)
                    ttranspose(pe, "proj", (0,))
                if b == 1 and t == PROJECT_AT:
                    project(0)
                if b == 1 and t == MIX_AT:
                    pe.wait_ge(s("att_proj_out"), 3)
                    xturn(pe, "ln2_0", IMAGE[0], 0)
                if b == 1 and t == GATE_AT:
                    gate_logits(pe, 0, 0)
            pe.wait_ge(s("x_lo"), B * X_TURN["ln2"] + 1)
            hidden(pe, 0, 0, 0, 0, (0,))
            pv(2 * 3 * HEADS - 1)
            hidden(pe, 0, 0, 0, 0, (1,))
            turn_outputs(2 * B + 1)
            pe.wait_ge(s("m0_logits_out"), 2)
            hidden(pe, 0, 0, 0, 0, (2,))
            pe.wait_ge(s("att_o"), 3 * B * 3)
            ttranspose(pe, "proj", (1,))
            hidden(pe, 0, 0, 0, 0, (3,))
            project(1)
            hidden(pe, 0, 0, 0, 0, (4, 5))
            pe.wait_ge(s("att_proj_out"), NT)
            moe_tensor(pe, 0)

            def queries(b):
                pe.wait_ge(s("turned_out"), 2 * B * TURN["att1"] + 2 * (b + 1))
                for g in range(G1):
                    if b:
                        pe.wait_ge(s("q1_lo"), g + 1)
                    for k in range(2):
                        last = mm(P[:, 2 + g, 0:NP], w1q[:, k, g * 128:(g + 1) * 128], tT[:, k, b * NP:(b + 1) * NP],
                                  start=(k == 0), stop=(k == 1))
                    last.then_inc(s("q1"), 1)

            def key_values(b):
                pe.wait_ge(s("turned_out"), 2 * B * TURN["att1"] + 2 * (b + 1))
                for i in IMAGE[b]:
                    if b:
                        pe.wait_ge(s("kv1_out"), i - 2)
                    r = ROWS[i % 3]
                    for k in range(2):
                        last = mm(P[0:r, 4 + i % 3, 0:2 * C], tT[:, k, col(i):col(i) + r], w1kv[:, k, :], start=(k == 0), stop=(k == 1))
                    last.then_inc(s("kv1"), 1)

            def contexts(b):
                pe.wait_ge(s("kv1_out"), 3 * (b + 1))
                for g in range(G1):
                    for j in range(3):
                        r = ROWS[j]
                        last = mm(P[0:CH, 7 if b == 0 else 0, g * CH:(g + 1) * CH], kv[0:r, b * 3 + j, g * CH:(g + 1) * CH],
                                  kv[0:r, b * 3 + j, C + g * CH:C + (g + 1) * CH], start=(j == 0), stop=(j == 2))
                last.then_inc(s("ctx1"), 1)

            def turn_contexts(b):
                pe.wait_ge(s("ctx_soft"), b + 1)
                if b:
                    pe.wait_ge(s("at_spread"), 4)
                for g in range(G1):
                    last = nc.tensor.transpose(P[:, 1, g * CH:(g + 1) * CH], at[:, 2 * b + g, :, :].rearrange("p z e -> p (z e)"),
                                               ident[0:CH, 0:CH])
                last.then_inc(s("at_turned"), 1)

            def heads(b):
                pe.wait_ge(s("at_spread"), 4 * (b + 1))
                pe.wait_ge(s("q1_lo"), G1 * (b + 1))
                for u in range(8 * b, 8 * b + 8):
                    if u >= 4:
                        pe.wait_ge(s("heads1_odd" if u % 2 else "heads1_even"), (u - 4) // 2 + 1)
                    hh, g = u % 8 // G1, u % G1
                    mm(P[:, 4 + u % 4, 0:NP], atS[:, b, g, hh, :, :].rearrange("p q d -> p (q d)"), q1s[:, g, b * NP:(b + 1) * NP],
                       start=True, stop=True).then_inc(s("heads1"), 1)

            def attended(b):
                pe.wait_ge(s("heads1_even"), 4 * (b + 1))
                pe.wait_ge(s("heads1_odd"), 4 * (b + 1))
                for i in IMAGE[b]:
                    r = ROWS[i % 3]
                    if i >= 2:
                        pe.wait_ge(s("att1_o_out"), i - 1)
                    first = (i % 3) * 256
                    for half in range(2):
                        last = mm(P[0:r, 2 + i % 2, 0:C], mixed[:, b, first + half:first + half + 2 * r - 1:2], w1p[:, half, :],
                                  start=(half == 0), stop=(half == 1))
                    last.then_inc(s("att1_o"), 1)

            ttranspose(pe, "att1", (0,))
            queries(0)
            pe.wait_ge(s("m0_acc"), NT * (EXPERTS + 1))
            key_values(0)
            ttranspose(pe, "att1", (1,))
            contexts(0)
            key_values(1)
            queries(1)
            contexts(1)
            turn_contexts(0)
            heads(0)
            turn_contexts(1)
            heads(1)
            attended(0)
            attended(1)
            xturn(pe, "ffn1_0", IMAGE[0], 0)
            gate_logits(pe, 1, 0)
            pe.wait_ge(s("x_hi"), 2 * B * X_TURN["ffn1"] + 2)
            pe.wait_ge(s("x_lo"), B * X_TURN["ffn1"] + 1)
            hidden(pe, 1, 0, 0, 0, (0, 1))
            pe.wait_ge(s("att1_o_out"), NT)
            xturn(pe, "ffn1_1", IMAGE[1], 2)
            gate_logits(pe, 1, 1)
            pe.wait_ge(s("x_hi"), 2 * B * (X_TURN["ffn1"] + 1))
            hidden(pe, 1, 0, 0, 0, (2, 3, 4, 5))
            for chain in range(CHAINS):
                for p, k in ((slice(0, 128), 0), (slice(0, 64), 1)):
                    seq = xf[p, k, chain % B * NP:chain % B * NP + N]
                    last = mm(P[0:CHAINS, 6, 0:N], wgate[p, k, 16 + 4 * chain:20 + 4 * chain], seq[:, ::-1] if chain >= B else seq,
                              start=(chain == 0 and k == 0), stop=(chain == CHAINS - 1 and k == 1))
            last.then_inc(s("spec_v"), 1)
            pe.wait_ge(s("m1_logits_out"), 2 * B)
            moe_tensor(pe, 1)


def kernel(**inputs):
    import numpy as np
    import concourse.bacc as bacc
    from concourse.bass_utils import run_bass_kernel_spmd as run

    x = {k: np.asarray(v) for k, v in inputs.items()}
    f = np.float32
    T = np.transpose
    pad = lambda w, n: np.concatenate([w, np.zeros((w.shape[0], n - w.shape[1]), w.dtype)], axis=1)
    vw = x["L1_ffn_v_w"][:, None]
    own = [np.concatenate([vw if m == n else np.zeros_like(vw) for m in range(CHAINS)], axis=1) for n in range(CHAINS)]
    gate = np.concatenate([x["L0_ffn_gate_w"].T, x["L1_ffn_gate_w"], *own], axis=1)
    two = lambda w: T(np.concatenate([w, np.zeros((64, w.shape[1]), f)]).reshape(2, 128, -1), (1, 0, 2))
    bc = lambda v_: np.broadcast_to(v_, (C,))
    heads = x["L0_ffn_qkv_w"][:2 * C].reshape(2, HEADS, 1, HD, C)
    qk = np.broadcast_to(heads, (2, HEADS, 4, HD, C)).reshape(2, HEADS * 4 * HD, C)
    wq1 = x["L1_attn_Wq"]
    wp1 = x["L1_attn_Wproj"].reshape(2, 4, HD1, C)
    spread = T(np.concatenate([wp1, np.zeros((2, 4, 32 - HD1, C), f)], axis=2), (1, 2, 0, 3)).reshape(128, 2, C)
    diff = np.arange(N)[None, :] - np.arange(384)[:, None]
    decay = np.where(diff >= 0, np.float64(f(0.99)) ** np.maximum(diff, 0), 0.0) / np.sqrt(float(C))
    p = np.arange(128)
    copy = (p // HD) % 4
    ln = "L0_tok_ln"
    arrays = {
        "patches": T(x["x"].reshape(B, 32, 16, 8, 16, 8), (1, 3, 5, 0, 2, 4)).reshape(2048, B * TOK),
        "conv_w": x["L0_tok_conv_w"].reshape(D, 2048).T,
        "qkv_w": x["L0_tok_qkv_w"], "out_w": x["L0_tok_out_w"], "ff1_w": x["L0_tok_ff1_w"], "ff2_w": x["L0_tok_ff2_w"],
        "head_w": x["L0_tok_head_w"],
        "ret_w": x["L0_attn_W_qkv"].T, "v_w": two(x["L0_ffn_qkv_w"][2 * C:].T), "proj_w": x["L0_ffn_proj_w"].T,
        "gate_w": two(gate),
        "q1_w": np.concatenate([pad(wq1[:, g * HD1:(g + 1) * HD1], 32) for g in range(G1) for copy_ in range(4)], axis=1),
        "kv1_w": x["L1_attn_Wkv"], "proj1_w": spread, "qk_w": T(qk, (0, 2, 1)),
        "w1": np.stack([T(x["L0_ffn_w1"], (0, 2, 1)), x["L1_ffn_w1"]]),
        "w2": np.stack([T(x["L0_ffn_w2"], (0, 2, 1)), x["L1_ffn_w2"]]),
        "b1": T(np.stack([x["L0_ffn_b1"], x["L1_ffn_b1"]]).reshape(2, EXPERTS, HC, 128), (3, 0, 1, 2)),
        "b2": np.stack([x["L0_ffn_b2"], x["L1_ffn_b2"]]),
        "txt": x["txt"],
        "rows": np.stack([x["L0_tok_head_b"], x["L0_attn_b_qkv"][2 * C:], x["L0_ffn_proj_b"], x["L1_attn_bproj"],
                          x["L1_ffn_out_b"], x["L1_ffn_bk_scale"], bc(x["L1_ffn_v_b"])]),
        "tok_rows": np.concatenate([x["L0_tok_conv_b"][None], x["L0_tok_out_b"], x["L0_tok_ff2_b"]]),
        "tok_cols": np.stack([x[ln + n][l] for l in range(LAYERS) for n in ("1_g", "1_b", "2_g", "2_b")]
                             + [x[ln + "f_g"], x[ln + "f_b"]], axis=1),
        "ff1_b": T(x["L0_tok_ff1_b"].reshape(LAYERS * 4, 128), (1, 0)),
        "ch_cols": x["L0_attn_b_qkv"][:2 * C].reshape(4, CH).T,
        "mix_cols": np.stack([np.concatenate([x["L0_ffn_" + n][128:]] * 2) if k else x["L0_ffn_" + n][:128] for n in ("ln1_g", "ln1_b", "ln2_g", "ln2_b")
                             for k in range(2)], axis=1),
        "gate_rows": np.stack([x["L0_ffn_gate_b"], x["L1_ffn_gate_b"], np.arange(EXPERTS, dtype=f)]),
        "outw_rows": np.stack([np.concatenate([x["L1_ffn_out_w"][:, None], np.zeros((2, 1, C), f)][::1 - 2 * b], axis=1)
                               for b in range(B)]),
        "ident": np.eye(128, dtype=f),
        "decay": T(decay.reshape(3, 128, N), (1, 0, 2)).astype(f),
        "signs": (np.array([[1, 0, 0], [-1, 1, 0], [-1, 0, -1], [1, 1, 1]]) * np.array([HD ** -0.5, 1, HD ** -0.5]))[copy].astype(f),
        "sel": np.broadcast_to(-np.eye(HEADS, dtype=f)[:, :, None], (HEADS, HEADS, 128)),
        "gmask": np.broadcast_to((np.arange(CH)[:, None] // HD1 == np.arange(HG)[None, :])[:, :, None],
                                 (CH, HG, HD1)).astype(f),
    }
    arrays = {"in_" + k: np.ascontiguousarray(v) for k, v in arrays.items()}
    nc = bacc.Bacc("TRN2", target_bir_lowering=False, num_devices=1)
    aps = {k[3:]: nc.dram_tensor(k, v.shape, mybir.dt.from_np(v.dtype), kind="ExternalInput").ap() for k, v in arrays.items()}
    out = nc.dram_tensor("out_0", (B, N, C), F32, kind="ExternalOutput").ap()
    fusion_kernel(nc, aps, out)
    return run(nc, [arrays], core_ids=[0]).results[0]["out_0"]
```
